# Optimizing a Trainium2 kernel written in Bass

```python
import numpy as np
import jax
import jax.numpy as jnp

def _softmax(x, axis=-1):
    return jax.nn.softmax(x, axis=axis)

def _gelu(x):
    return jax.nn.gelu(x, approximate=True)

def _silu(x):
    return jax.nn.silu(x)

def _sigmoid(x):
    return jax.nn.sigmoid(x)

def _layernorm(x, axis=-1, eps=1e-05):
    m = jnp.mean(x, axis=axis, keepdims=True)
    v = jnp.var(x, axis=axis, keepdims=True)
    return (x - m) / jnp.sqrt(v + eps)

def _scatter_add(tgt, idx, src, axis=0):
    return tgt.at[idx].add(src)

def _segment_sum(src, seg, n):
    return jax.ops.segment_sum(src, seg, n)
kernel_name = 'mk_adaln_d2_jaxref_r8_23cd5a'

def setup_inputs(seed: int=0):
    np.random.seed(seed)
    _w = jnp.asarray

    def _L0_attn_setup():
        import jax, jax.numpy as jnp
        import numpy as np
        import math
        B, S, E = (2, 256, 128)
        H, DC, DR = (16, 32, 128)
        HD = E // H

        def _linear_params(key, din, dout):
            k1, k2 = jax.random.split(key)
            bound = 1.0 / math.sqrt(din)
            w = jax.random.uniform(k1, (din, dout), minval=-bound, maxval=bound, dtype=jnp.float32)
            b = jax.random.uniform(k2, (dout,), minval=-bound, maxval=bound, dtype=jnp.float32)
            return (w, b)

        def _gelu(x):
            return jax.nn.gelu(x, approximate=False)

        def _rope_cos_sin(seq_len, d_rope):
            inv_freq = 1.0 / 10000.0 ** (jnp.arange(0, d_rope, 2, dtype=jnp.float32) / d_rope)
            t = jnp.arange(seq_len, dtype=jnp.float32)
            freqs = t[:, None] * inv_freq[None, :]
            emb = jnp.concatenate([freqs, freqs], axis=-1)
            return (jnp.cos(emb), jnp.sin(emb))

        def _apply_rope(x, cos, sin):
            d = x.shape[-1]
            x1, x2 = (x[..., :d // 2], x[..., d // 2:])
            rot = jnp.concatenate([-x2, x1], axis=-1)
            return x * cos + rot * sin
        key = jax.random.key(seed)
        ks = jax.random.split(key, 10)
        x = jax.random.normal(ks[0], (B, S, E), dtype=jnp.float32)
        wq, bq = _linear_params(ks[1], E, DC)
        wqc, bqc = _linear_params(ks[2], DC, E - DR)
        wqr, bqr = _linear_params(ks[3], E, DR)
        wkv, bkv = _linear_params(ks[4], E, DC)
        wkr, bkr = _linear_params(ks[5], E, DR)
        wkc, bkc = _linear_params(ks[6], DC, E - DR)
        wv, bv = _linear_params(ks[7], DC, E)
        wo, bo = _linear_params(ks[8], E, E)
        return dict(x=x, wq=wq, bq=bq, wqc=wqc, bqc=bqc, wqr=wqr, bqr=bqr, wkv=wkv, bkv=bkv, wkr=wkr, bkr=bkr, wkc=wkc, bkc=bkc, wv=wv, bv=bv, wo=wo, bo=bo)
    _L0_attn_in = _L0_attn_setup()

    def _L0_ffn_setup():
        import jax, jax.numpy as jnp
        import numpy as np
        H, I, E, K = (128, 64, 32, 8)
        B, S = (4, 128)

        def silu(x):
            return x * jax.nn.sigmoid(x)
        key = jax.random.key(seed)
        ks = jax.random.split(key, 14)

        def w(k, shape, fan_in):
            return jax.random.normal(k, shape, jnp.float32) / np.float32(np.sqrt(fan_in))
        return {'hidden_states': jax.random.normal(ks[0], (B, S, H), jnp.float32), 'Wr': w(ks[1], (H, E), H), 'br': jnp.zeros((E,), jnp.float32), 'Wg_s': w(ks[2], (H, I), H), 'bg_s': jnp.zeros((I,), jnp.float32), 'Wu_s': w(ks[3], (H, I), H), 'bu_s': jnp.zeros((I,), jnp.float32), 'Wd_s': w(ks[4], (I, H), I), 'bd_s': jnp.zeros((H,), jnp.float32), 'Wg': w(ks[5], (E, H, I), H), 'bg': jnp.zeros((E, I), jnp.float32), 'Wu': w(ks[6], (E, H, I), H), 'bu': jnp.zeros((E, I), jnp.float32), 'Wd': w(ks[7], (E, I, H), I), 'bd': jnp.zeros((E, H), jnp.float32)}
    _L0_ffn_in = _L0_ffn_setup()
    _L0_c = _w((lambda *s: np.random.randn(*s).astype(np.float32) * 0.05)(4, 128))
    _L0_wmod = _w((lambda *s: np.random.randn(*s).astype(np.float32) * 0.05)(128, 6 * 128) * 128 ** (-0.5))

    def _L1_attn_setup():
        import math
        import jax, jax.numpy as jnp
        import numpy as np
        D_MODEL = 128
        NUM_SCALES = 4
        STATE_SIZE = 16
        EXPAND = 2
        D_INNER = D_MODEL * EXPAND
        D_PER_SCALE = D_INNER // NUM_SCALES
        BATCH, SEQ = (4, 512)

        def _make_A_log():
            base = np.arange(1, STATE_SIZE + 1, dtype=np.float32)
            parts = [np.broadcast_to(base * 2.0 ** i, (D_PER_SCALE, STATE_SIZE)) for i in range(NUM_SCALES)]
            A = np.concatenate(parts, axis=0)
            return jnp.asarray(np.log(A))

        def _selective_scan(x_ssm, A, B_mat, C_mat, dt):
            b, L, d = x_ssm.shape
            N = A.shape[1]
            h0 = jnp.zeros((b, d, N), dtype=jnp.float32)

            def step(h, inp):
                dt_t, B_t, C_t, x_t = inp
                A_bar = jnp.exp(jnp.minimum(dt_t[..., None] * A, 20.0))
                B_bar = dt_t[..., None] * B_t[:, None, :]
                h = A_bar * h + B_bar * x_t[..., None]
                y_t = jnp.einsum('bdn,bn->bd', h, C_t)
                return (h, y_t)
            xs = (jnp.swapaxes(dt, 0, 1), jnp.swapaxes(B_mat, 0, 1), jnp.swapaxes(C_mat, 0, 1), jnp.swapaxes(x_ssm, 0, 1))
            _, ys = jax.lax.scan(step, h0, xs)
            return jnp.swapaxes(ys, 0, 1)
        key = jax.random.key(seed)
        ks = jax.random.split(key, 8)
        scale = 0.02
        x = jax.random.normal(ks[0], (BATCH, SEQ, D_MODEL), dtype=jnp.float32)
        W_in = jax.random.normal(ks[1], (2 * D_INNER, D_MODEL), dtype=jnp.float32) * scale
        W_B = jax.random.normal(ks[2], (STATE_SIZE, D_INNER), dtype=jnp.float32) * scale
        W_C = jax.random.normal(ks[3], (STATE_SIZE, D_INNER), dtype=jnp.float32) * scale
        W_dt = jax.random.normal(ks[4], (D_INNER, D_INNER), dtype=jnp.float32) * scale
        u = jax.random.uniform(ks[5], (D_INNER,), dtype=jnp.float32)
        b_dt = u * (math.log(0.1) - math.log(0.001)) + math.log(0.001)
        W_out = jax.random.normal(ks[6], (D_MODEL, D_INNER), dtype=jnp.float32) * scale
        A_log = _make_A_log()
        D = jnp.ones((D_INNER,), dtype=jnp.float32)
        output_gate = jnp.zeros((1,), dtype=jnp.float32)
        return {'x': x, 'W_in': W_in, 'A_log': A_log, 'W_B': W_B, 'W_C': W_C, 'W_dt': W_dt, 'b_dt': b_dt, 'D': D, 'output_gate': output_gate, 'W_out': W_out}
    _L1_attn_in = _L1_attn_setup()

    def _L1_ffn_setup():
        import jax, jax.numpy as jnp
        import numpy as np
        DIM = 128
        DEPTH = 2
        HEADS = 8
        DIM_HEAD = 64
        WINDOW = 64
        INNER = HEADS * DIM_HEAD
        HID = int(DIM * 4 * 2 / 3)
        B, N = (2, 1024)
        QK_SCALE = 8.0

        def shift_token(t):
            t1, t2 = jnp.split(t, 2, axis=-1)
            t2 = jnp.pad(t2, ((0, 0), (1, 0), (0, 0)))[:, :-1]
            return jnp.concatenate([t1, t2], axis=-1)

        def l2norm(t):
            return t / jnp.clip(jnp.linalg.norm(t, axis=-1, keepdims=True), 1e-12)

        def rotate_half(x):
            x1, x2 = jnp.split(x, 2, axis=-1)
            return jnp.concatenate([-x2, x1], axis=-1)

        def rotary_xpos(q, k):
            n = q.shape[-2]
            half_idx = jnp.arange(0, DIM_HEAD, 2, dtype=jnp.float32)
            inv_freq = 1.0 / 10000.0 ** (half_idx / DIM_HEAD)
            t = jnp.arange(n, dtype=jnp.float32)
            freqs = t[:, None] * inv_freq[None, :]
            freqs = jnp.concatenate([freqs, freqs], axis=-1)
            base = (half_idx + 0.4 * DIM_HEAD) / (1.4 * DIM_HEAD)
            power = (t - n // 2) / float(WINDOW // 2)
            scale = base[None, :] ** power[:, None]
            scale = jnp.concatenate([scale, scale], axis=-1)
            cos, sin = (jnp.cos(freqs), jnp.sin(freqs))
            q = q * cos * scale + rotate_half(q) * sin * scale
            k = k * cos / scale + rotate_half(k) * sin / scale
            return (q, k)

        def local_attention(q, k, v):
            b, h, n, d = q.shape
            w = n // WINDOW
            bq = q.reshape(b, h, w, WINDOW, d) * QK_SCALE
            bk = k.reshape(b, h, w, WINDOW, d)
            bv = v.reshape(b, h, w, WINDOW, d)

            def look_around(t):
                p = jnp.pad(t, ((0, 0), (0, 0), (1, 0), (0, 0), (0, 0)))
                return jnp.concatenate([p[:, :, :w], p[:, :, 1:]], axis=3)
            bk, bv = (look_around(bk), look_around(bv))
            bt = jnp.arange(n).reshape(w, WINDOW)
            btp = jnp.pad(bt, ((1, 0), (0, 0)), constant_values=-1)
            btk = jnp.concatenate([btp[:w], btp[1:]], axis=1)
            sim = jnp.einsum('bhwid,bhwjd->bhwij', bq, bk)
            i = bt[:, :, None]
            j = btk[:, None, :]
            mask = (i < j) | (i > j + WINDOW) | (j == -1)
            sim = jnp.where(mask, -jnp.finfo(sim.dtype).max, sim)
            attn = jax.nn.softmax(sim, axis=-1)
            out = jnp.einsum('bhwij,bhwjd->bhwid', attn, bv)
            return out.reshape(b, h, n, d)

        def _layer(x, wqkv, qs, ksc, wo, lg, lb, w1, b1, w2, b2):
            b, n, _ = x.shape
            h = shift_token(x)
            qkv = h @ wqkv
            q, k, v = jnp.split(qkv, 3, axis=-1)
            to_heads = lambda t: t.reshape(b, n, HEADS, DIM_HEAD).transpose(0, 2, 1, 3)
            q, k, v = (to_heads(q), to_heads(k), to_heads(v))
            q = l2norm(q) * qs
            k = l2norm(k) * ksc
            q, k = rotary_xpos(q, k)
            o = local_attention(q, k, v)
            o = o.transpose(0, 2, 1, 3).reshape(b, n, INNER)
            x = x + o @ wo
            h = shift_token(x)
            mu = h.mean(-1, keepdims=True)
            var = h.var(-1, keepdims=True)
            h = (h - mu) / jnp.sqrt(var + 1e-05) * lg + lb
            h = h @ w1 + b1
            a, g = jnp.split(h, 2, axis=-1)
            h = a * jax.nn.gelu(g, approximate=False)
            x = x + h @ w2 + b2
            return x
        key = jax.random.key(seed)
        ks = jax.random.split(key, 6)
        return {'x': jax.random.normal(ks[0], (B, N, DIM), jnp.float32), 'wqkv': jax.random.normal(ks[1], (DEPTH, DIM, 3 * INNER), jnp.float32) * 0.02, 'q_scale': jnp.ones((DEPTH, DIM_HEAD), jnp.float32), 'k_scale': jnp.ones((DEPTH, DIM_HEAD), jnp.float32), 'wo': jax.random.normal(ks[2], (DEPTH, INNER, DIM), jnp.float32) * 0.02, 'ln_g': jnp.ones((DEPTH, DIM), jnp.float32), 'ln_b': jnp.zeros((DEPTH, DIM), jnp.float32), 'w1': jax.random.normal(ks[3], (DEPTH, DIM, 2 * HID), jnp.float32) * 0.02, 'b1': jnp.zeros((DEPTH, 2 * HID), jnp.float32), 'w2': jax.random.normal(ks[4], (DEPTH, HID, DIM), jnp.float32) * 0.02, 'b2': jnp.zeros((DEPTH, DIM), jnp.float32)}
    _L1_ffn_in = _L1_ffn_setup()
    _L1_c = _w((lambda *s: np.random.randn(*s).astype(np.float32) * 0.05)(4, 128))
    _L1_wmod = _w((lambda *s: np.random.randn(*s).astype(np.float32) * 0.05)(128, 6 * 128) * 128 ** (-0.5))
    _d = {'L0_attn_x': _L0_attn_in['x'], 'L0_attn_wq': _L0_attn_in['wq'], 'L0_attn_bq': _L0_attn_in['bq'], 'L0_attn_wqc': _L0_attn_in['wqc'], 'L0_attn_bqc': _L0_attn_in['bqc'], 'L0_attn_wqr': _L0_attn_in['wqr'], 'L0_attn_bqr': _L0_attn_in['bqr'], 'L0_attn_wkv': _L0_attn_in['wkv'], 'L0_attn_bkv': _L0_attn_in['bkv'], 'L0_attn_wkr': _L0_attn_in['wkr'], 'L0_attn_bkr': _L0_attn_in['bkr'], 'L0_attn_wkc': _L0_attn_in['wkc'], 'L0_attn_bkc': _L0_attn_in['bkc'], 'L0_attn_wv': _L0_attn_in['wv'], 'L0_attn_bv': _L0_attn_in['bv'], 'L0_attn_wo': _L0_attn_in['wo'], 'L0_attn_bo': _L0_attn_in['bo'], 'L0_ffn_Wr': _L0_ffn_in['Wr'], 'L0_ffn_br': _L0_ffn_in['br'], 'L0_ffn_Wg_s': _L0_ffn_in['Wg_s'], 'L0_ffn_bg_s': _L0_ffn_in['bg_s'], 'L0_ffn_Wu_s': _L0_ffn_in['Wu_s'], 'L0_ffn_bu_s': _L0_ffn_in['bu_s'], 'L0_ffn_Wd_s': _L0_ffn_in['Wd_s'], 'L0_ffn_bd_s': _L0_ffn_in['bd_s'], 'L0_ffn_Wg': _L0_ffn_in['Wg'], 'L0_ffn_bg': _L0_ffn_in['bg'], 'L0_ffn_Wu': _L0_ffn_in['Wu'], 'L0_ffn_bu': _L0_ffn_in['bu'], 'L0_ffn_Wd': _L0_ffn_in['Wd'], 'L0_ffn_bd': _L0_ffn_in['bd'], 'L0_c': _L0_c, 'L0_wmod': _L0_wmod, 'L1_attn_W_in': _L1_attn_in['W_in'], 'L1_attn_A_log': _L1_attn_in['A_log'], 'L1_attn_W_B': _L1_attn_in['W_B'], 'L1_attn_W_C': _L1_attn_in['W_C'], 'L1_attn_W_dt': _L1_attn_in['W_dt'], 'L1_attn_b_dt': _L1_attn_in['b_dt'], 'L1_attn_D': _L1_attn_in['D'], 'L1_attn_output_gate': _L1_attn_in['output_gate'], 'L1_attn_W_out': _L1_attn_in['W_out'], 'L1_ffn_wqkv': _L1_ffn_in['wqkv'], 'L1_ffn_q_scale': _L1_ffn_in['q_scale'], 'L1_ffn_k_scale': _L1_ffn_in['k_scale'], 'L1_ffn_wo': _L1_ffn_in['wo'], 'L1_ffn_ln_g': _L1_ffn_in['ln_g'], 'L1_ffn_ln_b': _L1_ffn_in['ln_b'], 'L1_ffn_w1': _L1_ffn_in['w1'], 'L1_ffn_b1': _L1_ffn_in['b1'], 'L1_ffn_w2': _L1_ffn_in['w2'], 'L1_ffn_b2': _L1_ffn_in['b2'], 'L1_c': _L1_c, 'L1_wmod': _L1_wmod}
    _x0 = _d['L0_attn_x']
    _d['L0_attn_x'] = jax.random.normal(jax.random.fold_in(jax.random.key(seed), 1), (4, 1024, 128), dtype=_x0.dtype)
    del _x0
    return _d

def reference(L0_attn_x, L0_attn_wq, L0_attn_bq, L0_attn_wqc, L0_attn_bqc, L0_attn_wqr, L0_attn_bqr, L0_attn_wkv, L0_attn_bkv, L0_attn_wkr, L0_attn_bkr, L0_attn_wkc, L0_attn_bkc, L0_attn_wv, L0_attn_bv, L0_attn_wo, L0_attn_bo, L0_ffn_Wr, L0_ffn_br, L0_ffn_Wg_s, L0_ffn_bg_s, L0_ffn_Wu_s, L0_ffn_bu_s, L0_ffn_Wd_s, L0_ffn_bd_s, L0_ffn_Wg, L0_ffn_bg, L0_ffn_Wu, L0_ffn_bu, L0_ffn_Wd, L0_ffn_bd, L0_c, L0_wmod, L1_attn_W_in, L1_attn_A_log, L1_attn_W_B, L1_attn_W_C, L1_attn_W_dt, L1_attn_b_dt, L1_attn_D, L1_attn_output_gate, L1_attn_W_out, L1_ffn_wqkv, L1_ffn_q_scale, L1_ffn_k_scale, L1_ffn_wo, L1_ffn_ln_g, L1_ffn_ln_b, L1_ffn_w1, L1_ffn_b1, L1_ffn_w2, L1_ffn_b2, L1_c, L1_wmod):

    def _L0_attn_ref(x, wq, bq, wqc, bqc, wqr, bqr, wkv, bkv, wkr, bkr, wkc, bkc, wv, bv, wo, bo):
        import jax, jax.numpy as jnp
        import numpy as np
        import math
        B, S, E = (2, 256, 128)
        H, DC, DR = (16, 32, 128)
        HD = E // H

        def _linear_params(key, din, dout):
            k1, k2 = jax.random.split(key)
            bound = 1.0 / math.sqrt(din)
            w = jax.random.uniform(k1, (din, dout), minval=-bound, maxval=bound, dtype=jnp.float32)
            b = jax.random.uniform(k2, (dout,), minval=-bound, maxval=bound, dtype=jnp.float32)
            return (w, b)

        def _gelu(x):
            return jax.nn.gelu(x, approximate=False)

        def _rope_cos_sin(seq_len, d_rope):
            inv_freq = 1.0 / 10000.0 ** (jnp.arange(0, d_rope, 2, dtype=jnp.float32) / d_rope)
            t = jnp.arange(seq_len, dtype=jnp.float32)
            freqs = t[:, None] * inv_freq[None, :]
            emb = jnp.concatenate([freqs, freqs], axis=-1)
            return (jnp.cos(emb), jnp.sin(emb))

        def _apply_rope(x, cos, sin):
            d = x.shape[-1]
            x1, x2 = (x[..., :d // 2], x[..., d // 2:])
            rot = jnp.concatenate([-x2, x1], axis=-1)
            return x * cos + rot * sin
        b, s, _ = x.shape
        cq = _gelu(x @ wq + bq)
        q_c = cq @ wqc + bqc
        q_r = x @ wqr + bqr
        ckv = _gelu(x @ wkv + bkv)
        k_r = x @ wkr + bkr
        k_c = ckv @ wkc + bkc
        v = (ckv @ wv + bv).reshape(b, s, H, HD).transpose(0, 2, 1, 3)
        cos, sin = _rope_cos_sin(s, DR)
        q_r = _apply_rope(q_r, cos, sin)
        k_r = _apply_rope(k_r, cos, sin)
        q = _gelu(jnp.concatenate([q_c, q_r], axis=-1)).reshape(b, s, H, HD).transpose(0, 2, 1, 3)
        k = _gelu(jnp.concatenate([k_c, k_r], axis=-1)).reshape(b, s, H, HD).transpose(0, 2, 1, 3)
        scale = 1.0 / math.sqrt(HD)
        scores = jnp.einsum('bhqd,bhkd->bhqk', q, k) * scale
        causal = jnp.triu(jnp.ones((s, s), dtype=bool), k=1)
        scores = jnp.where(causal[None, None], -jnp.inf, scores)
        attn = jax.nn.softmax(scores, axis=-1)
        out = jnp.einsum('bhqk,bhkd->bhqd', attn, v)
        out = out.transpose(0, 2, 1, 3).reshape(b, s, E)
        return out @ wo + bo

    def _L0_ffn_ref(hidden_states, Wr, br, Wg_s, bg_s, Wu_s, bu_s, Wd_s, bd_s, Wg, bg, Wu, bu, Wd, bd):
        import jax, jax.numpy as jnp
        import numpy as np
        H, I, E, K = (128, 64, 32, 8)
        B, S = (4, 128)

        def silu(x):
            return x * jax.nn.sigmoid(x)
        b, s, h = hidden_states.shape
        T = b * s
        x = hidden_states.reshape(T, h)
        logits = jnp.dot(x.astype(jnp.float32), Wr) + br
        aff = jax.nn.sigmoid(logits)
        top_v, top_i = jax.lax.top_k(aff, K)
        top_w = top_v / (jnp.sum(top_v, axis=-1, keepdims=True) + 1e-09)
        top_w = top_w.astype(hidden_states.dtype)
        e_total = Wr.shape[1]
        w_full = jnp.zeros((T, e_total), hidden_states.dtype)
        w_full = w_full.at[jnp.arange(T)[:, None], top_i].set(top_w)
        shared = jnp.dot(silu(jnp.dot(x, Wg_s) + bg_s) * (jnp.dot(x, Wu_s) + bu_s), Wd_s) + bd_s
        gate = silu(jnp.einsum('th,ehi->eti', x, Wg) + bg[:, None, :])
        up = jnp.einsum('th,ehi->eti', x, Wu) + bu[:, None, :]
        down = jnp.einsum('eti,eih->eth', gate * up, Wd) + bd[:, None, :]
        routed = jnp.einsum('te,eth->th', w_full, down)
        return (shared + routed).reshape(b, s, h)

    def _L1_attn_ref(x, W_in, A_log, W_B, W_C, W_dt, b_dt, D, output_gate, W_out):
        import math
        import jax, jax.numpy as jnp
        import numpy as np
        D_MODEL = 128
        NUM_SCALES = 4
        STATE_SIZE = 16
        EXPAND = 2
        D_INNER = D_MODEL * EXPAND
        D_PER_SCALE = D_INNER // NUM_SCALES
        BATCH, SEQ = (4, 512)

        def _make_A_log():
            base = np.arange(1, STATE_SIZE + 1, dtype=np.float32)
            parts = [np.broadcast_to(base * 2.0 ** i, (D_PER_SCALE, STATE_SIZE)) for i in range(NUM_SCALES)]
            A = np.concatenate(parts, axis=0)
            return jnp.asarray(np.log(A))

        def _selective_scan(x_ssm, A, B_mat, C_mat, dt):
            b, L, d = x_ssm.shape
            N = A.shape[1]
            h0 = jnp.zeros((b, d, N), dtype=jnp.float32)

            def step(h, inp):
                dt_t, B_t, C_t, x_t = inp
                A_bar = jnp.exp(jnp.minimum(dt_t[..., None] * A, 20.0))
                B_bar = dt_t[..., None] * B_t[:, None, :]
                h = A_bar * h + B_bar * x_t[..., None]
                y_t = jnp.einsum('bdn,bn->bd', h, C_t)
                return (h, y_t)
            xs = (jnp.swapaxes(dt, 0, 1), jnp.swapaxes(B_mat, 0, 1), jnp.swapaxes(C_mat, 0, 1), jnp.swapaxes(x_ssm, 0, 1))
            _, ys = jax.lax.scan(step, h0, xs)
            return jnp.swapaxes(ys, 0, 1)
        xz = jnp.einsum('bld,ed->ble', x, W_in)
        x_ssm, z = jnp.split(xz, 2, axis=-1)
        A = -jnp.exp(A_log.astype(jnp.float32))
        B_mat = jnp.einsum('bld,nd->bln', x_ssm, W_B)
        C_mat = jnp.einsum('bld,nd->bln', x_ssm, W_C)
        dt = jax.nn.softplus(jnp.einsum('bld,ed->ble', x_ssm, W_dt) + b_dt)
        y = _selective_scan(x_ssm.astype(jnp.float32), A, B_mat.astype(jnp.float32), C_mat.astype(jnp.float32), dt.astype(jnp.float32))
        y = y + x_ssm * D[None, None, :]
        y = y * jax.nn.silu(z)
        out = jnp.einsum('ble,de->bld', y, W_out) * jax.nn.sigmoid(output_gate)
        return out

    def _L1_ffn_ref(x, wqkv, q_scale, k_scale, wo, ln_g, ln_b, w1, b1, w2, b2):
        import jax, jax.numpy as jnp
        import numpy as np
        DIM = 128
        DEPTH = 2
        HEADS = 8
        DIM_HEAD = 64
        WINDOW = 64
        INNER = HEADS * DIM_HEAD
        HID = int(DIM * 4 * 2 / 3)
        B, N = (2, 1024)
        QK_SCALE = 8.0

        def shift_token(t):
            t1, t2 = jnp.split(t, 2, axis=-1)
            t2 = jnp.pad(t2, ((0, 0), (1, 0), (0, 0)))[:, :-1]
            return jnp.concatenate([t1, t2], axis=-1)

        def l2norm(t):
            return t / jnp.clip(jnp.linalg.norm(t, axis=-1, keepdims=True), 1e-12)

        def rotate_half(x):
            x1, x2 = jnp.split(x, 2, axis=-1)
            return jnp.concatenate([-x2, x1], axis=-1)

        def rotary_xpos(q, k):
            n = q.shape[-2]
            half_idx = jnp.arange(0, DIM_HEAD, 2, dtype=jnp.float32)
            inv_freq = 1.0 / 10000.0 ** (half_idx / DIM_HEAD)
            t = jnp.arange(n, dtype=jnp.float32)
            freqs = t[:, None] * inv_freq[None, :]
            freqs = jnp.concatenate([freqs, freqs], axis=-1)
            base = (half_idx + 0.4 * DIM_HEAD) / (1.4 * DIM_HEAD)
            power = (t - n // 2) / float(WINDOW // 2)
            scale = base[None, :] ** power[:, None]
            scale = jnp.concatenate([scale, scale], axis=-1)
            cos, sin = (jnp.cos(freqs), jnp.sin(freqs))
            q = q * cos * scale + rotate_half(q) * sin * scale
            k = k * cos / scale + rotate_half(k) * sin / scale
            return (q, k)

        def local_attention(q, k, v):
            b, h, n, d = q.shape
            w = n // WINDOW
            bq = q.reshape(b, h, w, WINDOW, d) * QK_SCALE
            bk = k.reshape(b, h, w, WINDOW, d)
            bv = v.reshape(b, h, w, WINDOW, d)

            def look_around(t):
                p = jnp.pad(t, ((0, 0), (0, 0), (1, 0), (0, 0), (0, 0)))
                return jnp.concatenate([p[:, :, :w], p[:, :, 1:]], axis=3)
            bk, bv = (look_around(bk), look_around(bv))
            bt = jnp.arange(n).reshape(w, WINDOW)
            btp = jnp.pad(bt, ((1, 0), (0, 0)), constant_values=-1)
            btk = jnp.concatenate([btp[:w], btp[1:]], axis=1)
            sim = jnp.einsum('bhwid,bhwjd->bhwij', bq, bk)
            i = bt[:, :, None]
            j = btk[:, None, :]
            mask = (i < j) | (i > j + WINDOW) | (j == -1)
            sim = jnp.where(mask, -jnp.finfo(sim.dtype).max, sim)
            attn = jax.nn.softmax(sim, axis=-1)
            out = jnp.einsum('bhwij,bhwjd->bhwid', attn, bv)
            return out.reshape(b, h, n, d)

        def _layer(x, wqkv, qs, ksc, wo, lg, lb, w1, b1, w2, b2):
            b, n, _ = x.shape
            h = shift_token(x)
            qkv = h @ wqkv
            q, k, v = jnp.split(qkv, 3, axis=-1)
            to_heads = lambda t: t.reshape(b, n, HEADS, DIM_HEAD).transpose(0, 2, 1, 3)
            q, k, v = (to_heads(q), to_heads(k), to_heads(v))
            q = l2norm(q) * qs
            k = l2norm(k) * ksc
            q, k = rotary_xpos(q, k)
            o = local_attention(q, k, v)
            o = o.transpose(0, 2, 1, 3).reshape(b, n, INNER)
            x = x + o @ wo
            h = shift_token(x)
            mu = h.mean(-1, keepdims=True)
            var = h.var(-1, keepdims=True)
            h = (h - mu) / jnp.sqrt(var + 1e-05) * lg + lb
            h = h @ w1 + b1
            a, g = jnp.split(h, 2, axis=-1)
            h = a * jax.nn.gelu(g, approximate=False)
            x = x + h @ w2 + b2
            return x
        for l in range(DEPTH):
            x = _layer(x, wqkv[l], q_scale[l], k_scale[l], wo[l], ln_g[l], ln_b[l], w1[l], b1[l], w2[l], b2[l])
        return x
    x = L0_attn_x
    mod = (_silu(L0_c) @ L0_wmod).reshape(L0_c.shape[0], 6, 1, -1)
    sa, ca, ga, sb, cb, gb = (mod[:, 0], mod[:, 1], mod[:, 2], mod[:, 3], mod[:, 4], mod[:, 5])
    ga = (2 * (ga >= 0) - 1) * jnp.maximum(jnp.abs(ga), 0.25)
    gb = (2 * (gb >= 0) - 1) * jnp.maximum(jnp.abs(gb), 0.25)
    h = _layernorm(x, axis=-1) * (1 + ca) + sa
    x = x + ga * _L0_attn_ref(h, L0_attn_wq, L0_attn_bq, L0_attn_wqc, L0_attn_bqc, L0_attn_wqr, L0_attn_bqr, L0_attn_wkv, L0_attn_bkv, L0_attn_wkr, L0_attn_bkr, L0_attn_wkc, L0_attn_bkc, L0_attn_wv, L0_attn_bv, L0_attn_wo, L0_attn_bo)
    h = _layernorm(x, axis=-1) * (1 + cb) + sb
    x = x + gb * _L0_ffn_ref(h, L0_ffn_Wr, L0_ffn_br, L0_ffn_Wg_s, L0_ffn_bg_s, L0_ffn_Wu_s, L0_ffn_bu_s, L0_ffn_Wd_s, L0_ffn_bd_s, L0_ffn_Wg, L0_ffn_bg, L0_ffn_Wu, L0_ffn_bu, L0_ffn_Wd, L0_ffn_bd)
    mod = (_silu(L1_c) @ L1_wmod).reshape(L1_c.shape[0], 6, 1, -1)
    sa, ca, ga, sb, cb, gb = (mod[:, 0], mod[:, 1], mod[:, 2], mod[:, 3], mod[:, 4], mod[:, 5])
    ga = (2 * (ga >= 0) - 1) * jnp.maximum(jnp.abs(ga), 0.25)
    gb = (2 * (gb >= 0) - 1) * jnp.maximum(jnp.abs(gb), 0.25)
    h = _layernorm(x, axis=-1) * (1 + ca) + sa
    x = x + ga * _L1_attn_ref(h, L1_attn_W_in, L1_attn_A_log, L1_attn_W_B, L1_attn_W_C, L1_attn_W_dt, L1_attn_b_dt, L1_attn_D, L1_attn_output_gate, L1_attn_W_out)
    h = _layernorm(x, axis=-1) * (1 + cb) + sb
    x = x + gb * _L1_ffn_ref(h, L1_ffn_wqkv, L1_ffn_q_scale, L1_ffn_k_scale, L1_ffn_wo, L1_ffn_ln_g, L1_ffn_ln_b, L1_ffn_w1, L1_ffn_b1, L1_ffn_w2, L1_ffn_b2)
    return x

_drawn_inputs = setup_inputs


def setup_inputs(seed=0):
    import zlib

    import numpy as np

    out = dict(_drawn_inputs(seed))
    spreads = {'L0_ffn_br': (0.0, 0.466),
     'L0_ffn_bg_s': (0.0, 0.544),
     'L0_ffn_bu_s': (0.0, 0.594),
     'L0_ffn_bd_s': (0.0, 0.337),
     'L0_ffn_bg': (0.0, 0.8),
     'L0_ffn_bu': (0.0, 0.8),
     'L0_ffn_bd': (0.0, 0.8),
     'L1_attn_D': (1.0, 0.6),
     'L1_ffn_q_scale': (1.0, 0.6),
     'L1_ffn_k_scale': (1.0, 0.6),
     'L1_ffn_ln_g': (1.0, 0.6),
     'L1_ffn_ln_b': (0.0, 0.8),
     'L1_ffn_b1': (0.0, 0.8),
     'L1_ffn_b2': (0.0, 0.8)}
    factors = {'L0_attn_wqr': 8.0,
     'L0_attn_bqr': 8.0,
     'L0_attn_wkv': 8.0,
     'L0_attn_bkv': 8.0,
     'L0_attn_wkr': 8.0,
     'L0_attn_bkr': 8.0,
     'L0_attn_wv': 5.35,
     'L0_attn_bv': 3.178,
     'L0_attn_bo': 4.288,
     'L1_attn_W_in': 8.0,
     'L1_attn_A_log': 8.0,
     'L1_attn_W_B': 8.0,
     'L1_attn_W_C': 8.0,
     'L1_attn_W_dt': 8.0,
     'L1_attn_b_dt': 8.0,
     'L1_attn_W_out': 8.0,
     'L1_ffn_wqkv': 7.911,
     'L1_ffn_wo': 7.901,
     'L1_ffn_w1': 8.0,
     'L1_ffn_w2': 8.0}
    for name, (base, spread) in spreads.items():
        noise = np.random.default_rng([zlib.crc32(name.encode()), seed]).standard_normal(out[name].shape)
        drawn = base * np.exp(spread * noise) if base else spread * noise
        out[name] = jnp.asarray(drawn.astype(out[name].dtype))
    for name, factor in factors.items():
        out[name] = (out[name] * factor).astype(out[name].dtype)
    return out
```

```python
import numpy as np
from contextlib import ExitStack

import concourse.bass as bass
from concourse import mybir

FP = mybir.dt.float32
BF = mybir.dt.bfloat16
ALU = mybir.AluOpType
ACT = mybir.ActivationFunctionType
AX = mybir.AxisListType

P = 128
B = 4
S = 1024
E = 128
TOK = B * S
NT = TOK // P
TPB = S // P
CH = 512
NCH = TOK // CH
TPC = CH // P
MASKED = -3.0e38
LN_EPS = 1e-5

H0, HD0 = 16, 8
G0 = 4
NG0 = H0 // G0
TERMS = 6
KQK = TERMS * HD0
KQM = KQK + 3
QPART = (0, 0, 1, 1, 0, 2)
KPART = (0, 1, 0, 1, 2, 0)
NE, NI, TOPK = 32, 64, 8
NP_ = NE // 2
DI, NS = 256, 16
NH = DI // P
DEPTH, HL, DL, WIN = 2, 8, 64, 64
INNER = HL * DL
HID = 341
NHID = 3
KW = P + WIN


class Layout:

    def __init__(self, parts):
        self.at, n = {}, 0
        for name, w in parts:
            self.at[name] = (n, w)
            n += w
        self.width = n

    def __call__(self, tile, name, rows=P):
        n, w = self.at[name]
        return tile[0:rows, n:n + w]


MOD = Layout([("cT0", B), ("cT1", B), ("wmod0", 6 * E), ("wmod1", 6 * E)])
L0A = Layout([("wqr", E), ("wqr_rot", E), ("wkr", E), ("wkr_rot", E), ("wkv", 32), ("wv", E), ("wo", E),
              ("bqr", 1), ("bqr_rot", 1), ("bkr", 1), ("bkr_rot", 1), ("bkv", 1), ("bo", E),
              ("cos", S), ("sin", S)])
L0F = Layout([("Wr", NE), ("br", NE), ("Wg_s", NI), ("Wu_s", NI), ("Wd_s", E), ("bg_s", 1), ("bu_s", 1),
              ("bd_s", 1), ("bg", NP_), ("bu", NP_), ("bd", E),
              ("Wg", NE * NI), ("Wu", NE * NI), ("Wd", NP_ * E)])
L1A = Layout([("W_in", 2 * DI), ("W_bc", NH * 96), ("W_dt", NH * DI), ("b_dt", NH), ("A_log", NH * NS),
              ("D", NH), ("gate", 1), ("W_out", NH * E)])
L1F_ONE = [("wqkv", 3 * INNER), ("wo", 4 * E), ("ln_g", 1), ("ln_b", 1), ("w1a", NHID * P), ("w1g", NHID * P),
           ("b1a", NHID), ("b1g", NHID), ("w2", NHID * E), ("b2", 1), ("qs", DL), ("ks", DL)]
L1F = Layout([(f"{n}{l}", w) for l in range(DEPTH) for n, w in L1F_ONE]
             + [(t, TPB * DL) for t in ("cos_q", "sin_q", "cos_k", "sin_k")])
SA, CA, GA, SB, CB, GB = range(6)


def build(nc, dram, out):
    ctx = ExitStack()
    with ctx:
        sb = lambda name, shape, dt=FP: ctx.enter_context(nc.sbuf_tensor(name, shape, dt))
        resid = sb("resid", [P, NT * E])
        hT = sb("hT", [P, TOK + B])
        mod = sb("mod", [P, 2 * 6 * B])
        ident = sb("ident", [P, P])
        ident_bf = sb("ident_bf", [P, P], BF)
        w_even = sb("w_even", [P, max(L0A.width, L1A.width)])
        w_odd = sb("w_odd", [P, max(L0F.width, L1F.width)])
        ps = ctx.enter_context(nc.psum_tensor("ps", [P, 8, CH], FP))
        g = dict(resid=resid, hT=hT, mod=mod, ident=ident, ident_bf=ident_bf, ps=ps,
                 w_even=w_even, w_odd=w_odd, taken=[])
        sems = {n: ctx.enter_context(nc.semaphore(n)) for n in
                ("x_loaded", "mod_loaded", "l0a_loaded", "l0f_loaded", "l1a_loaded", "l1f_loaded")}
        g.update(sems)
        setup(nc, dram, g)
        layer_norm(nc, g, "n0", 0, CA, SA)
        causal_attention(nc, dram, g)
        layer_norm(nc, g, "n1", 0, CB, SB)
        experts(nc, dram, g)
        layer_norm(nc, g, "n2", 1, CA, SA)
        state_space(nc, dram, g)
        layer_norm(nc, g, "n3", 1, CB, SB, pad=1)
        local_transformer(nc, dram, g)
        store(nc, g, out)


def take_semaphore(nc, g, name):
    s = nc.alloc_semaphore(name=name)
    g["taken"].append(s)
    return s


def mod_col(layer, which, b):
    return (layer * 6 + which) * B + b


def setup(nc, dram, g):
    with ExitStack() as ctx:
        sb = lambda name, shape, dt=FP: ctx.enter_context(nc.sbuf_tensor(name, shape, dt))
        sem = lambda name: take_semaphore(nc, g, name)
        w = sb("su_w", [P, MOD.width])
        c_act = sb("su_c", [P, 2 * B])
        gates = sb("su_g", [P, 4 * B])
        sign = sb("su_s", [P, 4 * B])
        zero_set, ident_set, ident_cast, silu_done = sem("su_z"), sem("su_i"), sem("su_ib"), sem("su_silu")
        mod_ready, mod_copied, step = sem("su_mm"), sem("su_mc"), sem("su_st")
        ps, mod, ident = g["ps"], g["mod"], g["ident"]
        with nc.Block() as block:
            @block.sync
            def _(sp):
                sp.dma_start(w[:, :], dram["w_mod"]).then_inc(g["mod_loaded"], 16)
                for b in range(B):
                    sp.dma_start(g["resid"][:, b * TPB * E:(b + 1) * TPB * E].rearrange("p (t e) -> p t e", e=E),
                                 dram["x"][b].rearrange("(t p) e -> p t e", p=P)).then_inc(g["x_loaded"], 16)
                sp.dma_start(g["w_even"][:, 0:L0A.width], dram["w_l0a"]).then_inc(g["l0a_loaded"], 16)
                sp.dma_start(g["w_odd"][:, 0:L0F.width], dram["w_l0f"]).then_inc(g["l0f_loaded"], 16)

            @block.gpsimd
            def _(pool):
                nc.gpsimd.memset(ident[:, :], 0.0).then_inc(zero_set, 1)
                pool.wait_ge(zero_set, 1)
                nc.gpsimd.affine_select(out=ident[:, :], in_=ident[:, :], compare_op=ALU.not_equal, fill=1.0,
                                        base=0, pattern=[[-1, P]], channel_multiplier=1).then_inc(ident_set, 1)
                pool.wait_ge(ident_set, 1)
                nc.gpsimd.tensor_copy(g["ident_bf"][:, :], ident[:, :]).then_inc(ident_cast, 1)

            @block.scalar
            def _(act):
                act.wait_ge(g["mod_loaded"], 16)
                nc.scalar.activation(c_act[:, :], w[:, 0:2 * B], ACT.Silu).then_inc(silu_done, 1)

            @block.tensor
            def _(pe):
                pe.wait_ge(silu_done, 1)
                for layer in range(2):
                    wm = MOD(w, f"wmod{layer}")
                    for k in range(6):
                        at = mod_col(layer, k, 0)
                        mm = nc.tensor.matmul(ps[:, 0, at:at + B], wm[:, k * E:(k + 1) * E],
                                              c_act[:, layer * B:(layer + 1) * B], start=True, stop=True)
                mm.then_inc(mod_ready, 1)

            @block.vector
            def _(dve):
                dve.wait_ge(mod_ready, 1)
                nc.vector.tensor_copy(mod[:, :], ps[:, 0, 0:2 * 6 * B]).then_inc(step, 1)
                dve.wait_ge(step, 1)
                n = 1
                for layer in range(2):
                    for k in (CA, CB):
                        at = mod_col(layer, k, 0)
                        nc.vector.tensor_scalar(mod[:, at:at + B], mod[:, at:at + B], 1.0, None, ALU.add).then_inc(step, 1)
                        n += 1
                    for k in (GA, GB):
                        at = mod_col(layer, k, 0)
                        s = (2 * layer + (k == GB)) * B
                        nc.vector.tensor_scalar(sign[:, s:s + B], mod[:, at:at + B], 0.0, 2.0, ALU.is_ge,
                                                ALU.mult).then_inc(step, 1)
                        nc.vector.tensor_scalar(gates[:, s:s + B], mod[:, at:at + B], -1.0, None, ALU.mult).then_inc(step, 1)
                        n += 2
                        dve.wait_ge(step, n)
                        nc.vector.scalar_tensor_tensor(gates[:, s:s + B], gates[:, s:s + B], 0.25, mod[:, at:at + B],
                                                       ALU.max, ALU.max).then_inc(step, 1)
                        n += 1
                        dve.wait_ge(step, n)
                        nc.vector.scalar_tensor_tensor(mod[:, at:at + B], sign[:, s:s + B], -1.0, gates[:, s:s + B],
                                                       ALU.add, ALU.mult).then_inc(step, 1)
                        n += 1


def layer_norm(nc, g, tag, layer, scale, shift, pad=0):
    with ExitStack() as ctx:
        spent, g["taken"] = g["taken"], []
        sb = lambda name, shape, dt=FP: ctx.enter_context(nc.sbuf_tensor(tag + name, shape, dt))
        sem = lambda name: take_semaphore(nc, g, tag + name)
        stats = sb("stats", [P, NT * 6])
        mv = sb("mv", [P, 2 * NT])
        rstd = sb("rstd", [P, NT])
        power = sb("power", [P, NT])
        xh = [sb(f"xh{i}", [P, CH]) for i in range(2)]
        stats_step, mv_ready, pow_set, rstd_ready = sem("ss"), sem("mv"), sem("pw"), sem("rs")
        xh_ready, t_ready, t_copied = sem("xh"), sem("tr"), sem("tc")
        resid, hT, mod, ps = g["resid"], g["hT"], g["mod"], g["ps"]
        mv3 = mv[:, :].rearrange("p (t two) -> p t two", two=2)
        with nc.Block() as block:
            @block.gpsimd
            def _(pool):
                nc.gpsimd.memset(power[:, :], -0.5).then_inc(pow_set, 1)
                for s in spent:
                    pool.sem_clear(s)
                pool.wait_ge(pow_set, 1)
                pool.wait_ge(mv_ready, 1)
                nc.gpsimd.tensor_scalar(rstd[:, :], mv3[:, :, 1], LN_EPS, None, ALU.add).then_inc(pow_set, 1)
                pool.wait_ge(pow_set, 2)
                nc.gpsimd.tensor_tensor(rstd[:, :], rstd[:, :], power[:, :], ALU.pow).then_inc(rstd_ready, 1)

            @block.vector
            def _(dve):
                dve.wait_ge(g["x_loaded"], 16 * B)
                for t in range(NT):
                    nc.vector.bn_stats(stats[:, 6 * t:6 * t + 6], resid[:, t * E:(t + 1) * E]).then_inc(stats_step, 1)
                dve.wait_ge(stats_step, NT)
                for t in range(NT):
                    last = nc.vector.bn_aggr(mv[:, 2 * t:2 * t + 2], stats[:, 6 * t:6 * t + 6])
                last.then_inc(mv_ready, 1)
                dve.wait_ge(rstd_ready, 1)
                for c in range(NCH):
                    if c >= 2:
                        dve.wait_ge(t_ready, c - 1)
                    for j in range(TPC):
                        t = c * TPC + j
                        last = nc.vector.tensor_scalar(xh[c % 2][:, j * P:(j + 1) * P], resid[:, t * E:(t + 1) * E],
                                                       mv[:, 2 * t:2 * t + 1], rstd[:, t:t + 1], ALU.subtract, ALU.mult)
                    last.then_inc(xh_ready, 1)

            @block.tensor
            def _(pe):
                for c in range(NCH):
                    pe.wait_ge(xh_ready, c + 1)
                    if c >= 2:
                        pe.wait_ge(t_copied, c - 1)
                    for j in range(TPC):
                        last = nc.tensor.transpose(ps[:, c % 2, j * P:(j + 1) * P], xh[c % 2][:, j * P:(j + 1) * P],
                                                   g["ident"][:, :])
                    last.then_inc(t_ready, 1)

            @block.scalar
            def _(act):
                for c in range(NCH):
                    b = c // (S // CH)
                    sc, sh = mod_col(layer, scale, b), mod_col(layer, shift, b)
                    act.wait_ge(t_ready, c + 1)
                    at = c * CH + pad * (b + 1)
                    nc.scalar.activation(hT[:, at:at + CH], ps[:, c % 2, :], ACT.Identity,
                                         bias=mod[:, sh:sh + 1], scale=mod[:, sc:sc + 1]).then_inc(t_copied, 1)
    for s in spent:
        nc.release_semaphore(s)


def causal_attention(nc, dram, g):
    parts = nc.dram_tensor("qk_parts", [2, H0, TERMS, HD0, TOK], BF, kind="Internal").ap()
    with ExitStack() as ctx:
        v_tok = ctx.enter_context(nc.sbuf_tensor("ca_v", [P, NT * E], FP))
        o_tok = ctx.enter_context(nc.sbuf_tensor("ca_o", [P, NT * E], FP))
        project(nc, g, parts, v_tok)
        attend(nc, g, parts, v_tok, o_tok)
        attention_out(nc, g, o_tok)


def project(nc, g, parts, v_tok):
    with ExitStack() as ctx:
        sb = lambda name, shape, dt=FP: ctx.enter_context(nc.sbuf_tensor("pj_" + name, shape, dt))
        sem = lambda name: take_semaphore(nc, g, "pj_" + name)
        hT, ps, w = g["hT"], g["ps"], g["w_even"]
        straight = sb("straight", [P, 2, CH])
        turned = sb("turned", [P, 2, CH])
        act_out = [sb(f"act{i}", [P, 2, CH]) for i in range(2)]
        rest = sb("rest", [P, 2, CH])
        piece = [[sb(f"piece{i}{k}", [P, 2, CH], BF) for k in range(3)] for i in range(2)]
        ckv = [sb(f"ckv{i}", [33, CH]) for i in range(2)]
        proj_ready, proj_free = sem("pr"), sem("pf")
        rot_step, gelu_ready, ckv_ready, v_ready, v_copied = sem("rt"), sem("gl"), sem("cr"), sem("vr"), sem("vc")
        split_step, ones_set = sem("sp"), sem("on")
        pool_past = sem("pp")
        stored = [sem(f"st{i}") for i in range(2)]
        STORES = 2 * TERMS * 16
        with nc.Block() as block:
            @block.tensor
            def _(pe):
                pe.wait_ge(g["l0a_loaded"], 16)

                def chunk(c, half):
                    pe.wait_ge(proj_free, 2 * c + 2)
                    rhs = hT[:, bass.ds(c * CH, CH)]
                    for k, name in enumerate(("wqr", "wqr_rot", "wkr", "wkr_rot")):
                        nc.tensor.matmul(ps[:, k, :], L0A(w, name), rhs, start=True, stop=True)
                    nc.tensor.matmul(ps[0:32, 4, :], L0A(w, "wkv"), rhs, start=True, stop=True).then_inc(proj_ready, 1)
                    pe.wait_ge(ckv_ready, c + 1)
                    pe.wait_ge(v_copied, c + 1)
                    for j in range(TPC):
                        last = nc.tensor.matmul(ps[:, 5, j * P:(j + 1) * P], ckv[half][:, j * P:(j + 1) * P],
                                                L0A(w, "wv", 33), start=True, stop=True)
                    last.then_inc(v_ready, 1)

                with pe.Fori(0, NCH // 2) as i:
                    for half in range(2):
                        chunk(i * 2 + half, half)

            @block.vector
            def _(dve):
                dve.sem_inc(proj_free, 1)
                for half in range(2):
                    nc.vector.memset(ckv[half][32:33, :], 1.0).then_inc(ones_set, 1)
                dve.wait_ge(g["l0a_loaded"], 16)

                def chunk(i, half):
                    c = i * 2 + half
                    dve.wait_ge(proj_ready, c + 1)
                    dve.wait_ge(gelu_ready, c + 1)
                    cos = w[:, L0A.at["cos"][0] + half * CH:L0A.at["cos"][0] + (half + 1) * CH]
                    sin = w[:, L0A.at["sin"][0] + half * CH:L0A.at["sin"][0] + (half + 1) * CH]
                    for k, n in enumerate(("bqr", "bkr")):
                        nc.vector.scalar_tensor_tensor(straight[:, k, :], ps[:, 2 * k, :], L0A(w, n), cos,
                                                       ALU.add, ALU.mult).then_inc(rot_step, 1)
                        last = nc.vector.scalar_tensor_tensor(turned[:, k, :], ps[:, 2 * k + 1, :], L0A(w, n + "_rot"),
                                                              sin, ALU.add, ALU.mult)
                        last.then_inc(rot_step, 1)
                    dve.wait_ge(rot_step, 5 * c + 4)
                    nc.vector.tensor_tensor(straight[:, :, :], straight[:, :, :], turned[:, :, :],
                                            ALU.add).then_inc(rot_step, 1)
                    dve.wait_ge(rot_step, 5 * c + 5)
                    dve.sem_inc(proj_free, 1)

                with dve.Fori(0, NCH // 2) as i:
                    for half in range(2):
                        chunk(i, half)

            @block.scalar
            def _(act):
                nc.scalar.preload_act_table_set("gelu_and_others")
                act.sem_inc(proj_free, 1)
                act.sem_inc(gelu_ready, 1)
                act.sem_inc(v_copied, 1)
                act.wait_ge(ones_set, 2)
                act.wait_ge(g["l0a_loaded"], 16)

                def chunk(i, half):
                    c = i * 2 + half
                    act.wait_ge(proj_ready, c + 1)
                    nc.scalar.activation(ckv[half][0:32, :], ps[0:32, 4, :], ACT.Gelu,
                                         bias=L0A(w, "bkv", 32)).then_inc(ckv_ready, 1)
                    act.wait_ge(ckv_ready, c + 1)
                    act.sem_inc(proj_free, 1)
                    act.wait_ge(rot_step, 5 * c + 5)
                    act.wait_ge(split_step, 5 * c + 5)
                    nc.scalar.activation(act_out[half][:, :, :], straight[:, :, :], ACT.Gelu).then_inc(gelu_ready, 1)
                    act.wait_ge(v_ready, c + 1)
                    nc.scalar.activation(v_tok[:, bass.ds(c * CH, CH)], ps[:, 5, :], ACT.Copy).then_inc(v_copied, 1)

                with act.Fori(0, NCH // 2) as i:
                    for half in range(2):
                        chunk(i, half)

            @block.gpsimd
            def _(pool):
                pool.sem_inc(split_step, 5)
                for half in range(2):
                    pool.sem_inc(stored[half], STORES)

                def chunk(i, half):
                    c = i * 2 + half
                    x = act_out[half][:, :, :]
                    p = [t[:, :, :] for t in piece[half]]
                    pool.wait_ge(gelu_ready, c + 2)
                    pool.wait_ge(stored[half], i * STORES + STORES)
                    pool.sem_inc(pool_past, 1)
                    ops = (lambda: nc.gpsimd.tensor_copy(p[0], x),
                           lambda: nc.gpsimd.tensor_tensor(rest[:, :, :], x, p[0], ALU.subtract),
                           lambda: nc.gpsimd.tensor_copy(p[1], rest[:, :, :]),
                           lambda: nc.gpsimd.tensor_tensor(rest[:, :, :], rest[:, :, :], p[1], ALU.subtract),
                           lambda: nc.gpsimd.tensor_copy(p[2], rest[:, :, :]))
                    for n, op in enumerate(ops):
                        op().then_inc(split_step, 1)
                        pool.wait_ge(split_step, 5 * c + 6 + n)
                        pool.sem_inc(pool_past, 1)

                with pool.Fori(0, NCH // 2) as i:
                    for half in range(2):
                        chunk(i, half)

            @block.sync
            def _(sp):
                with sp.Fori(0, NCH // 2) as i:
                    for half in range(2):
                        c = i * 2 + half
                        sp.wait_ge(split_step, 5 * c + 10)
                        for op, use in enumerate((QPART, KPART)):
                            for t in range(TERMS):
                                sp.dma_start(parts[op, :, t, :, bass.ds(c * CH, CH)],
                                             piece[half][use[t]][:, op, :]).then_inc(stored[half], 16)
                for half in range(2):
                    sp.wait_ge(stored[half], (NCH // 2 + 1) * STORES)


def units():
    return [(qt, k0, min((qt + 1) * P - k0, CH)) for qt in range(TPB) for k0 in range(0, (qt + 1) * P, CH)]


def units_t(kt):
    return [(c, max(c * CH, kt * P), (c + 1) * CH - max(c * CH, kt * P)) for c in range(S // CH)
            if (c + 1) * CH > kt * P]


def attend(nc, g, parts, v_tok, o_tok):
    with ExitStack() as ctx:
        sb = lambda name, shape, dt=FP: ctx.enter_context(nc.sbuf_tensor("at_" + name, shape, dt))
        sem = lambda name: take_semaphore(nc, g, "at_" + name)
        ps = g["ps"]
        q_rows = [sb(f"q{i}", [64, G0, S], BF) for i in range(2)]
        k_rows = [sb(f"k{i}", [64, G0, S], BF) for i in range(2)]
        values = [sb(f"v{i}", [P, TPB, G0, 32]) for i in range(2)]
        above = sb("above", [P, P], BF)
        below = sb("below", [P, P], BF)
        mask32 = sb("mask32", [P, P])
        part_max = [sb(f"pm{i}", [P, G0, TPB, 2]) for i in range(2)]
        neg_max = [sb(f"nm{i}", [P, G0 * TPB]) for i in range(2)]
        max_part = [sb(f"mp{i}", [G0 * TPB, 3, P], BF) for i in range(2)]
        max_left = sb("ml", [G0 * TPB, P])
        probs = [sb(f"p{i}", [P, G0, S]) for i in range(2)]
        oT = sb("oT", [P, S])
        inv = sb("inv", [P, TPC, G0])
        NIT = B * NG0
        U = units()
        NU = G0 * len(U)
        rows_loaded = [sem(f"rl{i}") for i in range(2)]
        masks_set, v_set, v_ready = sem("ms"), sem("vs"), sem("vr")
        s1_ready, s1_free, nm_ready, nmT_ready, nmT_step, max_sent = (sem(n) for n in ("s1", "f1", "nm", "nt", "ns", "mx"))
        s2_ready, p_ready, pv_done, o_copied, oT_ready, o_step = (sem(n) for n in ("s2", "pr", "pv", "oc", "ot", "os"))
        nm_step = sem("nq")
        pool_past = sem("pp")
        BANK_S1, BANK_S2, BANK_PV, BANK_M, BANK_O = 0, 2, 4, 6, 7
        NPV = TPB
        with nc.Block() as block:
            @block.sync
            def _(sp):
                def load(it, half):
                    b, grp = it // NG0, it % NG0
                    for op, dst in ((0, q_rows), (1, k_rows)):
                        src = parts[op].rearrange("h t d k -> (t d) h k")
                        sp.dma_start(dst[half][0:KQK, :, :],
                                     src[:, bass.ds(grp * G0, G0), bass.ds(b * S, S)]).then_inc(rows_loaded[half], 16)

                def send_max(it, half):
                    sp.wait_ge(nmT_step, 5 * it + 5)
                    for k in range(3):
                        sp.dma_start(q_rows[half][KQK + k:KQK + k + 1, :, :].rearrange("o h (t q) -> o (h t) q", q=P),
                                     max_part[half][:, k, :]).then_inc(max_sent, 16)

                sp.wait_ge(masks_set, 6)
                load(0, 0)
                load(1, 1)
                send_max(0, 0)

                def body(it, half, more, two_more):
                    if more:
                        send_max(it + 1, 1 - half)
                    if two_more:
                        sp.wait_ge(pv_done, NPV * (it + 1))
                        load(it + 2, half)

                with sp.Fori(0, NIT // 2 - 1) as i:
                    for half in range(2):
                        body(i * 2 + half, half, True, True)
                body(NIT - 2, 0, True, False)

            @block.gpsimd
            def _(pool):
                for half in range(2):
                    nc.gpsimd.memset(k_rows[half][:, :, :], 1.0).then_inc(masks_set, 1)
                for half in range(2):
                    nc.gpsimd.memset(values[half][:, :, :, :], 0.0).then_inc(v_set, 1)
                pool.wait_ge(v_set, 2)
                for half in range(2):
                    nc.gpsimd.memset(values[half][:, :, :, HD0:HD0 + 1], 1.0).then_inc(v_set, 1)
                pool.wait_ge(v_set, 4)
                n = 2
                for dst, mult, step in ((above, 1, -1), (below, -1, 1)):
                    nc.gpsimd.memset(mask32[:, :], 0.0).then_inc(masks_set, 1)
                    pool.wait_ge(masks_set, n + 1)
                    nc.gpsimd.affine_select(out=dst[:, :], in_=mask32[:, :], compare_op=ALU.is_ge, fill=MASKED,
                                            base=0, pattern=[[step, P]], channel_multiplier=mult).then_inc(masks_set, 1)
                    n += 2
                    pool.wait_ge(masks_set, n)

                v5 = v_tok[:, :].rearrange("p (b t h d) -> p b t h d", b=B, t=TPB, h=H0)

                def fill(it, half):
                    b, grp = it // NG0, it % NG0
                    at = b * (TPB * E) + grp * (G0 * HD0)
                    for t in range(TPB):
                        last = nc.gpsimd.tensor_copy(
                            values[half][:, t, :, 0:HD0],
                            v_tok[:, bass.ds(at + t * E, G0 * HD0)].rearrange("p (h d) -> p h d", h=G0))
                    last.then_inc(v_ready, 1)

                fill(0, 0)
                fill(1, 1)
                with pool.Fori(0, NIT // 2 - 1) as i:
                    for half in range(2):
                        it = i * 2 + half
                        pool.wait_ge(pv_done, NPV * (it + 1))
                        pool.sem_inc(pool_past, 1)
                        fill(it + 2, half)

            @block.tensor
            def _(pe):
                def score(it, half, u):
                    h, (qt, k0, n) = u // len(U), U[u % len(U)]
                    pe.wait_ge(s1_free, it * NU + u + 1)
                    bank = BANK_S1 + u % 2
                    diag = k0 + n == (qt + 1) * P
                    last = nc.tensor.matmul(ps[:, bank, 0:n], q_rows[half][0:KQK, h, qt * P:(qt + 1) * P],
                                            k_rows[half][0:KQK, h, k0:k0 + n], start=True, stop=not diag)
                    if diag:
                        last = nc.tensor.matmul(ps[:, bank, n - P:n], g["ident_bf"][:, :], above[:, :],
                                                start=False, stop=True)
                    last.then_inc(s1_ready, 1)

                def maxima(it, half):
                    pe.wait_ge(nm_ready, it + 1)
                    nc.tensor.transpose(ps[0:G0 * TPB, BANK_M, 0:P], neg_max[half][:, :], g["ident"][:, :]).then_inc(nmT_ready, 1)

                def probs_of(it, half, kt, u0):
                    u = u0
                    for h in range(G0):
                        for c, q0, n in units_t(kt):
                            pe.wait_ge(p_ready, it * NU + u + 1)
                            bank = BANK_S2 + u % 2
                            diag = q0 == kt * P
                            last = nc.tensor.matmul(ps[:, bank, 0:n], k_rows[half][0:KQM, h, kt * P:(kt + 1) * P],
                                                    q_rows[half][0:KQM, h, q0:q0 + n], start=True, stop=not diag)
                            if diag:
                                last = nc.tensor.matmul(ps[:, bank, 0:P], g["ident_bf"][:, :], below[:, :],
                                                        start=False, stop=True)
                            last.then_inc(s2_ready, 1)
                            u += 1
                            yield

                def weigh(it, half, kt, done):
                    pe.wait_ge(p_ready, it * NU + done + 2)
                    if kt == 0:
                        pe.wait_ge(v_ready, it + 1)
                        pe.wait_ge(o_copied, 2 * it + 2)
                    for c, q0, n in units_t(kt):
                        for h in range(G0):
                            lo = q0 - c * CH
                            last = nc.tensor.matmul(ps[32 * h:32 * h + 32, BANK_PV + c, lo:lo + n],
                                                    values[half][:, kt, h, :],
                                                    probs[kt % 2][:, h, q0:q0 + n], start=(kt == 0),
                                                    stop=(kt == (c + 1) * TPC - 1))
                    last.then_inc(pv_done, 1)

                def turn_out(it):
                    for c in range(2):
                        pe.wait_ge(o_copied, 2 * it + 3 + c)
                        pe.wait_ge(o_step, 4 * it + 2 * c + 2)
                        for j in range(TPC):
                            t = c * TPC + j
                            last = nc.tensor.transpose(ps[:, BANK_O, j * P:(j + 1) * P], oT[:, t * P:(t + 1) * P],
                                                       g["ident"][:, :])
                        last.then_inc(oT_ready, 1)

                pe.wait_ge(masks_set, 6)
                pe.wait_ge(rows_loaded[0], 32)
                for u in range(NU):
                    score(0, 0, u)
                maxima(0, 0)

                def body(i, half, more):
                    it = i * 2 + half
                    pe.wait_ge(max_sent, 48 * (it + 1))
                    if more:
                        pe.wait_ge(rows_loaded[1 - half], 32 * (i + half + 1))
                    u1 = u2 = 0
                    for kt in range(TPB):
                        before = u2
                        for _ in probs_of(it, half, kt, u2):
                            u2 += 1
                            if more and u1 < NU:
                                score(it + 1, 1 - half, u1)
                                u1 += 1
                        if kt:
                            weigh(it, half, kt - 1, before)
                    weigh(it, half, TPB - 1, u2)
                    if more:
                        maxima(it + 1, 1 - half)
                    turn_out(it)

                with pe.Fori(0, NIT // 2 - 1) as i:
                    for half in range(2):
                        body(i, half, True)
                body(NIT // 2 - 1, 0, True)
                body(NIT // 2 - 1, 1, False)

            @block.scalar
            def _(act):
                nc.scalar.preload_act_table_set("exp_and_others")
                act.sem_inc(p_ready, 2)
                act.sem_inc(o_copied, 2)

                def body(it, half):
                    u = 0
                    for kt in range(TPB):
                        if kt >= 2:
                            act.wait_ge(pv_done, NPV * it + kt - 1)
                        for h in range(G0):
                            for c, q0, n in units_t(kt):
                                act.wait_ge(s2_ready, it * NU + u + 1)
                                nc.scalar.activation(probs[kt % 2][:, h, q0:q0 + n], ps[:, BANK_S2 + u % 2, 0:n], ACT.Exp,
                                                     scale=HD0 ** -0.5).then_inc(p_ready, 1)
                                u += 1
                    act.wait_ge(pv_done, NPV * (it + 1))
                    act.wait_ge(oT_ready, 2 * it + 2)
                    for c in range(2):
                        nc.scalar.activation(oT[:, c * CH:(c + 1) * CH], ps[:, BANK_PV + c, :],
                                             ACT.Copy).then_inc(o_copied, 1)

                act.sem_inc(oT_ready, 2)
                with act.Fori(0, NIT // 2) as i:
                    for half in range(2):
                        body(i * 2 + half, half)

            @block.vector
            def _(dve):
                dve.sem_inc(s1_free, 2)
                dve.sem_inc(o_step, 2)
                for half in range(2):
                    nc.vector.memset(part_max[half][:, :, :, :], -MASKED).then_inc(nm_step, 1)
                dve.wait_ge(nm_step, 2)

                def maxima(it, half):
                    for u in range(NU):
                        h, (qt, k0, n) = u // len(U), U[u % len(U)]
                        dve.wait_ge(s1_ready, it * NU + u + 1)
                        nc.vector.tensor_reduce(part_max[half][:, h, qt, k0 // CH:k0 // CH + 1], ps[:, BANK_S1 + u % 2, 0:n],
                                                axis=AX.X, op=ALU.max, negate=True).then_inc(s1_free, 1)
                        yield
                    dve.wait_ge(s1_free, it * NU + NU + 2)
                    nc.vector.tensor_reduce(neg_max[half][:, :], part_max[half][:, :, :, :].rearrange("p h t c -> p (h t) c"),
                                            axis=AX.X, op=ALU.min).then_inc(nm_ready, 1)

                def cut(it, half):
                    dve.wait_ge(nmT_ready, it + 1)
                    src = ps[0:G0 * TPB, BANK_M, 0:P]
                    m = max_part[half]
                    ops = (lambda: nc.vector.tensor_copy(m[:, 0, :], src),
                           lambda: nc.vector.scalar_tensor_tensor(max_left[:, :], m[:, 0, :], -1.0, src, ALU.mult, ALU.add),
                           lambda: nc.vector.tensor_copy(m[:, 1, :], max_left[:, :]),
                           lambda: nc.vector.tensor_tensor(max_left[:, :], max_left[:, :], m[:, 1, :], ALU.subtract),
                           lambda: nc.vector.tensor_copy(m[:, 2, :], max_left[:, :]))
                    for n, op in enumerate(ops):
                        op().then_inc(nmT_step, 1)
                        dve.wait_ge(nmT_step, 5 * it + 1 + n)

                def divide(it):
                    b, grp = it // NG0, it % NG0
                    for c in range(2):
                        dve.wait_ge(oT_ready, 2 * it + 3 + c)
                        o4 = ps[:, BANK_O, :].rearrange("p (t h d) -> p t h d", t=TPC, h=G0)
                        nc.vector.reciprocal(inv[:, :, :], o4[:, :, :, HD0]).then_inc(o_step, 1)
                        dve.wait_ge(o_step, 4 * it + 2 * c + 3)
                        for t in range(TPC):
                            at = b * (TPB * E) + grp * (G0 * HD0) + (c * TPC + t) * E
                            last = nc.vector.tensor_tensor(
                                o_tok[:, bass.ds(at, G0 * HD0)].rearrange("p (h d) -> p h d", h=G0),
                                o4[:, t, :, 0:HD0], inv[:, t, :].unsqueeze(2).to_broadcast([P, G0, HD0]), ALU.mult)
                        last.then_inc(o_step, 1)

                for _ in maxima(0, 0):
                    pass
                cut(0, 0)

                def body(it, half, more):
                    if more:
                        dve.wait_ge(max_sent, 48 * (it + 1))
                        for _ in maxima(it + 1, 1 - half):
                            pass
                        cut(it + 1, 1 - half)
                    divide(it)

                with dve.Fori(0, NIT // 2 - 1) as i:
                    for half in range(2):
                        body(i * 2 + half, half, True)
                body(NIT - 2, 0, True)
                body(NIT - 1, 1, False)


def attention_out(nc, g, o_tok):
    with ExitStack() as ctx:
        oT = [ctx.enter_context(nc.sbuf_tensor(f"ao_oT{i}", [P, CH], FP)) for i in range(2)]
        bias = ctx.enter_context(nc.sbuf_tensor("ao_b", [P, 1], FP))
        turned, copied, mapped = (take_semaphore(nc, g, "ao_" + n) for n in ("t", "c", "m"))
        ps, w = g["ps"], g["w_even"]
        tail = Residual(nc, g, "ao", ctx)
        with nc.Block() as block:
            @block.tensor
            def _(pe):
                for c in range(NCH + 1):
                    if c < NCH:
                        if c >= 2:
                            pe.wait_ge(copied, c - 1)
                        for j in range(TPC):
                            t = c * TPC + j
                            last = nc.tensor.transpose(ps[:, c % 2, j * P:(j + 1) * P], o_tok[:, t * P:(t + 1) * P],
                                                       g["ident"][:, :])
                        last.then_inc(turned, 1)
                        pe.wait_ge(copied, c + 1)
                        if c >= 2:
                            pe.wait_ge(tail.gated, c - 1)
                        nc.tensor.matmul(ps[:, 2 + c % 2, :], L0A(w, "wo"), oT[c % 2][:, :], start=True,
                                         stop=True).then_inc(mapped, 1)
                    if c:
                        tail.turn(pe, c - 1)

            @block.vector
            def _(dve):
                for c in range(NCH + 1):
                    if c < NCH:
                        dve.wait_ge(turned, c + 1)
                        if c >= 2:
                            dve.wait_ge(mapped, c - 1)
                        nc.vector.tensor_copy(oT[c % 2][:, :], ps[:, c % 2, :]).then_inc(copied, 1)
                    if c:
                        tail.add(dve, c - 1)

            @block.scalar
            def _(act):
                for c in range(NCH):
                    act.wait_ge(mapped, c + 1)
                    tail.gate(act, c, ps[:, 2 + c % 2, :], L0A(w, "bo")[:, 0:1], mod_col(0, GA, c // 2))


class Residual:

    def __init__(self, nc, g, tag, ctx):
        self.nc, self.g = nc, g
        self.y = [ctx.enter_context(nc.sbuf_tensor(f"{tag}_y{i}", [P, CH], FP)) for i in range(2)]
        self.z = [ctx.enter_context(nc.sbuf_tensor(f"{tag}_z{i}", [P, CH], FP)) for i in range(2)]
        self.biased, self.gated, self.back, self.added = (
            take_semaphore(nc, g, f"{tag}_{n}") for n in ("bi", "ga", "bk", "ad"))

    def gate(self, act, c, src, bias, col):
        nc, g = self.nc, self.g
        if c >= 2:
            act.wait_ge(self.back, c - 1)
        nc.scalar.activation(self.y[c % 2][:, :], src, ACT.Identity, bias=bias).then_inc(self.biased, 1)
        act.wait_ge(self.biased, c + 1)
        nc.scalar.activation(self.z[c % 2][:, :], self.y[c % 2][:, :], ACT.Copy,
                             scale=g["mod"][:, col:col + 1]).then_inc(self.gated, 1)

    def turn(self, pe, c):
        nc, g = self.nc, self.g
        pe.wait_ge(self.gated, c + 1)
        if c >= 2:
            pe.wait_ge(self.added, c - 1)
        for j in range(TPC):
            last = nc.tensor.transpose(g["ps"][:, 4 + c % 2, j * P:(j + 1) * P], self.z[c % 2][:, j * P:(j + 1) * P],
                                       g["ident"][:, :])
        last.then_inc(self.back, 1)

    def add(self, dve, c):
        nc, g = self.nc, self.g
        dve.wait_ge(self.back, c + 1)
        r = g["resid"][:, c * CH:(c + 1) * CH]
        nc.vector.tensor_tensor(r, r, g["ps"][:, 4 + c % 2, :], ALU.add).then_inc(self.added, 1)


def store(nc, g, out):
    with ExitStack() as ctx:
        stored = ctx.enter_context(nc.semaphore("stored"))
        with nc.Block() as block:
            @block.sync
            def _(sp):
                sp.wait_ge(g["x_loaded"], 16 * B)
                for b in range(B):
                    sp.dma_start(out[b].rearrange("(t p) e -> p t e", p=P),
                                 g["resid"][:, b * TPB * E:(b + 1) * TPB * E].rearrange("p (t e) -> p t e", e=E)
                                 ).then_inc(stored, 16)
                sp.wait_ge(stored, 16 * B)


def experts(nc, dram, g):
    with ExitStack() as ctx:
        weights_T = ctx.enter_context(nc.sbuf_tensor("ex_wT", [P, TOK], BF))
        exact_T = ctx.enter_context(nc.sbuf_tensor("ex_wTf", [NE, TOK], FP))
        select = ctx.enter_context(nc.sbuf_tensor("ex_sel", [3 * NE, NP_, P], BF))
        route(nc, dram, g, weights_T, exact_T, select)
        mix(nc, g, weights_T, exact_T, select)


def route(nc, dram, g, weights_T, exact_T, select):
    with ExitStack() as ctx:
        sb = lambda name, shape, dt=FP: ctx.enter_context(nc.sbuf_tensor("ro_" + name, shape, dt))
        sem = lambda name: take_semaphore(nc, g, "ro_" + name)
        hT, ps, w = g["hT"], g["ps"], g["w_odd"]
        aff = sb("aff", [P, NT, NE])
        left = sb("left", [P, NT, NE])
        top = sb("top", [P, NT, TOPK])
        total = sb("total", [P, NT])
        spread = sb("spread", [P, NT, P])
        part = sb("part", [P, NT, NE], BF)
        zero_set, sel_step, logits_ready, biased, aff_ready = sem("z"), sem("se"), sem("lg"), sem("bi"), sem("af")
        step, turned, copied = sem("st"), sem("tu"), sem("co")
        cut = [sem(f"cu{k}") for k in range(3)]
        with nc.Block() as block:
            @block.sync
            def _(sp):
                sp.wait_ge(g["l0a_loaded"], 16)
                sp.dma_start(g["w_even"][:, 0:L1A.width], dram["w_l1a"]).then_inc(g["l1a_loaded"], 16)

            @block.gpsimd
            def _(pool):
                nc.gpsimd.memset(select[:, :, :], 0.0).then_inc(zero_set, 1)
                pool.wait_ge(zero_set, 1)
                for k in range(3):
                    v = select[k * NE:(k + 1) * NE, :, :].rearrange("r p (k i) -> r p k i", k=2)
                    nc.gpsimd.affine_select(out=v, in_=v, compare_op=ALU.not_equal, fill=1.0, base=0,
                                            pattern=[[-2, NP_], [-1, 2], [0, NI]], channel_multiplier=1).then_inc(sel_step, 1)

            @block.tensor
            def _(pe):
                pe.wait_ge(g["l0f_loaded"], 16)
                for t in range(NT):
                    last = nc.tensor.matmul(ps[:, t // 16, (t % 16) * NE:(t % 16 + 1) * NE], hT[:, t * P:(t + 1) * P],
                                            L0F(w, "Wr"), start=True, stop=True)
                last.then_inc(logits_ready, 1)
                pe.wait_ge(step, 10)
                for c in range(NCH):
                    if c >= 2:
                        pe.wait_ge(copied, 2 * (c - 1))
                    for j in range(TPC):
                        last = nc.tensor.transpose(ps[:, 2 + c % 2, j * P:(j + 1) * P], spread[:, c * TPC + j, :],
                                                   g["ident"][:, :])
                    last.then_inc(turned, 1)

            @block.scalar
            def _(act):
                act.wait_ge(biased, 1)
                nc.scalar.activation(aff[:, :, :], left[:, :, :], ACT.Sigmoid).then_inc(aff_ready, 1)
                for c in range(NCH):
                    act.wait_ge(turned, c + 1)
                    nc.scalar.activation(weights_T[0:3 * NE, c * CH:(c + 1) * CH], ps[0:3 * NE, 2 + c % 2, :],
                                         ACT.Copy).then_inc(copied, 1)
                    nc.scalar.activation(exact_T[:, c * CH:(c + 1) * CH], ps[3 * NE:P, 2 + c % 2, :],
                                         ACT.Copy).then_inc(copied, 1)

            @block.vector
            def _(dve):
                dve.wait_ge(logits_ready, 1)
                nc.vector.tensor_tensor(left[:, :, :], ps[:, 0:2, :].rearrange("p c (t e) -> p (c t) e", e=NE),
                                        L0F(w, "br").unsqueeze(1).to_broadcast([P, NT, NE]), ALU.add).then_inc(biased, 1)
                dve.wait_ge(aff_ready, 1)
                for t in range(NT):
                    last = nc.vector.max(top[:, t, :], aff[:, t, :])
                last.then_inc(step, 1)
                dve.wait_ge(step, 1)
                for t in range(NT):
                    last = nc.vector.match_replace(left[:, t, :], top[:, t, :], aff[:, t, :], -1.0)
                last.then_inc(step, 1)
                dve.wait_ge(step, 2)
                full = spread[:, :, 3 * NE:P]
                nc.vector.scalar_tensor_tensor(full, left[:, :, :], 0.0, aff[:, :, :], ALU.is_lt, ALU.mult).then_inc(step, 1)
                nc.vector.tensor_reduce(total[:, :], top[:, :, :], axis=AX.X, op=ALU.add).then_inc(step, 1)
                dve.wait_ge(step, 4)
                nc.vector.tensor_scalar(total[:, :], total[:, :], 1e-9, None, ALU.add).then_inc(step, 1)
                dve.wait_ge(step, 5)
                nc.vector.reciprocal(total[:, :], total[:, :]).then_inc(step, 1)
                dve.wait_ge(step, 6)
                nc.vector.tensor_tensor(full, full, total[:, :].unsqueeze(2).to_broadcast([P, NT, NE]), ALU.mult).then_inc(step, 1)
                dve.wait_ge(step, 7)
                src = full
                for k in range(3):
                    nc.vector.tensor_copy(part[:, :, :], src).then_inc(cut[k], 1)
                    dve.wait_ge(cut[k], 1)
                    nc.vector.tensor_copy(spread[:, :, k * NE:(k + 1) * NE], part[:, :, :]).then_inc(step, 1)
                    if k < 2:
                        nc.vector.tensor_tensor(left[:, :, :], src, part[:, :, :], ALU.subtract).then_inc(cut[k], 1)
                        dve.wait_ge(cut[k], 2)
                        src = left[:, :, :]


def mix(nc, g, weights_T, exact_T, select):
    with ExitStack() as ctx:
        sb = lambda name, shape, dt=FP: ctx.enter_context(nc.sbuf_tensor("mi_" + name, shape, dt))
        sem = lambda name: take_semaphore(nc, g, "mi_" + name)
        hT, ps, w, mod, resid = g["hT"], g["ps"], g["w_odd"], g["mod"], g["resid"]
        gate = [sb(f"gate{i}", [P, CH]) for i in range(2)]
        up = [sb(f"up{i}", [P, CH]) for i in range(2)]
        prod = [sb(f"prod{i}", [P, CH]) for i in range(2)]
        y = sb("y", [P, CH])
        NU = NP_ + 1
        BG, BU, BW, BY, BT = 0, 2, 4, 6, 7
        made, gated, upped, used, downed = sem("ma"), sem("ga"), sem("up"), sem("us"), sem("do")
        y_ready, y_copied, y_turned, y_added = sem("yr"), sem("yc"), sem("yt"), sem("ya")
        early = lambda u: 1 if u == 0 else 0
        with nc.Block() as block:
            @block.tensor
            def _(pe):
                def make(c, u):
                    s = u % 2
                    rhs = hT[:, bass.ds(c * CH, CH)]
                    pe.wait_ge(used, c * NU + u + 1 + early(u))
                    if u < NP_:
                        nc.tensor.matmul(ps[:, BG + s, :], L0F(w, "Wg")[:, u * P:(u + 1) * P], rhs, start=True, stop=True)
                        nc.tensor.matmul(ps[:, BU + s, :], L0F(w, "Wu")[:, u * P:(u + 1) * P], rhs, start=True, stop=True)
                        nc.tensor.matmul(ps[:, BW + s, :], select[:, u, :], weights_T[0:3 * NE, bass.ds(c * CH, CH)],
                                         start=True, stop=True).then_inc(made, 1)
                    else:
                        nc.tensor.matmul(ps[0:NI, BG + s, :], L0F(w, "Wg_s"), rhs, start=True, stop=True)
                        nc.tensor.matmul(ps[0:NI, BU + s, :], L0F(w, "Wu_s"), rhs, start=True, stop=True).then_inc(made, 1)

                def down(c, u):
                    s = u % 2
                    pe.wait_ge(used, c * NU + u + 3)
                    if u == 0:
                        pe.wait_ge(y_copied, c + 1)
                    if u < NP_:
                        nc.tensor.matmul(ps[:, BY, :], L0F(w, "Wd")[:, u * E:(u + 1) * E], prod[s][:, :],
                                         start=(u == 0), stop=False).then_inc(downed, 1)
                    else:
                        nc.tensor.matmul(ps[:, BY, :], L0F(w, "Wd_s", NI), prod[s][0:NI, :], start=False,
                                         stop=False).then_inc(downed, 1)
                        nc.tensor.matmul(ps[:, BY, :], L0F(w, "bd", NE), exact_T[:, bass.ds(c * CH, CH)], start=False,
                                         stop=True).then_inc(y_ready, 1)

                with pe.Fori(0, NCH) as c:
                    for u in range(NU):
                        make(c, u)
                        if u:
                            down(c, u - 1)
                    down(c, NU - 1)
                    pe.wait_ge(y_copied, c + 2)
                    pe.wait_ge(y_added, c + 1)
                    for j in range(TPC):
                        last = nc.tensor.transpose(ps[:, BT, j * P:(j + 1) * P], y[:, j * P:(j + 1) * P], g["ident"][:, :])
                    last.then_inc(y_turned, 1)

            @block.scalar
            def _(act):
                nc.scalar.preload_act_table_set("silu_and_others")
                with act.Fori(0, NCH) as c:
                    for u in range(NU):
                        s, n = u % 2, (P if u < NP_ else NI)
                        bias = L0F(w, "bg")[:, u:u + 1] if u < NP_ else L0F(w, "bg_s", NI)
                        act.wait_ge(made, c * NU + u + 1)
                        act.wait_ge(used, c * NU + u + 1 + early(u))
                        nc.scalar.activation(gate[s][0:n, :], ps[0:n, BG + s, :], ACT.Silu, bias=bias).then_inc(gated, 1)

            @block.vector
            def _(dve):
                dve.sem_inc(used, 2)
                dve.sem_inc(downed, 2)
                dve.sem_inc(y_copied, 1)
                dve.sem_inc(y_added, 1)
                dve.sem_inc(y_turned, 1)
                with dve.Fori(0, B) as b:
                    for half in range(2):
                        c = b * 2 + half
                        for u in range(NU):
                            s, n = u % 2, (P if u < NP_ else NI)
                            bias = L0F(w, "bu")[:, u:u + 1] if u < NP_ else L0F(w, "bu_s", NI)
                            dve.wait_ge(gated, c * NU + u + 1)
                            if u < NP_:
                                nc.vector.scalar_tensor_tensor(up[s][:, :], ps[:, BU + s, :], bias, gate[s][:, :],
                                                               ALU.add, ALU.mult).then_inc(upped, 1)
                                dve.wait_ge(upped, c * NP_ + u + 1)
                                dve.wait_ge(downed, c * NU + u + 1 + early(u))
                                nc.vector.tensor_tensor(prod[s][:, :], up[s][:, :], ps[:, BW + s, :], ALU.mult).then_inc(used, 1)
                            else:
                                dve.wait_ge(downed, c * NU + u + 1)
                                nc.vector.scalar_tensor_tensor(prod[s][0:n, :], ps[0:n, BU + s, :], bias, gate[s][0:n, :],
                                                               ALU.add, ALU.mult).then_inc(used, 1)
                        dve.wait_ge(y_ready, c + 1)
                        dve.wait_ge(y_turned, c + 1)
                        nc.vector.tensor_scalar(y[:, :], ps[:, BY, :], L0F(w, "bd_s"), mod[:, bass.ds(mod_col(0, GB, b), 1)],
                                                ALU.add, ALU.mult).then_inc(y_copied, 1)
                        dve.wait_ge(y_turned, c + 2)
                        r = resid[:, bass.ds(c * CH, CH)]
                        nc.vector.tensor_tensor(r, r, ps[:, BT, :], ALU.add).then_inc(y_added, 1)


def state_space(nc, dram, g):
    with ExitStack() as ctx:
        sb = lambda name, shape, dt=FP: ctx.enter_context(nc.sbuf_tensor("ss_" + name, shape, dt))
        t = dict(xs=sb("xs", [P, NH, TOK]), sz=sb("sz", [P, NH, TOK]), bc=sb("bc", [3 * 32, TOK], BF),
                 select=sb("sel", [3 * 32, 32, P], BF), neg_a=sb("a", [P, NH * NS]), gain=sb("gain", [P, B]))
        scan_inputs(nc, dram, g, t)
        scan(nc, g, t)


def scan_inputs(nc, dram, g, t):
    with ExitStack() as ctx:
        sb = lambda name, shape, dt=FP: ctx.enter_context(nc.sbuf_tensor("si_" + name, shape, dt))
        sem = lambda name: take_semaphore(nc, g, "si_" + name)
        hT, ps, w, mod = g["hT"], g["ps"], g["w_even"], g["mod"]
        tmp = sb("tmp", [P, 1])
        p_all = sb("p", [96, CH], BF)
        rest = sb("rest", [96, CH])
        zero_set, sel_step, exp_done, vstep = sem("z"), sem("se"), sem("ex"), sem("vs")
        xz_ready, x_copied, z_copied, bc_ready, cut = sem("xz"), sem("xc"), sem("zc"), sem("br"), sem("cu")
        with nc.Block() as block:
            @block.gpsimd
            def _(pool):
                nc.gpsimd.memset(t["select"][:, :, :], 0.0).then_inc(zero_set, 1)
                pool.wait_ge(zero_set, 1)
                for k in range(3):
                    v = t["select"][k * 32:(k + 1) * 32, :, :]
                    nc.gpsimd.affine_select(out=v, in_=v, compare_op=ALU.not_equal, fill=1.0, base=0,
                                            pattern=[[-1, 32], [0, P]], channel_multiplier=1).then_inc(sel_step, 1)

            @block.sync
            def _(sp):
                sp.wait_ge(g["l0f_loaded"], 16)
                sp.dma_start(g["w_odd"][:, 0:L1F.width], dram["w_l1f"]).then_inc(g["l1f_loaded"], 16)

            @block.tensor
            def _(pe):
                pe.wait_ge(g["l1a_loaded"], 16)
                with pe.Fori(0, NCH) as c:
                    rhs = hT[:, bass.ds(c * CH, CH)]
                    pe.wait_ge(x_copied, c + 1)
                    pe.wait_ge(z_copied, c + 1)
                    for k in range(4):
                        last = nc.tensor.matmul(ps[:, k, :], L1A(w, "W_in")[:, k * P:(k + 1) * P], rhs, start=True, stop=True)
                    last.then_inc(xz_ready, 1)
                    pe.wait_ge(x_copied, c + 2)
                    pe.wait_ge(cut, 8 * c + 8)
                    for k in range(NH):
                        last = nc.tensor.matmul(ps[0:96, 4, :], L1A(w, "W_bc")[:, k * 96:(k + 1) * 96],
                                                t["xs"][:, k, bass.ds(c * CH, CH)], start=(k == 0), stop=(k == NH - 1))
                    last.then_inc(bc_ready, 1)

            @block.scalar
            def _(act):
                act.wait_ge(g["l1a_loaded"], 16)
                nc.scalar.activation(t["neg_a"][:, :], L1A(w, "A_log"), ACT.Exp).then_inc(exp_done, 1)
                nc.scalar.activation(tmp[:, :], L1A(w, "gate"), ACT.Exp, scale=-1.0).then_inc(exp_done, 1)
                nc.scalar.preload_act_table_set("silu_and_others")
                act.sem_inc(z_copied, 1)
                with act.Fori(0, NCH) as c:
                    act.wait_ge(xz_ready, c + 1)
                    nc.scalar.activation(t["sz"][:, :, bass.ds(c * CH, CH)], ps[:, 2:4, :], ACT.Silu).then_inc(z_copied, 1)

            @block.vector
            def _(dve):
                dve.wait_ge(exp_done, 2)
                nc.vector.tensor_scalar(t["neg_a"][:, :], t["neg_a"][:, :], -1.0, None, ALU.mult).then_inc(vstep, 1)
                nc.vector.tensor_scalar(tmp[:, :], tmp[:, :], 1.0, None, ALU.add).then_inc(vstep, 1)
                dve.wait_ge(vstep, 2)
                nc.vector.reciprocal(tmp[:, :], tmp[:, :]).then_inc(vstep, 1)
                dve.wait_ge(vstep, 3)
                at = mod_col(1, GA, 0)
                nc.vector.tensor_scalar(t["gain"][:, :], mod[:, at:at + B], tmp[:, 0:1], None, ALU.mult).then_inc(vstep, 1)
                dve.sem_inc(x_copied, 1)
                dve.sem_inc(cut, 8)
                with dve.Fori(0, NCH) as c:
                    dve.wait_ge(xz_ready, c + 1)
                    nc.vector.tensor_copy(t["xs"][:, :, bass.ds(c * CH, CH)], ps[:, 0:2, :]).then_inc(x_copied, 1)
                    dve.wait_ge(bc_ready, c + 1)
                    src, dst = ps[0:96, 4, :], t["bc"]
                    at = bass.ds(c * CH, CH)
                    n = 8 * c + 8
                    nc.vector.tensor_copy(p_all[:, :], src).then_inc(cut, 1)
                    dve.wait_ge(cut, n + 1)
                    nc.vector.tensor_copy(dst[0:32, at], p_all[0:32, :]).then_inc(cut, 1)
                    nc.vector.scalar_tensor_tensor(rest[:, :], p_all[:, :], -1.0, src, ALU.mult, ALU.add).then_inc(cut, 1)
                    dve.wait_ge(cut, n + 3)
                    nc.vector.tensor_copy(p_all[:, :], rest[:, :]).then_inc(cut, 1)
                    dve.wait_ge(cut, n + 4)
                    nc.vector.tensor_copy(dst[32:64, at], p_all[32:64, :]).then_inc(cut, 1)
                    nc.vector.tensor_tensor(rest[:, :], rest[:, :], p_all[:, :], ALU.subtract).then_inc(cut, 1)
                    dve.wait_ge(cut, n + 6)
                    nc.vector.tensor_copy(p_all[:, :], rest[:, :]).then_inc(cut, 1)
                    dve.wait_ge(cut, n + 7)
                    nc.vector.tensor_copy(dst[64:96, at], p_all[64:96, :]).then_inc(cut, 1)
                    dve.wait_ge(cut, n + 8)


def scan(nc, g, t):
    with ExitStack() as ctx:
        sb = lambda name, shape, dt=FP: ctx.enter_context(nc.sbuf_tensor("sc_" + name, shape, dt))
        sem = lambda name: take_semaphore(nc, g, "sc_" + name)
        ps, w, resid = g["ps"], g["w_even"], g["resid"]
        dt = sb("dt", [P, NH, S])
        drive = sb("drive", [P, NH, S])
        decay = [sb(f"decay{i}", [P, S]) for i in range(NH)]
        push = [sb(f"push{i}", [P, S]) for i in range(NH)]
        state = [sb(f"state{i}", [P, S]) for i in range(NH)]
        seen = [sb(f"seen{i}", [P, S]) for i in range(NH)]
        v_ready, act_step, soft_step, dt_ready = sem("vr"), sem("as"), sem("so"), sem("dr")
        b_ready, c_ready, decayed, pushed, scanned, weighed, summed = (sem(n) for n in ("b", "c", "d", "p", "s", "w", "u"))
        y_step, mapped, scaled, turned, added = (sem(n) for n in ("y", "m", "sl", "t", "a"))
        exp_done, series_step = sem("ed"), sem("sr")
        NSOFT, NY = 3, 4
        SMALL = 2.0 ** -6
        with nc.Block() as block:
            def add_up(pe, b, n):
                for half in range(NH):
                    pe.wait_ge(weighed, 2 * NS * b + 2 * n + half + 1)
                    for c in range(2):
                        last = nc.tensor.matmul(ps[:, 4 + 2 * half + c, :], g["ident"][:, :],
                                                seen[half][:, c * CH:(c + 1) * CH], start=(n == 0), stop=(n == NS - 1))
                    last.then_inc(summed, 1)

            @block.tensor
            def _(pe):
                with pe.Fori(0, B) as b:
                    pe.wait_ge(added, b + 1)
                    for half in range(NH):
                        for c in range(2):
                            for k in range(NH):
                                last = nc.tensor.matmul(
                                    ps[:, 2 * half + c, :], L1A(w, "W_dt")[:, k * DI + half * P:k * DI + (half + 1) * P],
                                    t["xs"][:, k, bass.ds(b * S + c * CH, CH)], start=(k == 0), stop=(k == NH - 1))
                    last.then_inc(v_ready, 1)
                    for n in range(NS):
                        for which, bank, ready in ((0, 0, b_ready), (1, 2, c_ready)):
                            if n == 0:
                                pe.wait_ge(soft_step, NSOFT * b + 2)
                                pe.wait_ge(act_step, 4 * b + 2)
                            elif which == 0:
                                pe.wait_ge(pushed, 2 * NS * b + 2 * n)
                            else:
                                pe.wait_ge(weighed, 2 * NS * b + 2 * n)
                            for c in range(2):
                                last = nc.tensor.matmul(ps[:, bank + c, :], t["select"][:, which * NS + n, :],
                                                        t["bc"][:, bass.ds(b * S + c * CH, CH)], start=True, stop=True)
                            last.then_inc(ready, 1)
                        if n:
                            add_up(pe, b, n - 1)
                    add_up(pe, b, NS - 1)
                    pe.wait_ge(y_step, NY * b + NY)
                    for c in range(2):
                        for k in range(NH):
                            last = nc.tensor.matmul(ps[:, c, :], L1A(w, "W_out")[:, k * E:(k + 1) * E],
                                                    seen[k][:, c * CH:(c + 1) * CH], start=(k == 0), stop=(k == NH - 1))
                    last.then_inc(mapped, 1)
                    pe.wait_ge(scaled, b + 1)
                    for j in range(TPB):
                        last = nc.tensor.transpose(ps[:, 2 + j // TPC, (j % TPC) * P:(j % TPC + 1) * P],
                                                   drive[:, 0, j * P:(j + 1) * P], g["ident"][:, :])
                    last.then_inc(turned, 1)

            @block.scalar
            def _(act):
                nc.scalar.preload_act_table_set("natural_log_exp_and_others")
                with act.Fori(0, B) as b:
                    act.wait_ge(v_ready, b + 1)
                    for half in range(NH):
                        act.wait_ge(soft_step, NSOFT * b + half + 1)
                        nc.scalar.activation(drive[:, half, :], ps[:, 2 * half:2 * half + 2, :].rearrange("p c n -> p (c n)"),
                                             ACT.Abs, bias=L1A(w, "b_dt")[:, half:half + 1]).then_inc(act_step, 1)
                    act.wait_ge(act_step, 4 * b + 2)
                    for half in range(NH):
                        nc.scalar.activation(push[half][:, :], drive[:, half, :], ACT.Exp, scale=-1.0).then_inc(exp_done, 1)
                        act.wait_ge(exp_done, 2 * b + half + 1)
                        nc.scalar.activation(state[half][:, :], push[half][:, :], ACT.Ln, bias=1.0).then_inc(act_step, 1)
                    act.wait_ge(dt_ready, b + 1)
                    for n in range(NS):
                        for half in range(NH):
                            if n:
                                act.wait_ge(scanned, 2 * NS * b + 2 * n + half - 1)
                            a = half * NS + n
                            nc.scalar.activation(decay[half][:, :], dt[:, half, :], ACT.Exp,
                                                 scale=t["neg_a"][:, a:a + 1]).then_inc(decayed, 1)

            @block.vector
            def _(dve):
                dve.sem_inc(added, 1)
                with dve.Fori(0, B) as b:
                    dve.wait_ge(v_ready, b + 1)
                    n = 0
                    for half in range(NH):
                        nc.vector.tensor_scalar(dt[:, half, :], ps[:, 2 * half:2 * half + 2, :].rearrange("p c n -> p (c n)"),
                                                L1A(w, "b_dt")[:, half:half + 1], 0.0, ALU.add, ALU.max).then_inc(soft_step, 1)
                    for half in range(NH):
                        e, ln, ser = push[half][:, :], state[half][:, :], seen[half][:, :]
                        dve.wait_ge(act_step, 4 * b + 3 + half)
                        ops = (lambda: nc.vector.tensor_scalar(ser, e, -0.25, 1.0 / 3.0, ALU.mult, ALU.add),
                               lambda: nc.vector.tensor_tensor(ser, ser, e, ALU.mult),
                               lambda: nc.vector.scalar_tensor_tensor(ser, ser, -0.5, e, ALU.add, ALU.mult),
                               lambda: nc.vector.scalar_tensor_tensor(ser, ser, 1.0, e, ALU.add, ALU.mult),
                               lambda: nc.vector.tensor_tensor(ser, ser, ln, ALU.subtract),
                               lambda: nc.vector.scalar_tensor_tensor(ser, e, SMALL, ser, ALU.is_lt, ALU.mult),
                               lambda: nc.vector.tensor_tensor(ln, ln, ser, ALU.add),
                               lambda: nc.vector.tensor_tensor(dt[:, half, :], dt[:, half, :], ln, ALU.add))
                        for op in ops:
                            op().then_inc(series_step, 1)
                            n += 1
                            dve.wait_ge(series_step, 16 * b + n)
                    dve.sem_inc(dt_ready, 1)
                    dve.wait_ge(soft_step, NSOFT * b + 2)
                    nc.vector.tensor_tensor(drive[:, :, :], dt[:, :, :], t["xs"][:, :, bass.ds(b * S, S)],
                                            ALU.mult).then_inc(soft_step, NSOFT - 2)
                    dve.wait_ge(soft_step, NSOFT * b + NSOFT)
                    for n in range(NS):
                        at = 2 * NS * b + 2 * n
                        dve.wait_ge(b_ready, NS * b + n + 1)
                        for half in range(NH):
                            nc.vector.tensor_tensor(push[half][:, :], drive[:, half, :],
                                                    ps[:, 0:2, :].rearrange("p c n -> p (c n)"), ALU.mult).then_inc(pushed, 1)
                        for half in range(NH):
                            dve.wait_ge(pushed, at + half + 1)
                            dve.wait_ge(decayed, at + half + 1)
                            nc.vector.tensor_tensor_scan(state[half][:, :], decay[half][:, :], push[half][:, :], 0.0,
                                                         ALU.mult, ALU.add).then_inc(scanned, 1)
                        dve.wait_ge(c_ready, NS * b + n + 1)
                        for half in range(NH):
                            dve.wait_ge(scanned, at + half + 1)
                            if n:
                                dve.wait_ge(summed, at + half - 1)
                            nc.vector.tensor_tensor(seen[half][:, :], state[half][:, :],
                                                    ps[:, 2:4, :].rearrange("p c n -> p (c n)"), ALU.mult).then_inc(weighed, 1)
                    dve.wait_ge(summed, 2 * NS * (b + 1))
                    for half in range(NH):
                        nc.vector.scalar_tensor_tensor(
                            push[half][:, :], t["xs"][:, half, bass.ds(b * S, S)], L1A(w, "D")[:, half:half + 1],
                            ps[:, 4 + 2 * half:6 + 2 * half, :].rearrange("p c n -> p (c n)"), ALU.mult, ALU.add).then_inc(y_step, 1)
                    dve.wait_ge(y_step, NY * b + 2)
                    for half in range(NH):
                        nc.vector.tensor_tensor(seen[half][:, :], push[half][:, :], t["sz"][:, half, bass.ds(b * S, S)],
                                                ALU.mult).then_inc(y_step, 1)
                    dve.wait_ge(mapped, b + 1)
                    nc.vector.tensor_scalar(drive[:, 0, :], ps[:, 0:2, :].rearrange("p c n -> p (c n)"),
                                            t["gain"][:, bass.ds(b, 1)], None, ALU.mult).then_inc(scaled, 1)
                    dve.wait_ge(turned, b + 1)
                    r = resid[:, bass.ds(b * S, S)]
                    nc.vector.tensor_tensor(r, r, ps[:, 2:4, :].rearrange("p c n -> p (c n)"), ALU.add).then_inc(added, 1)
                    dve.wait_ge(added, b + 2)


SP1 = S + 1


def local_transformer(nc, dram, g):
    with ExitStack() as ctx:
        other = ctx.enter_context(nc.sbuf_tensor("lt_x", [P, B * SP1], FP))
        masks = ctx.enter_context(nc.sbuf_tensor("lt_masks", [P, 2 * KW], BF))
        window_masks(nc, g, other, masks)
        for layer in range(DEPTH):
            local_attention(nc, g, layer, g["hT"], other, masks)
            feed_forward(nc, g, layer, other, g["hT"])
        add_branch(nc, g, g["hT"])


def window_masks(nc, g, other, masks):
    with ExitStack() as ctx:
        zero = ctx.enter_context(nc.sbuf_tensor("wm_z", [P, 2 * KW], FP))
        step = take_semaphore(nc, g, "wm_s")
        with nc.Block() as block:
            @block.gpsimd
            def _(pool):
                nc.gpsimd.memset(zero[:, :], 0.0).then_inc(step, 1)
                for x in (g["hT"], other):
                    pads = x[:, :].rearrange("p (b s) -> p b s", s=SP1)[:, :, 0:1]
                    nc.gpsimd.memset(pads, 0.0).then_inc(step, 1)
                pool.wait_ge(step, 3)
                z3 = zero[:, :].rearrange("p (v k) -> p v k", v=2)
                m3 = masks[:, :].rearrange("p (v k) -> p v k", v=2)
                nc.gpsimd.affine_select(out=z3, in_=z3, compare_op=ALU.is_ge, fill=MASKED, base=WIN,
                                        pattern=[[0, 2], [-1, KW]], channel_multiplier=1).then_inc(step, 1)
                pool.wait_ge(step, 4)
                nc.gpsimd.affine_select(out=m3, in_=z3, compare_op=ALU.is_ge, fill=MASKED, base=0,
                                        pattern=[[0, 2], [1, KW]], channel_multiplier=-1).then_inc(step, 1)
                pool.wait_ge(step, 5)
                nc.gpsimd.memset(masks[:, 0:WIN], MASKED).then_inc(step, 1)


def local_attention(nc, g, layer, x, out, masks):
    with ExitStack() as ctx:
        tag = f"la{layer}_"
        sb = lambda name, shape, dt=FP: ctx.enter_context(nc.sbuf_tensor(tag + name, shape, dt))
        sem = lambda name: take_semaphore(nc, g, tag + name)
        ps, w, ident = g["ps"], g["w_odd"], g["ident"]
        W = lambda n: L1F(w, f"{n}{layer}")
        QK = 2 * INNER
        cos = sb("cos", [P, TPB, 2, DL])
        sin = sb("sin", [P, TPB, 2, DL])
        shifted = [sb(f"hs{i}", [P, P]) for i in range(2)]
        square = sb("sq", [P, QK])
        straight = sb("t1", [P, QK])
        turned = sb("t2", [P, QK])
        qk = sb("qk", [P, QK])
        sumsq = sb("ss", [P, 16])
        rnorm = sb("rn", [P, 16])
        power = sb("pw", [P, 16])
        qT = [sb(f"qT{i}", [P, 4, 2, P]) for i in range(2)]
        kT = [sb(f"kT{i}", [P, 4, KW]) for i in range(2)]
        v = [sb(f"v{i}", [P, INNER]) for i in range(2)]
        probs = [sb(f"p{i}", [P, 2, 2 * P]) for i in range(2)]
        probsT = [sb(f"pT{i}", [P, 2, 2, P]) for i in range(2)]
        neg_max = [sb(f"nm{i}", [P, 2]) for i in range(2)]
        sums = [sb(f"rs{i}", [P, HL]) for i in range(2)]
        inv = sb("inv", [P, HL])
        o = sb("o", [P, INNER])
        oT = sb("oT", [P, 4, P])
        (tables, shift_ready, qk_made, v_made, squared, v_kept, roped, ss_ready, joined, rn_step, scaled, qT_turned,
         qT_kept, kT_turned, kT_kept, k_tail, scored, maxed, exped, pT_turned, pT_kept, pv_done, normed, oT_turned,
         oT_kept, y_made, y_added, preset, pool_past) = (sem(n) for n in (
             "tb", "sh", "qm", "vm", "sq", "vk", "ro", "ss", "jo", "rn", "sc", "qt", "qk", "kt", "kk", "kl", "so", "mx",
             "ex", "pt", "pk", "pv", "no", "ot", "ok", "ym", "ya", "pr", "pp"))
        NPAIR = HL // 2
        PRESET = 9
        later = lambda n: not isinstance(n, int) or n > 0

        def tiles(engine, body):
            body(0, 0, 2)
            with engine.Fori(0, NT // 2 - 2) as i:
                body(i * 2 + 1, 1, 2)
                body(i * 2 + 2, 0, 2)
            body(NT - 3, 1, 2)
            body(NT - 2, 0, 1)
            body(NT - 1, 1, 0)

        with nc.Block() as block:
            @block.gpsimd
            def _(pool):
                nc.gpsimd.memset(power[:, :], -0.5).then_inc(preset, 1)
                for i in range(2):
                    nc.gpsimd.memset(probs[i][:, :, 0:WIN], 0.0).then_inc(preset, 1)
                    nc.gpsimd.memset(v[i][:, :], 0.0).then_inc(preset, 1)
                    nc.gpsimd.memset(kT[i][:, :, :], 0.0).then_inc(preset, 1)
                    nc.gpsimd.memset(qT[i][:, :, :, :], 0.0).then_inc(preset, 1)
                pool.wait_ge(preset, PRESET)

                def past():
                    pool.sem_inc(pool_past, 1)

                def shift(n, half):
                    at = n * P + n // TPB
                    nc.gpsimd.tensor_copy(shifted[half][0:64, :], x[0:64, bass.ds(at + 1, P)]).then_inc(shift_ready, 1)
                    pool.wait_ge(shift_ready, 2 * n + 1)
                    past()
                    nc.gpsimd.tensor_copy(shifted[half][64:P, :], x[64:P, bass.ds(at, P)]).then_inc(shift_ready, 1)
                    pool.wait_ge(shift_ready, 2 * n + 2)
                    past()

                def join(n):
                    pool.wait_ge(roped, 3 * n + 3)
                    past()
                    nc.gpsimd.tensor_tensor(straight[:, :], straight[:, :], turned[:, :], ALU.add).then_inc(joined, 1)
                    pool.wait_ge(ss_ready, n + 1)
                    past()
                    nc.gpsimd.tensor_scalar(rnorm[:, :], sumsq[:, :], 1e-24, None, ALU.max).then_inc(rn_step, 1)
                    pool.wait_ge(rn_step, 3 * n + 1)
                    past()
                    nc.gpsimd.tensor_tensor(rnorm[:, :], rnorm[:, :], power[:, :], ALU.pow).then_inc(rn_step, 1)
                    pool.wait_ge(rn_step, 3 * n + 2)
                    past()
                    nc.gpsimd.tensor_scalar(rnorm[:, 0:HL], rnorm[:, 0:HL], 8.0, None, ALU.mult).then_inc(rn_step, 1)

                def tail(n, half):
                    pool.wait_ge(kT_kept, n + 1)
                    past()
                    nc.gpsimd.tensor_copy(kT[1 - half][:, :, 0:WIN], kT[half][:, :, P:KW]).then_inc(k_tail, 1)

                shift(0, 0)
                shift(1, 1)
                join(0)
                tail(0, 0)

                def body(n, half, follow):
                    if follow > 1:
                        pool.wait_ge(v_made, n + 1)
                        past()
                        shift(n + 2, half)
                    if follow:
                        join(n + 1)
                    if follow > 1:
                        pool.wait_ge(scored, NPAIR * (n + 1))
                        past()
                        tail(n + 1, 1 - half)

                tiles(pool, body)

            @block.tensor
            def _(pe):
                pe.wait_ge(g["l1f_loaded"], 16)
                pe.wait_ge(preset, PRESET)

                def project_qk(n, half):
                    pe.wait_ge(shift_ready, 2 * n + 2)
                    for k, kept in ((0, qT_kept), (1, kT_kept)):
                        if later(n):
                            pe.wait_ge(kept, n)
                        last = nc.tensor.matmul(ps[:, k, :], shifted[half][:, :], W("wqkv")[:, k * INNER:(k + 1) * INNER],
                                                start=True, stop=True)
                    last.then_inc(qk_made, 1)

                def project_v(n, half):
                    nc.tensor.matmul(ps[:, 2, :], shifted[half][:, :], W("wqkv")[:, 2 * INNER:3 * INNER],
                                     start=True, stop=True).then_inc(v_made, 1)

                def turn(n, k):
                    pe.wait_ge(scaled, n + 1)
                    for j in range(4):
                        last = nc.tensor.transpose(ps[:, k, j * P:(j + 1) * P], qk[:, (4 * k + j) * P:(4 * k + j + 1) * P],
                                                   ident[:, :])
                    last.then_inc((qT_turned, kT_turned)[k], 1)

                def score(n, half, p):
                    s = p % 2
                    if p == 0:
                        pe.wait_ge(kT_kept, n + 1)
                        if later(n):
                            pe.wait_ge(k_tail, n)
                    pe.wait_ge(exped, 2 * NPAIR * n + 2 * p + 2)
                    for r in range(2):
                        dst = ps[:, 4 + s, r * KW:(r + 1) * KW]
                        nc.tensor.matmul(dst, qT[half][:, p, r, :], kT[half][:, p, :], start=True, stop=False)
                        at = KW if half else ((n % TPB + TPB - 1) // TPB) * KW
                        last = nc.tensor.matmul(dst, g["ident_bf"][:, :], masks[:, bass.ds(at, KW)], start=False, stop=True)
                    last.then_inc(scored, 1)

                def turn_probs(n, p):
                    m = NPAIR * n + p
                    pe.wait_ge(exped, 2 * m + 6)
                    pe.wait_ge(pT_kept, m + 1)
                    for r in range(2):
                        for k in range(2):
                            last = nc.tensor.transpose(ps[:, 6, (2 * r + k) * P:(2 * r + k + 1) * P],
                                                       probs[p % 2][:, r, k * P:(k + 1) * P], ident[:, :])
                    last.then_inc(pT_turned, 1)

                def weigh(n, half, p):
                    if p == 0:
                        pe.wait_ge(normed, 2 * n + 2)
                        pe.wait_ge(v_kept, n + 1)
                    pe.wait_ge(pT_kept, NPAIR * n + p + 2)
                    for r in range(2):
                        h = 2 * p + r
                        for k in range(2):
                            last = nc.tensor.matmul(ps[:, 7, h * DL:(h + 1) * DL], probsT[p % 2][:, r, k, :],
                                                    v[half if k else 1 - half][:, h * DL:(h + 1) * DL],
                                                    start=(k == 0), stop=(k == 1))
                    last.then_inc(pv_done, 1)

                def turn_out(n):
                    pe.wait_ge(normed, 2 * n + 4)
                    for j in range(4):
                        last = nc.tensor.transpose(ps[:, 3, j * P:(j + 1) * P], o[:, j * P:(j + 1) * P], ident[:, :])
                    last.then_inc(oT_turned, 1)

                def map_out(n):
                    pe.wait_ge(oT_kept, n + 1)
                    for j in range(4):
                        last = nc.tensor.matmul(ps[:, 2, 0:P], W("wo")[:, j * E:(j + 1) * E], oT[:, j, :],
                                                start=(j == 0), stop=(j == 3))
                    last.then_inc(y_made, 1)

                def body(n, half, follow):
                    if follow:
                        project_qk(n + 1, 1 - half)
                    score(n, half, 0)
                    if later(n):
                        turn_out(n - 1)
                    score(n, half, 1)
                    turn_probs(n, 0)
                    pe.wait_ge(v_kept, n + 1)
                    if later(n):
                        map_out(n - 1)
                    score(n, half, 2)
                    turn_probs(n, 1)
                    weigh(n, half, 0)
                    if follow:
                        if later(n):
                            pe.wait_ge(y_added, n)
                        project_v(n + 1, 1 - half)
                    score(n, half, 3)
                    turn_probs(n, 2)
                    weigh(n, half, 1)
                    turn_probs(n, 3)
                    if follow:
                        turn(n + 1, 0)
                    weigh(n, half, 2)
                    if follow:
                        turn(n + 1, 1)
                    weigh(n, half, 3)

                project_qk(0, 0)
                project_v(0, 0)
                turn(0, 0)
                turn(0, 1)
                tiles(pe, body)
                turn_out(NT - 1)
                map_out(NT - 1)

            @block.scalar
            def _(act):
                nc.scalar.preload_act_table_set("exp_and_others")
                act.sem_inc(exped, 4)
                act.sem_inc(pT_kept, 1)
                act.wait_ge(preset, PRESET)

                def square_qk(n):
                    act.wait_ge(qk_made, n + 1)
                    if later(n):
                        act.wait_ge(ss_ready, n)
                    nc.scalar.activation(square[:, :], ps[:, 0:2, :].rearrange("p c n -> p (c n)"), ACT.Square).then_inc(squared, 1)

                def keep_v(n, half):
                    act.wait_ge(v_made, n + 1)
                    if later(n):
                        act.wait_ge(pv_done, NPAIR * n)
                    nc.scalar.activation(v[half][:, :], ps[:, 2, :], ACT.Copy).then_inc(v_kept, 1)

                def keep_qkT(n, half):
                    act.wait_ge(qT_turned, n + 1)
                    for r in range(2):
                        rows = slice(64 * r, 64 * r + 64)
                        last = nc.scalar.activation(qT[half][rows, :, r, :],
                                                    ps[rows, 0, :].rearrange("p (j q) -> p j q", j=4), ACT.Copy)
                    last.then_inc(qT_kept, 1)
                    act.wait_ge(kT_turned, n + 1)
                    nc.scalar.activation(kT[half][:, :, WIN:KW], ps[:, 1, :].rearrange("p (j q) -> p j q", j=4),
                                         ACT.Copy).then_inc(kT_kept, 1)

                def exps(n, half, p):
                    s = p % 2
                    m = NPAIR * n + p
                    act.wait_ge(maxed, m + 1)
                    act.wait_ge(pT_turned, m + 1)
                    for r in range(2):
                        h = 2 * p + r
                        nc.scalar.activation(probs[s][:, r, WIN:2 * P], ps[:, 4 + s, r * KW:(r + 1) * KW], ACT.Exp,
                                             bias=neg_max[s][:, r:r + 1],
                                             accum_out=sums[half][:, h:h + 1]).then_inc(exped, 1)

                def keep_pT(n, p):
                    act.wait_ge(pT_turned, NPAIR * n + p + 3)
                    nc.scalar.activation(probsT[p % 2][:, :, :, :].rearrange("p r k q -> p (r k q)"), ps[:, 6, :],
                                         ACT.Copy).then_inc(pT_kept, 1)

                def keep_oT(n):
                    act.wait_ge(oT_turned, n + 1)
                    if later(n):
                        act.wait_ge(y_made, n)
                    nc.scalar.activation(oT[:, :, :], ps[:, 3, :].rearrange("p (j q) -> p j q", j=4),
                                         ACT.Copy).then_inc(oT_kept, 1)

                def body(n, half, follow):
                    if follow:
                        square_qk(n + 1)
                    exps(n, half, 0)
                    if later(n):
                        keep_oT(n - 1)
                    exps(n, half, 1)
                    keep_pT(n, 0)
                    exps(n, half, 2)
                    exps(n, half, 3)
                    keep_pT(n, 2)
                    if follow:
                        keep_qkT(n + 1, 1 - half)
                        keep_v(n + 1, 1 - half)

                square_qk(0)
                keep_qkT(0, 0)
                keep_v(0, 0)
                tiles(act, body)
                keep_oT(NT - 1)

            @block.vector
            def _(dve):
                dve.wait_ge(g["l1f_loaded"], 16)
                dve.wait_ge(preset, PRESET)
                base = lambda n: w[:, L1F.at[n][0]:L1F.at[n][0] + TPB * DL].rearrange("p (t d) -> p t d", t=TPB)
                for k, (n, sc) in enumerate((("q", "qs"), ("k", "ks"))):
                    s3 = lambda lo, hi: W(sc)[:, lo:hi].unsqueeze(1).to_broadcast([P, TPB, hi - lo])
                    nc.vector.tensor_tensor(cos[:, :, k, :], base("cos_" + n), s3(0, DL), ALU.mult).then_inc(tables, 1)
                    nc.vector.tensor_tensor(sin[:, :, k, 0:32], base("sin_" + n)[:, :, 0:32], s3(32, 64), ALU.mult).then_inc(tables, 1)
                    nc.vector.tensor_tensor(sin[:, :, k, 32:64], base("sin_" + n)[:, :, 32:64], s3(0, 32), ALU.mult).then_inc(tables, 1)
                dve.wait_ge(tables, 6)
                dve.sem_inc(pT_turned, 2)
                dve.sem_inc(normed, 2)
                split = lambda t: t.rearrange("p (k h d) -> p k h d", k=2, h=HL)
                src = ps[:, 0:2, :].rearrange("p k (h d) -> p k h d", h=HL)

                def table(t, n, lo, hi):
                    j = n % TPB
                    flat = t[:, :, :, :].rearrange("p t k d -> p (t k d)")
                    one = flat[:, bass.ds(j * (2 * DL), 2 * DL)].rearrange("p (k d) -> p k d", k=2)[:, :, lo:hi]
                    return one.unsqueeze(2).to_broadcast([P, 2, HL, hi - lo])

                def rope_straight(n):
                    dve.wait_ge(squared, n + 1)
                    if later(n):
                        dve.wait_ge(scaled, n)
                    nc.vector.tensor_tensor(split(straight[:, :]), src, table(cos, n, 0, DL), ALU.mult).then_inc(roped, 1)

                def rope_turned(n):
                    for lo, hi in ((0, 32), (32, 64)):
                        nc.vector.tensor_tensor(split(turned[:, :])[:, :, :, lo:hi], src[:, :, :, 32 - lo:64 - lo],
                                                table(sin, n, lo, hi), ALU.mult).then_inc(roped, 1)

                def sum_squares(n):
                    if later(n):
                        dve.wait_ge(rn_step, 3 * n)
                    nc.vector.tensor_reduce(sumsq[:, :], square[:, :].rearrange("p (h d) -> p h d", d=DL), axis=AX.X,
                                            op=ALU.add).then_inc(ss_ready, 1)

                def scale(n):
                    dve.wait_ge(joined, n + 1)
                    dve.wait_ge(rn_step, 3 * n + 3)
                    if later(n):
                        dve.wait_ge(kT_turned, n)
                    nc.vector.tensor_tensor(qk[:, :].rearrange("p (h d) -> p h d", d=DL),
                                            straight[:, :].rearrange("p (h d) -> p h d", d=DL),
                                            rnorm[:, :].unsqueeze(2).to_broadcast([P, 16, DL]), ALU.mult).then_inc(scaled, 1)

                def maxima(n, p):
                    s = p % 2
                    m = NPAIR * n + p
                    dve.wait_ge(scored, m + 1)
                    dve.wait_ge(exped, 2 * m + 2)
                    nc.vector.tensor_reduce(neg_max[s][:, :], ps[:, 4 + s, 0:2 * KW].rearrange("p (r k) -> p r k", r=2),
                                            axis=AX.X, op=ALU.max, negate=True).then_inc(maxed, 1)

                def keep_pT(n, p):
                    dve.wait_ge(pT_turned, NPAIR * n + p + 3)
                    nc.vector.tensor_copy(probsT[p % 2][:, :, :, :].rearrange("p r k q -> p (r k q)"),
                                          ps[:, 6, :]).then_inc(pT_kept, 1)

                def finish(n, half):
                    dve.wait_ge(pv_done, NPAIR * (n + 1))
                    nc.vector.reciprocal(inv[:, :], sums[half][:, :]).then_inc(normed, 1)
                    dve.wait_ge(normed, 2 * n + 3)
                    if later(n):
                        dve.wait_ge(oT_turned, n)
                    nc.vector.tensor_tensor(o[:, :].rearrange("p (h d) -> p h d", d=DL),
                                            ps[:, 7, :].rearrange("p (h d) -> p h d", d=DL),
                                            inv[:, :].unsqueeze(2).to_broadcast([P, HL, DL]), ALU.mult).then_inc(normed, 1)

                def add(n):
                    dve.wait_ge(y_made, n + 1)
                    at = bass.ds(n * P + n // TPB + 1, P)
                    nc.vector.tensor_tensor(out[:, at], x[:, at], ps[:, 2, 0:P], ALU.add).then_inc(y_added, 1)

                rope_straight(0)
                rope_turned(0)
                sum_squares(0)
                scale(0)

                def body(n, half, follow):
                    if later(n):
                        finish(n - 1, 1 - half)
                    maxima(n, 0)
                    if follow:
                        rope_straight(n + 1)
                    maxima(n, 1)
                    if follow:
                        rope_turned(n + 1)
                    if later(n):
                        add(n - 1)
                    maxima(n, 2)
                    if follow:
                        sum_squares(n + 1)
                    keep_pT(n, 1)
                    maxima(n, 3)
                    if follow:
                        scale(n + 1)
                    keep_pT(n, 3)

                tiles(dve, body)
                finish(NT - 1, 1)
                add(NT - 1)


def feed_forward(nc, g, layer, x, out):
    with ExitStack() as ctx:
        tag = f"ff{layer}_"
        sb = lambda name, shape, dt=FP: ctx.enter_context(nc.sbuf_tensor(tag + name, shape, dt))
        sem = lambda name: take_semaphore(nc, g, tag + name)
        ps, w, ident = g["ps"], g["w_odd"], g["ident"]
        W = lambda n: L1F(w, f"{n}{layer}")
        mean_w = sb("mw", [P, P])
        shifted = sb("hs", [P, CH])
        centred = sb("hc", [P, CH])
        square = sb("sq", [P, CH])
        var = sb("var", [P, TPC])
        rstd = sb("rs", [P, TPC])
        power = sb("pw", [P, TPC])
        rows = sb("rw", [P, TPC, P])
        scaled = sb("sc", [P, CH])
        normed = [sb(f"hn{i}", [P, CH]) for i in range(2)]
        gelu = [sb(f"ge{i}", [P, CH]) for i in range(2)]
        prod = [sb(f"pr{i}", [P, CH]) for i in range(2)]
        (preset, shift_ready, mean_ready, centred_ready, squared, var_ready, var_kept, rstd_ready, rows_ready, spread,
         scaled_ready, normed_ready, made, gelued, used, downed, y_made, y_added, pool_past) = (sem(n) for n in (
             "ps", "sh", "me", "ce", "sq", "va", "vk", "rd", "rr", "sp", "sl", "nr", "ma", "ge", "us", "do", "ym", "ya", "pp"))
        NU = NHID
        early = lambda u: 1 if u == 0 else 0
        with nc.Block() as block:
            @block.gpsimd
            def _(pool):
                nc.gpsimd.memset(power[:, :], -0.5).then_inc(preset, 1)
                nc.gpsimd.memset(mean_w[:, :], 1.0 / P).then_inc(preset, 1)
                pool.wait_ge(preset, 2)

                def norm(c, first):
                    b, half = c // 2, c % 2
                    at = c * CH + b
                    if not first:
                        pool.wait_ge(centred_ready, c)
                        pool.sem_inc(pool_past, 1)
                    nc.gpsimd.tensor_copy(shifted[0:64, :], x[0:64, bass.ds(at + 1, CH)]).then_inc(shift_ready, 1)
                    pool.wait_ge(shift_ready, 2 * c + 1)
                    pool.sem_inc(pool_past, 1)
                    nc.gpsimd.tensor_copy(shifted[64:P, :], x[64:P, bass.ds(at, CH)]).then_inc(shift_ready, 1)
                    pool.wait_ge(shift_ready, 2 * c + 2)
                    pool.sem_inc(pool_past, 1)
                    pool.wait_ge(var_kept, c + 1)
                    pool.sem_inc(pool_past, 1)
                    nc.gpsimd.tensor_tensor(rstd[:, :], var[:, :], power[:, :], ALU.pow).then_inc(rstd_ready, 1)
                    pool.wait_ge(rstd_ready, c + 1)
                    pool.wait_ge(spread, c + 1)
                    pool.sem_inc(pool_past, 1)
                    nc.gpsimd.tensor_copy(rows[:, :, :], rstd[:, :].unsqueeze(2).to_broadcast([P, TPC, P])).then_inc(rows_ready, 1)

                norm(0, True)
                with pool.Fori(1, NCH) as c:
                    norm(c, False)

            @block.tensor
            def _(pe):
                pe.wait_ge(preset, 2)

                def norm(c, step):
                    if step == 0:
                        pe.wait_ge(shift_ready, 2 * c + 2)
                        nc.tensor.matmul(ps[:, 0, :], mean_w[:, :], shifted[:, :], start=True, stop=True).then_inc(mean_ready, 1)
                    elif step == 1:
                        pe.wait_ge(squared, c + 1)
                        for j in range(TPC):
                            last = nc.tensor.matmul(ps[:, 1, j:j + 1], square[:, j * P:(j + 1) * P], mean_w[:, 0:1],
                                                    start=True, stop=True)
                        last.then_inc(var_ready, 1)
                    else:
                        pe.wait_ge(rows_ready, c + 1)
                        pe.wait_ge(scaled_ready, c + 1)
                        for j in range(TPC):
                            last = nc.tensor.matmul(ps[:, 2, j * P:(j + 1) * P], rows[:, j, :], ident[:, :], start=True, stop=True)
                        last.then_inc(spread, 1)

                def make(c, half, u):
                    s = u % 2
                    if u == 0:
                        pe.wait_ge(normed_ready, c + 1)
                    pe.wait_ge(used, NU * c + u + 1 + early(u))
                    nc.tensor.matmul(ps[:, 3 + s, :], W("w1g")[:, u * P:(u + 1) * P], normed[half][:, :], start=True, stop=True)
                    nc.tensor.matmul(ps[:, 5 + s, :], W("w1a")[:, u * P:(u + 1) * P], normed[half][:, :], start=True,
                                     stop=True).then_inc(made, 1)

                def down(c, u):
                    pe.wait_ge(used, NU * c + u + 3)
                    if u == 0:
                        pe.wait_ge(y_added, c + 1)
                    mm = nc.tensor.matmul(ps[:, 7, :], W("w2")[:, u * E:(u + 1) * E], prod[u % 2][:, :], start=(u == 0),
                                          stop=(u == NU - 1))
                    mm.then_inc(downed, 1)
                    return mm

                for step in range(3):
                    norm(0, step)

                def body(c, half, more):
                    for u in range(NU):
                        if more:
                            norm(c + 1, u)
                        make(c, half, u)
                        if u:
                            down(c, u - 1)
                    down(c, NU - 1)

                with pe.Fori(0, NCH // 2 - 1) as i:
                    for half in range(2):
                        body(i * 2 + half, half, True)
                body(NCH - 2, 0, True)
                body(NCH - 1, 1, False)

            @block.scalar
            def _(act):
                nc.scalar.preload_act_table_set("gelu_and_others")

                def norm(c, half, step):
                    if step == 0:
                        act.wait_ge(centred_ready, c + 1)
                        nc.scalar.activation(square[:, :], centred[:, :], ACT.Square).then_inc(squared, 1)
                    else:
                        act.wait_ge(scaled_ready, c + 2)
                        nc.scalar.activation(normed[half][:, :], scaled[:, :], ACT.Identity, bias=W("ln_b"),
                                             scale=W("ln_g")).then_inc(normed_ready, 1)

                norm(0, 0, 0)
                norm(0, 0, 1)

                def body(c, half, more):
                    for u in range(NU):
                        if more and u == 0:
                            norm(c + 1, 1 - half, 0)
                        act.wait_ge(made, NU * c + u + 1)
                        act.wait_ge(used, NU * c + u + 1 + early(u))
                        nc.scalar.activation(gelu[u % 2][:, :], ps[:, 3 + u % 2, :], ACT.Gelu,
                                             bias=W("b1g")[:, u:u + 1]).then_inc(gelued, 1)
                    if more:
                        norm(c + 1, 1 - half, 1)

                with act.Fori(0, NCH // 2 - 1) as i:
                    for half in range(2):
                        body(i * 2 + half, half, True)
                body(NCH - 2, 0, True)
                body(NCH - 1, 1, False)

            @block.vector
            def _(dve):
                dve.sem_inc(used, 2)
                dve.sem_inc(downed, 2)
                dve.sem_inc(y_added, 1)
                dve.sem_inc(scaled_ready, 1)
                dve.sem_inc(spread, 1)

                def norm(c, step):
                    if step == 0:
                        dve.wait_ge(mean_ready, c + 1)
                        if not isinstance(c, int) or c:
                            dve.wait_ge(scaled_ready, c + 1)
                        nc.vector.tensor_tensor(centred[:, :], shifted[:, :], ps[:, 0, :], ALU.subtract).then_inc(centred_ready, 1)
                    elif step == 1:
                        dve.wait_ge(var_ready, c + 1)
                        nc.vector.tensor_scalar(var[:, :], ps[:, 1, 0:TPC], LN_EPS, None, ALU.add).then_inc(var_kept, 1)
                    else:
                        dve.wait_ge(spread, c + 2)
                        if not isinstance(c, int) or c:
                            dve.wait_ge(normed_ready, c)
                        nc.vector.tensor_tensor(scaled[:, :], centred[:, :], ps[:, 2, :], ALU.mult).then_inc(scaled_ready, 1)

                for step in range(3):
                    norm(0, step)

                def body(c, half, more):
                    for u in range(NU):
                        if more:
                            norm(c + 1, u)
                        dve.wait_ge(gelued, NU * c + u + 1)
                        dve.wait_ge(downed, NU * c + u + 1 + early(u))
                        nc.vector.scalar_tensor_tensor(prod[u % 2][:, :], ps[:, 5 + u % 2, :], W("b1a")[:, u:u + 1],
                                                       gelu[u % 2][:, :], ALU.add, ALU.mult).then_inc(used, 1)
                    dve.wait_ge(downed, NU * (c + 1) + 2)
                    at = bass.ds(c * CH + c // 2 + 1, CH)
                    nc.vector.scalar_tensor_tensor(out[:, at], ps[:, 7, :], W("b2"), x[:, at], ALU.add, ALU.add).then_inc(y_added, 1)

                with dve.Fori(0, NCH // 2 - 1) as i:
                    for half in range(2):
                        body(i * 2 + half, half, True)
                body(NCH - 2, 0, True)
                body(NCH - 1, 1, False)


def add_branch(nc, g, x):
    with ExitStack() as ctx:
        tail = Residual(nc, g, "ab", ctx)
        with nc.Block() as block:
            @block.scalar
            def _(act):
                for c in range(NCH):
                    if c >= 2:
                        act.wait_ge(tail.back, c - 1)
                    at, col = c * CH + c // 2 + 1, mod_col(1, GB, c // 2)
                    nc.scalar.activation(tail.z[c % 2][:, :], x[:, at:at + CH], ACT.Copy,
                                         scale=g["mod"][:, col:col + 1]).then_inc(tail.gated, 1)

            @block.tensor
            def _(pe):
                for c in range(NCH):
                    tail.turn(pe, c)

            @block.vector
            def _(dve):
                for c in range(NCH):
                    tail.add(dve, c)



def rope_tables():
    f = (1.0 / np.float32(10000.0) ** (np.arange(0, E, 2, dtype=np.float32) / np.float32(E))).astype(np.float32)
    a = np.arange(S, dtype=np.float32)[:, None] * f[None, :]
    a = np.concatenate([a, a], -1)
    sign = np.where(np.arange(E) < E // 2, -1.0, 1.0).astype(np.float32)
    return np.cos(a).T.astype(np.float32), (np.sin(a) * sign).T.astype(np.float32)


def xpos_tables():
    half = np.arange(0, DL, 2, dtype=np.float32)
    f = (1.0 / np.float32(10000.0) ** (half / np.float32(DL))).astype(np.float32)
    t = np.arange(S, dtype=np.float32)
    a = t[:, None] * f[None, :]
    a = np.concatenate([a, a], -1)
    base = ((half + np.float32(0.4 * DL)) / np.float32(1.4 * DL)).astype(np.float32)
    power = ((t - S // 2) / np.float32(WIN // 2)).astype(np.float32)
    s = (base[None, :] ** power[:, None]).astype(np.float32)
    s = np.concatenate([s, s], -1)
    sign = np.where(np.arange(DL) < DL // 2, -1.0, 1.0).astype(np.float32)
    c, n = np.cos(a).astype(np.float32), np.sin(a).astype(np.float32)
    return [x.astype(np.float32) for x in (c * s, n * s * sign, c / s, n / s * sign)]


def pack(layout, **parts):
    a = np.zeros((P, layout.width), np.float32)
    for name, x in parts.items():
        n, w = layout.at[name]
        x = np.asarray(x)
        a[:x.shape[0], n:n + w] = x.reshape(x.shape[0], w)
    return a


def kernel(**i):
    import concourse.bacc as bacc
    from concourse.bass_utils import run_bass_kernel_spmd

    arrays = lay_out(i)
    nc = bacc.Bacc("TRN2", target_bir_lowering=False, num_devices=1)
    nc.disable_value_cache = True
    dram = {n: nc.dram_tensor(f"in_{n}", a.shape, FP, kind="ExternalInput").ap() for n, a in arrays.items()}
    out = nc.dram_tensor("out_0", (B, S, E), FP, kind="ExternalOutput").ap()
    build(nc, dram, out)
    r = run_bass_kernel_spmd(nc, [{f"in_{n}": a for n, a in arrays.items()}], core_ids=[0])
    return r.results[0]["out_0"]


def lay_out(i):
    i = {k: np.asarray(v) for k, v in i.items()}
    col = lambda v: np.reshape(v, (-1, 1))
    rows = lambda v, n=P: np.broadcast_to(np.reshape(v, (1, -1)), (n, np.size(v)))
    turn = np.concatenate([np.arange(E // 2, E), np.arange(E // 2)])
    a = lambda n: i["L0_attn_" + n]
    cos, sin = rope_tables()
    out = {"x": i["L0_attn_x"]}
    out["w_mod"] = pack(MOD, cT0=i["L0_c"].T, cT1=i["L1_c"].T, wmod0=i["L0_wmod"], wmod1=i["L1_wmod"])
    out["w_l0a"] = pack(L0A, wqr=a("wqr"), wqr_rot=a("wqr")[:, turn], wkr=a("wkr"), wkr_rot=a("wkr")[:, turn],
                        wkv=a("wkv"), wv=np.concatenate([a("wv"), a("bv")[None, :]]), wo=a("wo"),
                        bqr=col(a("bqr")), bqr_rot=col(a("bqr")[turn]), bkr=col(a("bkr")), bkr_rot=col(a("bkr")[turn]),
                        bkv=col(a("bkv")), bo=np.broadcast_to(col(a("bo")), (E, E)), cos=cos, sin=sin)
    f = lambda n: i["L0_ffn_" + n]
    out["w_l0f"] = pack(
        L0F, Wr=f("Wr"), br=rows(f("br")), Wg_s=f("Wg_s"), Wu_s=f("Wu_s"), Wd_s=f("Wd_s"), bg_s=col(f("bg_s")),
        bu_s=col(f("bu_s")), bd_s=col(f("bd_s")), bg=f("bg").reshape(NP_, 2 * NI).T, bu=f("bu").reshape(NP_, 2 * NI).T,
        bd=f("bd"), Wg=f("Wg").transpose(1, 0, 2).reshape(E, -1), Wu=f("Wu").transpose(1, 0, 2).reshape(E, -1),
        Wd=f("Wd").reshape(NP_, 2 * NI, E).transpose(1, 0, 2).reshape(2 * NI, -1))
    s = lambda n: i["L1_attn_" + n]
    halves = lambda m: m.reshape(NH, P, -1).transpose(1, 0, 2).reshape(P, -1)
    bc = np.concatenate([s("W_B"), s("W_C")]).T
    out["w_l1a"] = pack(L1A, W_in=s("W_in").T, W_bc=halves(np.concatenate([bc, bc, bc], 1)), W_dt=halves(s("W_dt").T),
                        b_dt=halves(s("b_dt")), A_log=halves(s("A_log")), D=halves(s("D")),
                        gate=rows(s("output_gate")), W_out=halves(s("W_out").T))
    t = lambda n, l: i["L1_ffn_" + n][l]
    parts = {}
    for l in range(DEPTH):
        def padded(m, w):
            z = np.zeros((m.shape[0], w), np.float32)
            z[:, :m.shape[1]] = m
            return z
        w2 = np.zeros((NHID * P, E), np.float32)
        w2[:HID] = t("w2", l)
        one = dict(wqkv=t("wqkv", l), wo=t("wo", l).reshape(4, P, E).transpose(1, 0, 2).reshape(P, -1),
                   ln_g=col(t("ln_g", l)), ln_b=col(t("ln_b", l)), w1a=padded(t("w1", l)[:, :HID], NHID * P),
                   w1g=padded(t("w1", l)[:, HID:], NHID * P),
                   b1a=padded(t("b1", l)[None, :HID], NHID * P).reshape(NHID, P).T,
                   b1g=padded(t("b1", l)[None, HID:], NHID * P).reshape(NHID, P).T,
                   w2=w2.reshape(NHID, P, E).transpose(1, 0, 2).reshape(P, -1), b2=col(t("b2", l)),
                   qs=rows(t("q_scale", l)), ks=rows(t("k_scale", l)))
        parts.update({f"{n}{l}": v for n, v in one.items()})
    for n, v in zip(("cos_q", "sin_q", "cos_k", "sin_k"), xpos_tables()):
        parts[n] = v.reshape(TPB, P, DL).transpose(1, 0, 2).reshape(P, -1)
    out["w_l1f"] = pack(L1F, **parts)
    return {n: np.ascontiguousarray(v) for n, v in out.items()}
```

```python
import numpy as np
from contextlib import ExitStack

import concourse.bass as bass
from concourse import mybir

FP = mybir.dt.float32
BF = mybir.dt.bfloat16
ALU = mybir.AluOpType
ACT = mybir.ActivationFunctionType
AX = mybir.AxisListType

P = 128
B = 4
S = 1024
E = 128
TOK = B * S
NT = TOK // P
TPB = S // P
CH = 512
NCH = TOK // CH
TPC = CH // P
MASKED = -3.0e38
LN_EPS = 1e-5

H0, HD0 = 16, 8
G0 = 4
NG0 = H0 // G0
TERMS = 6
KQK = TERMS * HD0
KQM = KQK + 3
PLACES = (((0,), (1,), (2,)), ((0, 2), (1,), (3,)))
QRUNS = ((0, 3), (0, 2), (0, 1))
KRUNS = ((0, 2), (0, 4))
NE, NI, TOPK = 32, 64, 8
NP_ = NE // 2
DI, NS = 256, 16
NH = DI // P
DEPTH, HL, DL, WIN = 2, 8, 64, 64
INNER = HL * DL
HID = 341
NHID = 3
KW = P + WIN


class Layout:

    def __init__(self, parts):
        self.at, n = {}, 0
        for name, w in parts:
            self.at[name] = (n, w)
            n += w
        self.width = n

    def __call__(self, tile, name, rows=P):
        n, w = self.at[name]
        return tile[0:rows, n:n + w]


MOD = Layout([("cT0", B), ("cT1", B), ("wmod0", 6 * E), ("wmod1", 6 * E)])
L0A = Layout([("wqr", E), ("wqr_rot", E), ("wkr", E), ("wkr_rot", E), ("wkv", 32), ("wv", E), ("wo", E),
              ("bqr", 1), ("bqr_rot", 1), ("bkr", 1), ("bkr_rot", 1), ("bkv", 1), ("bo", E),
              ("cos", S), ("sin", S)])
L0F = Layout([("Wr", NE), ("br", NE), ("Wg_s", NI), ("Wu_s", NI), ("Wd_s", E), ("bg_s", 1), ("bu_s", 1),
              ("bd_s", 1), ("bg", NP_), ("bu", NP_), ("bd", E),
              ("Wg", NE * NI), ("Wu", NE * NI), ("Wd", NP_ * E)])
L1A = Layout([("W_in", 2 * DI), ("W_bc", NH * 96), ("W_dt", NH * DI), ("b_dt", NH), ("A_log", NH * NS),
              ("D", NH), ("gate", 1), ("W_out", NH * E)])
L1F_ONE = [("wqkv", 3 * INNER), ("wo", 4 * E), ("ln_g", 1), ("ln_b", 1), ("w1a", NHID * P), ("w1g", NHID * P),
           ("b1a", NHID), ("b1g", NHID), ("w2", NHID * E), ("b2", 1), ("qs", DL), ("ks", DL)]
L1F = Layout([(f"{n}{l}", w) for l in range(DEPTH) for n, w in L1F_ONE]
             + [(t, TPB * DL) for t in ("cos_q", "sin_q", "cos_k", "sin_k")])
SA, CA, GA, SB, CB, GB = range(6)


def build(nc, dram, out):
    ctx = ExitStack()
    with ctx:
        sb = lambda name, shape, dt=FP: ctx.enter_context(nc.sbuf_tensor(name, shape, dt))
        resid = sb("resid", [P, NT * E])
        hT = sb("hT", [P, TOK + B])
        mod = sb("mod", [P, 2 * 6 * B])
        ident = sb("ident", [P, P])
        ident_bf = sb("ident_bf", [P, P], BF)
        w_even = sb("w_even", [P, max(L0A.width, L1A.width)])
        w_odd = sb("w_odd", [P, max(L0F.width, L1F.width)])
        ps = ctx.enter_context(nc.psum_tensor("ps", [P, 8, CH], FP))
        g = dict(resid=resid, hT=hT, mod=mod, ident=ident, ident_bf=ident_bf, ps=ps,
                 w_even=w_even, w_odd=w_odd, taken=[])
        sems = {n: ctx.enter_context(nc.semaphore(n)) for n in
                ("x_loaded", "mod_loaded", "l0a_loaded", "l0f_loaded", "l1a_loaded", "l1f_loaded")}
        g.update(sems)
        setup(nc, dram, g)
        layer_norm(nc, g, "n0", 0, CA, SA)
        causal_attention(nc, dram, g)
        layer_norm(nc, g, "n1", 0, CB, SB)
        experts(nc, dram, g)
        layer_norm(nc, g, "n2", 1, CA, SA)
        state_space(nc, dram, g)
        layer_norm(nc, g, "n3", 1, CB, SB, pad=1,
                   load=(w_odd[:, 0:L1F.width], dram["w_l1f"], g["l1f_loaded"]))
        local_transformer(nc, dram, g)
        store(nc, g, out)


def take_semaphore(nc, g, name):
    s = nc.alloc_semaphore(name=name)
    g["taken"].append(s)
    return s


def mod_col(layer, which, b):
    return (layer * 6 + which) * B + b


def setup(nc, dram, g):
    with ExitStack() as ctx:
        sb = lambda name, shape, dt=FP: ctx.enter_context(nc.sbuf_tensor(name, shape, dt))
        sem = lambda name: take_semaphore(nc, g, name)
        w = sb("su_w", [P, MOD.width])
        c_act = sb("su_c", [P, 2 * B])
        gates = sb("su_g", [P, 4 * B])
        sign = sb("su_s", [P, 4 * B])
        zero_set, ident_set, ident_cast, silu_done = sem("su_z"), sem("su_i"), sem("su_ib"), sem("su_silu")
        mod_ready, mod_copied, step = sem("su_mm"), sem("su_mc"), sem("su_st")
        ps, mod, ident = g["ps"], g["mod"], g["ident"]
        with nc.Block() as block:
            @block.sync
            def _(sp):
                sp.dma_start(w[:, :], dram["w_mod"]).then_inc(g["mod_loaded"], 16)
                for b in range(B):
                    sp.dma_start(g["resid"][:, b * TPB * E:(b + 1) * TPB * E].rearrange("p (t e) -> p t e", e=E),
                                 dram["x"][b].rearrange("(t p) e -> p t e", p=P)).then_inc(g["x_loaded"], 16)
                sp.dma_start(g["w_even"][:, 0:L0A.width], dram["w_l0a"]).then_inc(g["l0a_loaded"], 16)
                sp.dma_start(g["w_odd"][:, 0:L0F.width], dram["w_l0f"]).then_inc(g["l0f_loaded"], 16)

            @block.gpsimd
            def _(pool):
                nc.gpsimd.memset(ident[:, :], 0.0).then_inc(zero_set, 1)
                pool.wait_ge(zero_set, 1)
                nc.gpsimd.affine_select(out=ident[:, :], in_=ident[:, :], compare_op=ALU.not_equal, fill=1.0,
                                        base=0, pattern=[[-1, P]], channel_multiplier=1).then_inc(ident_set, 1)
                pool.wait_ge(ident_set, 1)
                nc.gpsimd.tensor_copy(g["ident_bf"][:, :], ident[:, :]).then_inc(ident_cast, 1)

            @block.scalar
            def _(act):
                act.wait_ge(g["mod_loaded"], 16)
                nc.scalar.activation(c_act[:, :], w[:, 0:2 * B], ACT.Silu).then_inc(silu_done, 1)

            @block.tensor
            def _(pe):
                pe.wait_ge(silu_done, 1)
                for layer in range(2):
                    wm = MOD(w, f"wmod{layer}")
                    for k in range(6):
                        at = mod_col(layer, k, 0)
                        mm = nc.tensor.matmul(ps[:, 0, at:at + B], wm[:, k * E:(k + 1) * E],
                                              c_act[:, layer * B:(layer + 1) * B], start=True, stop=True)
                mm.then_inc(mod_ready, 1)

            @block.vector
            def _(dve):
                dve.wait_ge(mod_ready, 1)
                nc.vector.tensor_copy(mod[:, :], ps[:, 0, 0:2 * 6 * B]).then_inc(step, 1)
                dve.wait_ge(step, 1)
                n = 1
                for layer in range(2):
                    for k in (CA, CB):
                        at = mod_col(layer, k, 0)
                        nc.vector.tensor_scalar(mod[:, at:at + B], mod[:, at:at + B], 1.0, None, ALU.add).then_inc(step, 1)
                        n += 1
                    for k in (GA, GB):
                        at = mod_col(layer, k, 0)
                        s = (2 * layer + (k == GB)) * B
                        nc.vector.tensor_scalar(sign[:, s:s + B], mod[:, at:at + B], 0.0, 2.0, ALU.is_ge,
                                                ALU.mult).then_inc(step, 1)
                        nc.vector.tensor_scalar(gates[:, s:s + B], mod[:, at:at + B], -1.0, None, ALU.mult).then_inc(step, 1)
                        n += 2
                        dve.wait_ge(step, n)
                        nc.vector.scalar_tensor_tensor(gates[:, s:s + B], gates[:, s:s + B], 0.25, mod[:, at:at + B],
                                                       ALU.max, ALU.max).then_inc(step, 1)
                        n += 1
                        dve.wait_ge(step, n)
                        nc.vector.scalar_tensor_tensor(mod[:, at:at + B], sign[:, s:s + B], -1.0, gates[:, s:s + B],
                                                       ALU.add, ALU.mult).then_inc(step, 1)
                        n += 1


def layer_norm(nc, g, tag, layer, scale, shift, pad=0, load=None):
    with ExitStack() as ctx:
        spent, g["taken"] = g["taken"], []
        sb = lambda name, shape, dt=FP: ctx.enter_context(nc.sbuf_tensor(tag + name, shape, dt))
        sem = lambda name: take_semaphore(nc, g, tag + name)
        stats = sb("stats", [P, NT * 6])
        mv = sb("mv", [P, 2 * NT])
        rstd = sb("rstd", [P, NT])
        power = sb("power", [P, NT])
        xh = [sb(f"xh{i}", [P, CH]) for i in range(2)]
        stats_step, mv_ready, pow_set, rstd_ready = sem("ss"), sem("mv"), sem("pw"), sem("rs")
        xh_ready, t_ready, t_copied = sem("xh"), sem("tr"), sem("tc")
        resid, hT, mod, ps = g["resid"], g["hT"], g["mod"], g["ps"]
        mv3 = mv[:, :].rearrange("p (t two) -> p t two", two=2)
        with nc.Block() as block:
            @block.sync
            def _(sp):
                if load:
                    sp.dma_start(load[0], load[1]).then_inc(load[2], 16)

            @block.gpsimd
            def _(pool):
                nc.gpsimd.memset(power[:, :], -0.5).then_inc(pow_set, 1)
                for s in spent:
                    pool.sem_clear(s)
                pool.wait_ge(pow_set, 1)
                pool.wait_ge(mv_ready, 1)
                nc.gpsimd.tensor_scalar(rstd[:, :], mv3[:, :, 1], LN_EPS, None, ALU.add).then_inc(pow_set, 1)
                pool.wait_ge(pow_set, 2)
                nc.gpsimd.tensor_tensor(rstd[:, :], rstd[:, :], power[:, :], ALU.pow).then_inc(rstd_ready, 1)

            @block.vector
            def _(dve):
                dve.wait_ge(g["x_loaded"], 16 * B)
                for t in range(NT):
                    nc.vector.bn_stats(stats[:, 6 * t:6 * t + 6], resid[:, t * E:(t + 1) * E]).then_inc(stats_step, 1)
                dve.wait_ge(stats_step, NT)
                for t in range(NT):
                    last = nc.vector.bn_aggr(mv[:, 2 * t:2 * t + 2], stats[:, 6 * t:6 * t + 6])
                last.then_inc(mv_ready, 1)
                dve.wait_ge(rstd_ready, 1)
                for c in range(NCH):
                    if c >= 2:
                        dve.wait_ge(t_ready, c - 1)
                    for j in range(TPC):
                        t = c * TPC + j
                        last = nc.vector.tensor_scalar(xh[c % 2][:, j * P:(j + 1) * P], resid[:, t * E:(t + 1) * E],
                                                       mv[:, 2 * t:2 * t + 1], rstd[:, t:t + 1], ALU.subtract, ALU.mult)
                    last.then_inc(xh_ready, 1)

            @block.tensor
            def _(pe):
                for c in range(NCH):
                    pe.wait_ge(xh_ready, c + 1)
                    if c >= 2:
                        pe.wait_ge(t_copied, c - 1)
                    for j in range(TPC):
                        last = nc.tensor.transpose(ps[:, c % 2, j * P:(j + 1) * P], xh[c % 2][:, j * P:(j + 1) * P],
                                                   g["ident"][:, :])
                    last.then_inc(t_ready, 1)

            @block.scalar
            def _(act):
                for c in range(NCH):
                    b = c // (S // CH)
                    sc, sh = mod_col(layer, scale, b), mod_col(layer, shift, b)
                    act.wait_ge(t_ready, c + 1)
                    at = c * CH + pad * (b + 1)
                    nc.scalar.activation(hT[:, at:at + CH], ps[:, c % 2, :], ACT.Identity,
                                         bias=mod[:, sh:sh + 1], scale=mod[:, sc:sc + 1]).then_inc(t_copied, 1)
    for s in spent:
        nc.release_semaphore(s)


def causal_attention(nc, dram, g):
    parts = nc.dram_tensor("qk_parts", [2, H0, 4, HD0, TOK], BF, kind="Internal").ap()
    with ExitStack() as ctx:
        v_tok = ctx.enter_context(nc.sbuf_tensor("ca_v", [P, (NT + 1) * E], FP))
        o_tok = ctx.enter_context(nc.sbuf_tensor("ca_o", [P, (NT + 1) * E], FP))
        project(nc, g, parts, v_tok)
        attend(nc, g, parts, v_tok, o_tok)
        attention_out(nc, g, o_tok)


def project(nc, g, parts, v_tok):
    with ExitStack() as ctx:
        sb = lambda name, shape, dt=FP: ctx.enter_context(nc.sbuf_tensor("pj_" + name, shape, dt))
        sem = lambda name: take_semaphore(nc, g, "pj_" + name)
        hT, ps, w = g["hT"], g["ps"], g["w_even"]
        pair = lambda name, shape, dt=FP: [sb(f"{name}{i}", shape, dt) for i in range(2)]
        straight = pair("straight", [P, 2, CH])
        turned = sb("turned", [P, 2, CH])
        act_out = pair("act", [P, 2, CH])
        rest = pair("rest", [P, 2, CH])
        piece = [[sb(f"piece{i}{k}", [P, 2, CH], BF) for k in range(3)] for i in range(2)]
        ckv = pair("ckv", [33, CH])
        proj_ready, pair_read, rot_step, gelu_ready = sem("pr"), sem("pf"), sem("rt"), sem("gl")
        ckv_made, ckv_ready, v_ready, v_copied, ones_set = sem("cm"), sem("cr"), sem("vr"), sem("vc"), sem("on")
        cut = [sem(f"ct{k}") for k in range(3)]
        left = [sem(f"lf{k}") for k in range(2)]
        stored = [[sem(f"st{i}{k}") for k in range(3)] for i in range(2)]
        STORES = [16 * sum(len(PLACES[op][k]) for op in range(2)) for k in range(3)]
        with nc.Block() as block:
            @block.tensor
            def _(pe):
                pe.wait_ge(g["l0a_loaded"], 16)

                def values(c):
                    pe.wait_ge(ckv_ready, c + 1)
                    if c >= 2:
                        pe.wait_ge(v_copied, c - 1)
                    for j in range(TPC):
                        last = nc.tensor.matmul(ps[:, 5 + c % 2, j * P:(j + 1) * P], ckv[c % 2][:, j * P:(j + 1) * P],
                                                L0A(w, "wv", 33), start=True, stop=True)
                    last.then_inc(v_ready, 1)

                for c in range(NCH):
                    rhs = hT[:, c * CH:(c + 1) * CH]
                    for k, name in enumerate(("wqr", "wqr_rot", "wkr", "wkr_rot")):
                        if k % 2 == 0 and c:
                            pe.wait_ge(pair_read, 2 * c - 1 + k // 2)
                        mm = nc.tensor.matmul(ps[:, k, :], L0A(w, name), rhs, start=True, stop=True)
                        if k % 2:
                            mm.then_inc(proj_ready, 1)
                    if c:
                        pe.wait_ge(ckv_ready, c)
                    nc.tensor.matmul(ps[0:32, 4, :], L0A(w, "wkv"), rhs, start=True, stop=True).then_inc(ckv_made, 1)
                    if c:
                        values(c - 1)
                values(NCH - 1)

            @block.vector
            def _(dve):
                for side in range(2):
                    nc.vector.memset(ckv[side][32:33, :], 1.0).then_inc(ones_set, 1)
                dve.wait_ge(g["l0a_loaded"], 16)
                for c in range(NCH + 1):
                    if c < NCH:
                        part, out = c % (S // CH), straight[c % 2]
                        cos = w[:, L0A.at["cos"][0] + part * CH:L0A.at["cos"][0] + (part + 1) * CH]
                        sin = w[:, L0A.at["sin"][0] + part * CH:L0A.at["sin"][0] + (part + 1) * CH]
                        if c >= 2:
                            dve.wait_ge(gelu_ready, c - 1)
                        if c:
                            dve.wait_ge(rot_step, 5 * c)
                        for k, n in enumerate(("bqr", "bkr")):
                            dve.wait_ge(proj_ready, 2 * c + k + 1)
                            nc.vector.scalar_tensor_tensor(out[:, k, :], ps[:, 2 * k, :], L0A(w, n), cos,
                                                           ALU.add, ALU.mult).then_inc(rot_step, 1)
                            nc.vector.scalar_tensor_tensor(turned[:, k, :], ps[:, 2 * k + 1, :], L0A(w, n + "_rot"),
                                                           sin, ALU.add, ALU.mult).then_inc(rot_step, 1)
                            dve.wait_ge(rot_step, 5 * c + 2 * k + 2)
                            dve.sem_inc(pair_read, 1)
                        nc.vector.tensor_tensor(out[:, :, :], out[:, :, :], turned[:, :, :], ALU.add).then_inc(rot_step, 1)
                    if c:
                        side = (c - 1) % 2
                        dve.wait_ge(left[0], c)
                        if c >= 3:
                            dve.wait_ge(stored[side][1], (c - 1) // 2 * STORES[1])
                        nc.vector.tensor_copy(piece[side][1][:, :, :], rest[side][:, :, :]).then_inc(cut[1], 1)

            @block.scalar
            def _(act):
                nc.scalar.preload_act_table_set("gelu_and_others")
                act.wait_ge(ones_set, 2)
                act.wait_ge(g["l0a_loaded"], 16)

                def last_part(c):
                    side = c % 2
                    act.wait_ge(left[1], c + 1)
                    if c >= 2:
                        act.wait_ge(stored[side][2], c // 2 * STORES[2])
                    nc.scalar.activation(piece[side][2][:, :, :], rest[side][:, :, :], ACT.Copy).then_inc(cut[2], 1)

                for c in range(NCH + 2):
                    side = c % 2
                    if c < NCH:
                        act.wait_ge(ckv_made, c + 1)
                        if c >= 2:
                            act.wait_ge(v_ready, c - 1)
                        nc.scalar.activation(ckv[side][0:32, :], ps[0:32, 4, :], ACT.Gelu,
                                             bias=L0A(w, "bkv", 32)).then_inc(ckv_ready, 1)
                        act.wait_ge(rot_step, 5 * c + 5)
                        if c >= 2:
                            act.wait_ge(left[0], c - 1)
                        nc.scalar.activation(act_out[side][:, :, :], straight[side][:, :, :], ACT.Gelu).then_inc(gelu_ready, 1)
                    if c >= 2:
                        last_part(c - 2)
                    if c < NCH:
                        act.wait_ge(gelu_ready, c + 1)
                        if c >= 2:
                            act.wait_ge(stored[side][0], c // 2 * STORES[0])
                        nc.scalar.activation(piece[side][0][:, :, :], act_out[side][:, :, :], ACT.Copy).then_inc(cut[0], 1)
                    if 0 < c <= NCH:
                        act.wait_ge(v_ready, c)
                        nc.scalar.activation(v_tok[:, (c - 1) * CH:c * CH], ps[:, 5 + (c - 1) % 2, :],
                                             ACT.Copy).then_inc(v_copied, 1)

            @block.gpsimd
            def _(pool):
                for c in range(NCH + 1):
                    if c < NCH:
                        side = c % 2
                        pool.wait_ge(cut[0], c + 1)
                        nc.gpsimd.tensor_tensor(rest[side][:, :, :], act_out[side][:, :, :], piece[side][0][:, :, :],
                                                ALU.subtract).then_inc(left[0], 1)
                    if c:
                        side = (c - 1) % 2
                        pool.wait_ge(cut[1], c)
                        nc.gpsimd.tensor_tensor(rest[side][:, :, :], rest[side][:, :, :], piece[side][1][:, :, :],
                                                ALU.subtract).then_inc(left[1], 1)

            @block.sync
            def _(sp):
                for step in range(NCH + 2):
                    for k in range(3):
                        c = step - k
                        if 0 <= c < NCH:
                            sp.wait_ge(cut[k], c + 1)
                            for op in range(2):
                                for place in PLACES[op][k]:
                                    sp.dma_start(parts[op, :, place, :, c * CH:(c + 1) * CH],
                                                 piece[c % 2][k][:, op, :]).then_inc(stored[c % 2][k], 16)
                for side in range(2):
                    for k in range(3):
                        sp.wait_ge(stored[side][k], NCH // 2 * STORES[k])


def units(c):
    return [(h, qt, k0, min((qt + 1) * P - k0, CH)) for h in range(G0)
            for qt in range(c * TPC, (c + 1) * TPC) for k0 in range(0, (qt + 1) * P, CH)]


def attend(nc, g, parts, v_tok, o_tok):
    with ExitStack() as ctx:
        sb = lambda name, shape, dt=FP: ctx.enter_context(nc.sbuf_tensor("at_" + name, shape, dt))
        sem = lambda name: take_semaphore(nc, g, "at_" + name)
        ps = g["ps"]
        q_rows = [sb(f"q{i}", [64, 2, G0, CH], BF) for i in range(2)]
        k_rows = [sb(f"k{i}", [64, G0, S], BF) for i in range(2)]
        values = [sb(f"v{i}", [P, TPB, G0, 32]) for i in range(2)]
        above = sb("above", [P, P], BF)
        below = sb("below", [P, P], BF)
        mask32 = [sb(f"mask32{i}", [P, P]) for i in range(2)]
        part_max = [sb(f"pm{i}", [P, 2, G0 * TPC, 2]) for i in range(2)]
        neg_max = [sb(f"nm{i}", [P, G0 * TPC]) for i in range(2)]
        max_row = [sb(f"mr{i}", [G0 * TPC, P]) for i in range(2)]
        max_part = [sb(f"mp{i}", [G0 * TPC, 3, P], BF) for i in range(2)]
        probs = [sb(f"p{i}", [P, G0, CH]) for i in range(3)]
        oT = sb("oT", [P, S])
        inv = sb("inv", [P, TPC, G0])
        NIT = B * NG0
        U = [units(c) for c in range(2)]
        BASE = (0, len(U[0]))
        NU = len(U[0]) + len(U[1])
        KT = (TPC, TPB)
        NPV = sum(KT)
        pv_of = lambda c, kt: c * TPC + kt
        SCORES = 3
        SENT = 3 * 16
        LOADED = (len(QRUNS) + len(KRUNS)) * 16
        rows_loaded = [[sem(f"rl{i}{k}") for k in range(2)] for i in range(2)]
        ones_set, masks_set, v_set, v_ready = sem("on"), sem("ms"), sem("vs"), sem("vr")
        s1_ready, s1_free, nm_ready, nmT_ready, nmT_step, max_sent = (sem(n) for n in ("s1", "f1", "nm", "nt", "ns", "mx"))
        s2_ready, p_ready, pv_done, o_copied, oT_ready, o_step = (sem(n) for n in ("s2", "pr", "pv", "oc", "ot", "os"))
        nm_step, max_kept = sem("nq"), sem("mk")
        pool_past = sem("pp")
        BANK_S1, BANK_S2, BANK_PV, BANK_T = 0, SCORES, SCORES + 2, SCORES + 4
        later = lambda it: not isinstance(it, int) or it > 0

        def iterations(engine, body):
            body(0, 0, 2)
            with engine.Fori(0, NIT // 2 - 2) as i:
                body(i * 2 + 1, 1, 2)
                body(i * 2 + 2, 0, 2)
            body(NIT - 3, 1, 2)
            body(NIT - 2, 0, 1)
            body(NIT - 1, 1, 0)

        with nc.Block() as block:
            @block.sync
            def _(sp):
                def load(it, side, part):
                    b, grp = it // NG0, it % NG0
                    for op, runs in enumerate((QRUNS, KRUNS)):
                        src = parts[op].rearrange("h t d k -> (t d) h k")
                        row = 0
                        for first, n in runs:
                            rows = slice(row, row + n * HD0)
                            dst = k_rows[side][rows, :, part * CH:(part + 1) * CH] if op else q_rows[side][rows, part, :, :]
                            sp.dma_start(dst, src[first * HD0:(first + n) * HD0, bass.ds(grp * G0, G0),
                                                  bass.ds(b * S + part * CH, CH)]).then_inc(rows_loaded[side][part], 16)
                            row += n * HD0

                def send_max(it, side, c):
                    sp.wait_ge(nmT_step, 10 * it + 5 * c + 5)
                    for k in range(3):
                        row = q_rows[side][KQK + k:KQK + k + 1, c, :, :]
                        sp.dma_start(row.rearrange("o h (t q) -> o (h t) q", q=P), max_part[c][:, k, :]).then_inc(max_sent, 16)

                sp.wait_ge(ones_set, 2)
                for it in range(2):
                    for part in range(2):
                        load(it, it, part)
                send_max(0, 0, 0)

                def body(it, side, follow):
                    send_max(it, side, 1)
                    if follow:
                        send_max(it + 1, 1 - side, 0)
                    if follow > 1:
                        sp.wait_ge(pv_done, NPV * it + pv_of(1, TPC))
                        load(it + 2, side, 0)
                        sp.wait_ge(pv_done, NPV * (it + 1))
                        load(it + 2, side, 1)

                iterations(sp, body)

            @block.gpsimd
            def _(pool):
                for k, (dst, mult, step) in enumerate(((above, 1, -1), (below, -1, 1))):
                    nc.gpsimd.memset(mask32[k][:, :], 0.0).then_inc(masks_set, 1)
                pool.wait_ge(masks_set, 2)
                for k, (dst, mult, step) in enumerate(((above, 1, -1), (below, -1, 1))):
                    nc.gpsimd.affine_select(out=dst[:, :], in_=mask32[k][:, :], compare_op=ALU.is_ge, fill=MASKED,
                                            base=0, pattern=[[step, P]], channel_multiplier=mult).then_inc(masks_set, 1)
                for side in range(2):
                    nc.gpsimd.memset(values[side][:, :, :, :], 0.0).then_inc(v_set, 1)
                pool.wait_ge(v_set, 2)
                for side in range(2):
                    nc.gpsimd.memset(values[side][:, :, :, HD0:HD0 + 1], 1.0).then_inc(v_set, 1)
                pool.wait_ge(v_set, 4)

                def fill(it, side):
                    b, grp = it // NG0, it % NG0
                    at = b * (TPB * E) + grp * (G0 * HD0)
                    src = v_tok[:, bass.ds(at, TPB * E)].rearrange("p (t e) -> p t e", e=E)[:, :, 0:G0 * HD0]
                    nc.gpsimd.tensor_copy(values[side][:, :, :, 0:HD0],
                                          src.rearrange("p t (h d) -> p t h d", h=G0)).then_inc(v_ready, 1)

                def cut(it, c):
                    left, m = max_row[c][:, :], max_part[c]
                    pool.wait_ge(max_kept, 2 * it + c + 1)
                    pool.sem_inc(pool_past, 1)
                    ops = (lambda: nc.gpsimd.tensor_copy(m[:, 0, :], left),
                           lambda: nc.gpsimd.tensor_tensor(left, left, m[:, 0, :], ALU.subtract),
                           lambda: nc.gpsimd.tensor_copy(m[:, 1, :], left),
                           lambda: nc.gpsimd.tensor_tensor(left, left, m[:, 1, :], ALU.subtract),
                           lambda: nc.gpsimd.tensor_copy(m[:, 2, :], left))
                    for n, op in enumerate(ops):
                        op().then_inc(nmT_step, 1)
                        pool.wait_ge(nmT_step, 10 * it + 5 * c + 1 + n)
                        pool.sem_inc(pool_past, 1)

                fill(0, 0)
                fill(1, 1)
                cut(0, 0)

                def body(it, side, follow):
                    cut(it, 1)
                    if follow and later(it):
                        pool.wait_ge(pv_done, NPV * it)
                        pool.sem_inc(pool_past, 1)
                        fill(it + 1, 1 - side)
                    if follow:
                        cut(it + 1, 0)

                iterations(pool, body)

            @block.tensor
            def _(pe):
                def score(it, side, c, n_):
                    h, qt, k0, n = U[c][n_]
                    u = BASE[c] + n_
                    pe.wait_ge(s1_free, it * NU + u + 1)
                    bank = BANK_S1 + u % SCORES
                    diag = k0 + n == (qt + 1) * P
                    last = nc.tensor.matmul(ps[:, bank, 0:n], q_rows[side][0:KQK, c, h, (qt % TPC) * P:(qt % TPC + 1) * P],
                                            k_rows[side][0:KQK, h, k0:k0 + n], start=True, stop=not diag)
                    if diag:
                        last = nc.tensor.matmul(ps[:, bank, n - P:n], g["ident_bf"][:, :], above[:, :],
                                                start=False, stop=True)
                    last.then_inc(s1_ready, 1)

                def maxima(it, c):
                    pe.wait_ge(nm_ready, 2 * it + c + 1)
                    nc.tensor.transpose(ps[0:G0 * TPC, BANK_T, 0:P], neg_max[c][:, :], g["ident"][:, :]).then_inc(nmT_ready, 1)

                def shifted_score(it, side, c, kt, h, u):
                    pe.wait_ge(p_ready, it * NU + u + 1)
                    bank = BANK_S2 + u % 2
                    q0 = max(c * CH, kt * P)
                    n = (c + 1) * CH - q0
                    diag = q0 == kt * P
                    last = nc.tensor.matmul(ps[:, bank, 0:n], k_rows[side][0:KQM, h, kt * P:(kt + 1) * P],
                                            q_rows[side][0:KQM, c, h, q0 - c * CH:CH], start=True, stop=not diag)
                    if diag:
                        last = nc.tensor.matmul(ps[:, bank, 0:P], g["ident_bf"][:, :], below[:, :],
                                                start=False, stop=True)
                    last.then_inc(s2_ready, 1)

                def weigh(it, side, c, kt):
                    pe.wait_ge(p_ready, it * NU + BASE[c] + (kt + 1) * G0 + 2)
                    if kt == 0:
                        if c == 0:
                            pe.wait_ge(v_ready, it + 1)
                        pe.wait_ge(o_copied, 2 * it + c + 1)
                    lo = max(0, kt * P - c * CH)
                    for h in range(G0):
                        last = nc.tensor.matmul(ps[32 * h:32 * h + 32, BANK_PV + c, lo:CH], values[side][:, kt, h, :],
                                                probs[pv_of(c, kt) % 3][:, h, lo:CH], start=(kt == 0),
                                                stop=(kt == KT[c] - 1))
                    last.then_inc(pv_done, 1)

                def turn_out(it, c):
                    pe.wait_ge(o_copied, 2 * it + 3 + c)
                    for j in range(TPC):
                        t = c * TPC + j
                        last = nc.tensor.transpose(ps[:, BANK_T, j * P:(j + 1) * P], oT[:, t * P:(t + 1) * P],
                                                   g["ident"][:, :])
                    last.then_inc(oT_ready, 1)

                pe.wait_ge(masks_set, 4)
                for c in range(2):
                    pe.wait_ge(rows_loaded[0][c], LOADED)
                    for n_ in range(len(U[c])):
                        score(0, 0, c, n_)
                        if c and n_ == 2:
                            maxima(0, 0)

                def body(it, side, follow):
                    for c in range(2):
                        pe.wait_ge(max_sent, SENT * (2 * it + c + 1))
                        u = 0
                        for kt in range(KT[c]):
                            for h in range(G0):
                                shifted_score(it, side, c, kt, h, BASE[c] + u)
                                if follow:
                                    if u == 0:
                                        pe.wait_ge(rows_loaded[1 - side][c], ((it + 1) // 2 + 1) * LOADED)
                                    score(it + 1, 1 - side, c, u)
                                u += 1
                            if kt:
                                weigh(it, side, c, kt - 1)
                            elif c:
                                weigh(it, side, 0, KT[0] - 1)
                            elif later(it):
                                weigh(it - 1, 1 - side, 1, KT[1] - 1)
                            if kt == 0 and c == 0:
                                if later(it):
                                    pe.wait_ge(o_step, 4 * it)
                                else:
                                    pe.wait_ge(max_kept, 1)
                                maxima(it, 1)
                            elif kt == 0 and follow:
                                if later(it):
                                    pe.wait_ge(o_step, 4 * it + 2)
                                else:
                                    pe.wait_ge(max_kept, 2)
                                maxima(it + 1, 0)
                            elif kt == 2 and c == 0 and later(it):
                                pe.wait_ge(max_kept, 2 * it + 2)
                                turn_out(it - 1, 1)
                            elif kt == 2 and c == 1:
                                if follow:
                                    pe.wait_ge(max_kept, 2 * it + 3)
                                else:
                                    pe.wait_ge(o_step, 4 * it + 2)
                                turn_out(it, 0)

                iterations(pe, body)
                weigh(NIT - 1, 1, 1, KT[1] - 1)
                pe.wait_ge(o_step, 4 * NIT)
                turn_out(NIT - 1, 1)

            @block.scalar
            def _(act):
                nc.scalar.preload_act_table_set("exp_and_others")
                act.sem_inc(p_ready, 2)
                act.sem_inc(o_copied, 2)
                act.sem_inc(oT_ready, 2)

                def keep_out(it, c):
                    act.wait_ge(pv_done, NPV * it + pv_of(c, KT[c]))
                    act.wait_ge(oT_ready, 2 * it + c + 1)
                    nc.scalar.activation(oT[:, c * CH:(c + 1) * CH], ps[:, BANK_PV + c, :],
                                         ACT.Copy).then_inc(o_copied, 1)

                def keep_max(it, c):
                    act.wait_ge(nmT_ready, 2 * it + c + 1)
                    if later(it):
                        act.wait_ge(nmT_step, 10 * it + 5 * c - 5)
                    nc.scalar.activation(max_row[c][:, :], ps[0:G0 * TPC, BANK_T, 0:P], ACT.Copy).then_inc(max_kept, 1)

                keep_max(0, 0)

                def body(it, side, follow):
                    for c in range(2):
                        u = BASE[c]
                        for kt in range(KT[c]):
                            back = pv_of(c, kt) - 2
                            if later(it) or back > 0:
                                act.wait_ge(pv_done, NPV * it + back)
                            lo = max(0, kt * P - c * CH)
                            for h in range(G0):
                                act.wait_ge(s2_ready, it * NU + u + 1)
                                nc.scalar.activation(probs[pv_of(c, kt) % 3][:, h, lo:CH], ps[:, BANK_S2 + u % 2, 0:CH - lo],
                                                     ACT.Exp, scale=HD0 ** -0.5).then_inc(p_ready, 1)
                                u += 1
                                if kt == 1 and h == 0:
                                    if c == 0:
                                        keep_max(it, 1)
                                    elif follow:
                                        keep_max(it + 1, 0)
                            if kt == 1 and c:
                                keep_out(it, 0)
                            elif kt == 1 and later(it):
                                keep_out(it - 1, 1)

                iterations(act, body)
                keep_out(NIT - 1, 1)

            @block.vector
            def _(dve):
                for side in range(2):
                    nc.vector.memset(k_rows[side][:, :, :], 1.0).then_inc(ones_set, 1)
                dve.sem_inc(s1_free, SCORES)
                dve.sem_inc(o_step, 2)
                for side in range(2):
                    nc.vector.memset(part_max[side][:, :, :, :], -MASKED).then_inc(nm_step, 1)
                dve.wait_ge(nm_step, 2)

                def maximum(it, side, c, n_):
                    h, qt, k0, n = U[c][n_]
                    u = BASE[c] + n_
                    dve.wait_ge(s1_ready, it * NU + u + 1)
                    nc.vector.tensor_reduce(part_max[side][:, c, h * TPC + qt % TPC, k0 // CH:k0 // CH + 1],
                                            ps[:, BANK_S1 + u % SCORES, 0:n],
                                            axis=AX.X, op=ALU.max, negate=True).then_inc(s1_free, 1)

                def join(it, side, c):
                    dve.wait_ge(s1_free, it * NU + BASE[c] + len(U[c]) + SCORES)
                    nc.vector.tensor_reduce(neg_max[c][:, :], part_max[side][:, c, :, :], axis=AX.X,
                                            op=ALU.min).then_inc(nm_ready, 1)

                def divide(it, c):
                    b, grp = it // NG0, it % NG0
                    dve.wait_ge(oT_ready, 2 * it + 3 + c)
                    o4 = ps[:, BANK_T, :].rearrange("p (t h d) -> p t h d", t=TPC, h=G0)
                    nc.vector.reciprocal(inv[:, :, :], o4[:, :, :, HD0]).then_inc(o_step, 1)
                    dve.wait_ge(o_step, 4 * it + 2 * c + 3)
                    at = b * (TPB * E) + grp * (G0 * HD0) + c * TPC * E
                    dst = o_tok[:, bass.ds(at, TPC * E)].rearrange("p (t e) -> p t e", e=E)[:, :, 0:G0 * HD0]
                    nc.vector.tensor_tensor(dst.rearrange("p t (h d) -> p t h d", h=G0), o4[:, :, :, 0:HD0],
                                            inv[:, :, :].unsqueeze(3).to_broadcast([P, TPC, G0, HD0]),
                                            ALU.mult).then_inc(o_step, 1)

                for c in range(2):
                    for n_ in range(len(U[c])):
                        maximum(0, 0, c, n_)
                    if c == 0:
                        join(0, 0, 0)

                def body(it, side, follow):
                    for c in range(2):
                        if c == 0:
                            join(it, side, 1)
                        elif follow:
                            join(it + 1, 1 - side, 0)
                        for n_ in range(len(U[c])):
                            if follow:
                                maximum(it + 1, 1 - side, c, n_)
                            if n_ == 3 * G0:
                                if c:
                                    divide(it, 0)
                                elif later(it):
                                    divide(it - 1, 1)

                iterations(dve, body)
                divide(NIT - 1, 1)


def attention_out(nc, g, o_tok):
    with ExitStack() as ctx:
        oT = [ctx.enter_context(nc.sbuf_tensor(f"ao_oT{i}", [P, CH], FP)) for i in range(2)]
        turned, copied, mapped = (take_semaphore(nc, g, "ao_" + n) for n in ("t", "c", "m"))
        ps, w = g["ps"], g["w_even"]
        tail = Residual(nc, g, "ao", ctx)
        with nc.Block() as block:
            @block.tensor
            def _(pe):
                for c in range(NCH + 1):
                    if c < NCH:
                        if c >= 2:
                            pe.wait_ge(copied, c - 1)
                        for j in range(TPC):
                            t = c * TPC + j
                            last = nc.tensor.transpose(ps[:, c % 2, j * P:(j + 1) * P], o_tok[:, t * P:(t + 1) * P],
                                                       g["ident"][:, :])
                        last.then_inc(turned, 1)
                        pe.wait_ge(copied, c + 1)
                        if c >= 2:
                            pe.wait_ge(tail.gated, c - 1)
                        nc.tensor.matmul(ps[:, 2 + c % 2, :], L0A(w, "wo"), oT[c % 2][:, :], start=True,
                                         stop=True).then_inc(mapped, 1)
                    if c:
                        tail.turn(pe, c - 1)

            @block.vector
            def _(dve):
                for c in range(NCH + 1):
                    if c < NCH:
                        dve.wait_ge(turned, c + 1)
                        if c >= 2:
                            dve.wait_ge(mapped, c - 1)
                        nc.vector.tensor_copy(oT[c % 2][:, :], ps[:, c % 2, :]).then_inc(copied, 1)
                    if c:
                        tail.add(dve, c - 1)

            @block.scalar
            def _(act):
                for c in range(NCH):
                    act.wait_ge(mapped, c + 1)
                    tail.gate(act, c, ps[:, 2 + c % 2, :], L0A(w, "bo")[:, 0:1], mod_col(0, GA, c // 2))


class Residual:

    def __init__(self, nc, g, tag, ctx):
        self.nc, self.g = nc, g
        self.y = [ctx.enter_context(nc.sbuf_tensor(f"{tag}_y{i}", [P, CH], FP)) for i in range(2)]
        self.z = [ctx.enter_context(nc.sbuf_tensor(f"{tag}_z{i}", [P, CH], FP)) for i in range(2)]
        self.biased, self.gated, self.back, self.added = (
            take_semaphore(nc, g, f"{tag}_{n}") for n in ("bi", "ga", "bk", "ad"))

    def gate(self, act, c, src, bias, col):
        nc, g = self.nc, self.g
        if c >= 2:
            act.wait_ge(self.back, c - 1)
        nc.scalar.activation(self.y[c % 2][:, :], src, ACT.Identity, bias=bias).then_inc(self.biased, 1)
        act.wait_ge(self.biased, c + 1)
        nc.scalar.activation(self.z[c % 2][:, :], self.y[c % 2][:, :], ACT.Copy,
                             scale=g["mod"][:, col:col + 1]).then_inc(self.gated, 1)

    def turn(self, pe, c):
        nc, g = self.nc, self.g
        pe.wait_ge(self.gated, c + 1)
        if c >= 2:
            pe.wait_ge(self.added, c - 1)
        for j in range(TPC):
            last = nc.tensor.transpose(g["ps"][:, 4 + c % 2, j * P:(j + 1) * P], self.z[c % 2][:, j * P:(j + 1) * P],
                                       g["ident"][:, :])
        last.then_inc(self.back, 1)

    def add(self, dve, c):
        nc, g = self.nc, self.g
        dve.wait_ge(self.back, c + 1)
        r = g["resid"][:, c * CH:(c + 1) * CH]
        nc.vector.tensor_tensor(r, r, g["ps"][:, 4 + c % 2, :], ALU.add).then_inc(self.added, 1)


def store(nc, g, out):
    with ExitStack() as ctx:
        stored = ctx.enter_context(nc.semaphore("stored"))
        with nc.Block() as block:
            @block.sync
            def _(sp):
                sp.wait_ge(g["x_loaded"], 16 * B)
                for b in range(B):
                    sp.dma_start(out[b].rearrange("(t p) e -> p t e", p=P),
                                 g["resid"][:, b * TPB * E:(b + 1) * TPB * E].rearrange("p (t e) -> p t e", e=E)
                                 ).then_inc(stored, 16)
                sp.wait_ge(stored, 16 * B)


def experts(nc, dram, g):
    with ExitStack() as ctx:
        weights_T = ctx.enter_context(nc.sbuf_tensor("ex_wT", [P, TOK], BF))
        exact_T = ctx.enter_context(nc.sbuf_tensor("ex_wTf", [NE, TOK], FP))
        select = ctx.enter_context(nc.sbuf_tensor("ex_sel", [3 * NE, NP_, P], BF))
        route(nc, dram, g, weights_T, exact_T, select)
        mix(nc, g, weights_T, exact_T, select)


def route(nc, dram, g, weights_T, exact_T, select):
    with ExitStack() as ctx:
        sb = lambda name, shape, dt=FP: ctx.enter_context(nc.sbuf_tensor("ro_" + name, shape, dt))
        sem = lambda name: take_semaphore(nc, g, "ro_" + name)
        hT, ps, w = g["hT"], g["ps"], g["w_odd"]
        aff = sb("aff", [P, NT, NE])
        left = sb("left", [P, NT, NE])
        top = sb("top", [P, NT, TOPK])
        total = sb("total", [P, NT])
        spread = sb("spread", [P, NT, P])
        part = sb("part", [P, NT, NE], BF)
        zero_set, sel_step, logits_ready, biased, aff_ready = sem("z"), sem("se"), sem("lg"), sem("bi"), sem("af")
        step, turned, copied = sem("st"), sem("tu"), sem("co")
        cut = [sem(f"cu{k}") for k in range(3)]
        with nc.Block() as block:
            @block.sync
            def _(sp):
                sp.wait_ge(g["l0a_loaded"], 16)
                sp.dma_start(g["w_even"][:, 0:L1A.width], dram["w_l1a"]).then_inc(g["l1a_loaded"], 16)

            @block.gpsimd
            def _(pool):
                nc.gpsimd.memset(select[:, :, :], 0.0).then_inc(zero_set, 1)
                pool.wait_ge(zero_set, 1)
                for k in range(3):
                    v = select[k * NE:(k + 1) * NE, :, :].rearrange("r p (k i) -> r p k i", k=2)
                    nc.gpsimd.affine_select(out=v, in_=v, compare_op=ALU.not_equal, fill=1.0, base=0,
                                            pattern=[[-2, NP_], [-1, 2], [0, NI]], channel_multiplier=1).then_inc(sel_step, 1)

            @block.tensor
            def _(pe):
                pe.wait_ge(g["l0f_loaded"], 16)
                for t in range(NT):
                    last = nc.tensor.matmul(ps[:, t // 16, (t % 16) * NE:(t % 16 + 1) * NE], hT[:, t * P:(t + 1) * P],
                                            L0F(w, "Wr"), start=True, stop=True)
                last.then_inc(logits_ready, 1)
                pe.wait_ge(step, 10)
                for c in range(NCH):
                    if c >= 2:
                        pe.wait_ge(copied, 2 * (c - 1))
                    for j in range(TPC):
                        last = nc.tensor.transpose(ps[:, 2 + c % 2, j * P:(j + 1) * P], spread[:, c * TPC + j, :],
                                                   g["ident"][:, :])
                    last.then_inc(turned, 1)

            @block.scalar
            def _(act):
                act.wait_ge(biased, 1)
                nc.scalar.activation(aff[:, :, :], left[:, :, :], ACT.Sigmoid).then_inc(aff_ready, 1)
                for c in range(NCH):
                    act.wait_ge(turned, c + 1)
                    nc.scalar.activation(weights_T[0:3 * NE, c * CH:(c + 1) * CH], ps[0:3 * NE, 2 + c % 2, :],
                                         ACT.Copy).then_inc(copied, 1)
                    nc.scalar.activation(exact_T[:, c * CH:(c + 1) * CH], ps[3 * NE:P, 2 + c % 2, :],
                                         ACT.Copy).then_inc(copied, 1)

            @block.vector
            def _(dve):
                dve.wait_ge(logits_ready, 1)
                nc.vector.tensor_tensor(left[:, :, :], ps[:, 0:2, :].rearrange("p c (t e) -> p (c t) e", e=NE),
                                        L0F(w, "br").unsqueeze(1).to_broadcast([P, NT, NE]), ALU.add).then_inc(biased, 1)
                dve.wait_ge(aff_ready, 1)
                for t in range(NT):
                    last = nc.vector.max(top[:, t, :], aff[:, t, :])
                last.then_inc(step, 1)
                dve.wait_ge(step, 1)
                for t in range(NT):
                    last = nc.vector.match_replace(left[:, t, :], top[:, t, :], aff[:, t, :], -1.0)
                last.then_inc(step, 1)
                dve.wait_ge(step, 2)
                full = spread[:, :, 3 * NE:P]
                nc.vector.scalar_tensor_tensor(full, left[:, :, :], 0.0, aff[:, :, :], ALU.is_lt, ALU.mult).then_inc(step, 1)
                nc.vector.tensor_reduce(total[:, :], top[:, :, :], axis=AX.X, op=ALU.add).then_inc(step, 1)
                dve.wait_ge(step, 4)
                nc.vector.tensor_scalar(total[:, :], total[:, :], 1e-9, None, ALU.add).then_inc(step, 1)
                dve.wait_ge(step, 5)
                nc.vector.reciprocal(total[:, :], total[:, :]).then_inc(step, 1)
                dve.wait_ge(step, 6)
                nc.vector.tensor_tensor(full, full, total[:, :].unsqueeze(2).to_broadcast([P, NT, NE]), ALU.mult).then_inc(step, 1)
                dve.wait_ge(step, 7)
                src = full
                for k in range(3):
                    nc.vector.tensor_copy(part[:, :, :], src).then_inc(cut[k], 1)
                    dve.wait_ge(cut[k], 1)
                    nc.vector.tensor_copy(spread[:, :, k * NE:(k + 1) * NE], part[:, :, :]).then_inc(step, 1)
                    if k < 2:
                        nc.vector.tensor_tensor(left[:, :, :], src, part[:, :, :], ALU.subtract).then_inc(cut[k], 1)
                        dve.wait_ge(cut[k], 2)
                        src = left[:, :, :]


def mix(nc, g, weights_T, exact_T, select):
    with ExitStack() as ctx:
        sb = lambda name, shape, dt=FP: ctx.enter_context(nc.sbuf_tensor("mi_" + name, shape, dt))
        sem = lambda name: take_semaphore(nc, g, "mi_" + name)
        hT, ps, w, mod, resid = g["hT"], g["ps"], g["w_odd"], g["mod"], g["resid"]
        gate = [sb(f"gate{i}", [P, CH]) for i in range(2)]
        up = [sb(f"up{i}", [P, CH]) for i in range(2)]
        prod = [sb(f"prod{i}", [P, CH]) for i in range(2)]
        y = sb("y", [P, CH])
        NU = NP_ + 1
        BG, BU, BW, BY, BT = 0, 2, 4, 6, 7
        made, gated, upped, used, downed = sem("ma"), sem("ga"), sem("up"), sem("us"), sem("do")
        y_ready, y_copied, y_turned, y_added = sem("yr"), sem("yc"), sem("yt"), sem("ya")
        early = lambda u: 1 if u == 0 else 0
        with nc.Block() as block:
            @block.tensor
            def _(pe):
                def make(c, u):
                    s = u % 2
                    rhs = hT[:, bass.ds(c * CH, CH)]
                    pe.wait_ge(used, c * NU + u + 1 + early(u))
                    if u < NP_:
                        nc.tensor.matmul(ps[:, BG + s, :], L0F(w, "Wg")[:, u * P:(u + 1) * P], rhs, start=True, stop=True)
                        nc.tensor.matmul(ps[:, BU + s, :], L0F(w, "Wu")[:, u * P:(u + 1) * P], rhs, start=True, stop=True)
                        nc.tensor.matmul(ps[:, BW + s, :], select[:, u, :], weights_T[0:3 * NE, bass.ds(c * CH, CH)],
                                         start=True, stop=True).then_inc(made, 1)
                    else:
                        nc.tensor.matmul(ps[0:NI, BG + s, :], L0F(w, "Wg_s"), rhs, start=True, stop=True)
                        nc.tensor.matmul(ps[0:NI, BU + s, :], L0F(w, "Wu_s"), rhs, start=True, stop=True).then_inc(made, 1)

                def down(c, u):
                    s = u % 2
                    pe.wait_ge(used, c * NU + u + 3)
                    if u == 0:
                        pe.wait_ge(y_copied, c + 1)
                    if u < NP_:
                        nc.tensor.matmul(ps[:, BY, :], L0F(w, "Wd")[:, u * E:(u + 1) * E], prod[s][:, :],
                                         start=(u == 0), stop=False).then_inc(downed, 1)
                    else:
                        nc.tensor.matmul(ps[:, BY, :], L0F(w, "Wd_s", NI), prod[s][0:NI, :], start=False,
                                         stop=False).then_inc(downed, 1)
                        nc.tensor.matmul(ps[:, BY, :], L0F(w, "bd", NE), exact_T[:, bass.ds(c * CH, CH)], start=False,
                                         stop=True).then_inc(y_ready, 1)

                with pe.Fori(0, NCH) as c:
                    for u in range(NU):
                        make(c, u)
                        if u:
                            down(c, u - 1)
                    down(c, NU - 1)
                    pe.wait_ge(y_copied, c + 2)
                    pe.wait_ge(y_added, c + 1)
                    for j in range(TPC):
                        last = nc.tensor.transpose(ps[:, BT, j * P:(j + 1) * P], y[:, j * P:(j + 1) * P], g["ident"][:, :])
                    last.then_inc(y_turned, 1)

            @block.scalar
            def _(act):
                nc.scalar.preload_act_table_set("silu_and_others")
                with act.Fori(0, NCH) as c:
                    for u in range(NU):
                        s, n = u % 2, (P if u < NP_ else NI)
                        bias = L0F(w, "bg")[:, u:u + 1] if u < NP_ else L0F(w, "bg_s", NI)
                        act.wait_ge(made, c * NU + u + 1)
                        act.wait_ge(used, c * NU + u + 1 + early(u))
                        nc.scalar.activation(gate[s][0:n, :], ps[0:n, BG + s, :], ACT.Silu, bias=bias).then_inc(gated, 1)

            @block.vector
            def _(dve):
                dve.sem_inc(used, 2)
                dve.sem_inc(downed, 2)
                dve.sem_inc(y_copied, 1)
                dve.sem_inc(y_added, 1)
                dve.sem_inc(y_turned, 1)
                with dve.Fori(0, B) as b:
                    for half in range(2):
                        c = b * 2 + half
                        for u in range(NU):
                            s, n = u % 2, (P if u < NP_ else NI)
                            bias = L0F(w, "bu")[:, u:u + 1] if u < NP_ else L0F(w, "bu_s", NI)
                            dve.wait_ge(gated, c * NU + u + 1)
                            if u < NP_:
                                nc.vector.scalar_tensor_tensor(up[s][:, :], ps[:, BU + s, :], bias, gate[s][:, :],
                                                               ALU.add, ALU.mult).then_inc(upped, 1)
                                dve.wait_ge(upped, c * NP_ + u + 1)
                                dve.wait_ge(downed, c * NU + u + 1 + early(u))
                                nc.vector.tensor_tensor(prod[s][:, :], up[s][:, :], ps[:, BW + s, :], ALU.mult).then_inc(used, 1)
                            else:
                                dve.wait_ge(downed, c * NU + u + 1)
                                nc.vector.scalar_tensor_tensor(prod[s][0:n, :], ps[0:n, BU + s, :], bias, gate[s][0:n, :],
                                                               ALU.add, ALU.mult).then_inc(used, 1)
                        dve.wait_ge(y_ready, c + 1)
                        dve.wait_ge(y_turned, c + 1)
                        nc.vector.tensor_scalar(y[:, :], ps[:, BY, :], L0F(w, "bd_s"), mod[:, bass.ds(mod_col(0, GB, b), 1)],
                                                ALU.add, ALU.mult).then_inc(y_copied, 1)
                        dve.wait_ge(y_turned, c + 2)
                        r = resid[:, bass.ds(c * CH, CH)]
                        nc.vector.tensor_tensor(r, r, ps[:, BT, :], ALU.add).then_inc(y_added, 1)


def state_space(nc, dram, g):
    with ExitStack() as ctx:
        sb = lambda name, shape, dt=FP: ctx.enter_context(nc.sbuf_tensor("ss_" + name, shape, dt))
        t = dict(xs=sb("xs", [P, NH, TOK]), sz=sb("sz", [P, NH, TOK]), bc=sb("bc", [3 * 32, TOK], BF),
                 select=sb("sel", [3 * 32, 32, P], BF), neg_a=sb("a", [P, NH * NS]), gain=sb("gain", [P, B]))
        t["dt"] = g["w_odd"][:, 0:NH * TOK].rearrange("p (h k) -> p h k", h=NH)
        scan_inputs(nc, dram, g, t)
        steps(nc, g, t)
        scan(nc, g, t)


def scan_inputs(nc, dram, g, t):
    with ExitStack() as ctx:
        sb = lambda name, shape, dt=FP: ctx.enter_context(nc.sbuf_tensor("si_" + name, shape, dt))
        sem = lambda name: take_semaphore(nc, g, "si_" + name)
        hT, ps, w, mod = g["hT"], g["ps"], g["w_even"], g["mod"]
        tmp = sb("tmp", [P, 1])
        p_all = sb("p", [96, CH], BF)
        rest = sb("rest", [96, CH])
        zero_set, sel_step, exp_done, vstep = sem("z"), sem("se"), sem("ex"), sem("vs")
        xz_ready, x_copied, z_copied, bc_ready, cut = sem("xz"), sem("xc"), sem("zc"), sem("br"), sem("cu")
        with nc.Block() as block:
            @block.gpsimd
            def _(pool):
                nc.gpsimd.memset(t["select"][:, :, :], 0.0).then_inc(zero_set, 1)
                pool.wait_ge(zero_set, 1)
                for k in range(3):
                    v = t["select"][k * 32:(k + 1) * 32, :, :]
                    nc.gpsimd.affine_select(out=v, in_=v, compare_op=ALU.not_equal, fill=1.0, base=0,
                                            pattern=[[-1, 32], [0, P]], channel_multiplier=1).then_inc(sel_step, 1)

            @block.tensor
            def _(pe):
                pe.wait_ge(g["l1a_loaded"], 16)
                with pe.Fori(0, NCH) as c:
                    rhs = hT[:, bass.ds(c * CH, CH)]
                    pe.wait_ge(x_copied, c + 1)
                    pe.wait_ge(z_copied, c + 1)
                    for k in range(4):
                        last = nc.tensor.matmul(ps[:, k, :], L1A(w, "W_in")[:, k * P:(k + 1) * P], rhs, start=True, stop=True)
                    last.then_inc(xz_ready, 1)
                    pe.wait_ge(x_copied, c + 2)
                    pe.wait_ge(cut, 8 * c + 8)
                    for k in range(NH):
                        last = nc.tensor.matmul(ps[0:96, 4, :], L1A(w, "W_bc")[:, k * 96:(k + 1) * 96],
                                                t["xs"][:, k, bass.ds(c * CH, CH)], start=(k == 0), stop=(k == NH - 1))
                    last.then_inc(bc_ready, 1)

            @block.scalar
            def _(act):
                act.wait_ge(g["l1a_loaded"], 16)
                nc.scalar.activation(t["neg_a"][:, :], L1A(w, "A_log"), ACT.Exp).then_inc(exp_done, 1)
                nc.scalar.activation(tmp[:, :], L1A(w, "gate"), ACT.Exp, scale=-1.0).then_inc(exp_done, 1)
                nc.scalar.preload_act_table_set("silu_and_others")
                act.sem_inc(z_copied, 1)
                with act.Fori(0, NCH) as c:
                    act.wait_ge(xz_ready, c + 1)
                    nc.scalar.activation(t["sz"][:, :, bass.ds(c * CH, CH)], ps[:, 2:4, :], ACT.Silu).then_inc(z_copied, 1)

            @block.vector
            def _(dve):
                dve.wait_ge(exp_done, 2)
                nc.vector.tensor_scalar(t["neg_a"][:, :], t["neg_a"][:, :], -1.0, None, ALU.mult).then_inc(vstep, 1)
                nc.vector.tensor_scalar(tmp[:, :], tmp[:, :], 1.0, None, ALU.add).then_inc(vstep, 1)
                dve.wait_ge(vstep, 2)
                nc.vector.reciprocal(tmp[:, :], tmp[:, :]).then_inc(vstep, 1)
                dve.wait_ge(vstep, 3)
                at = mod_col(1, GA, 0)
                nc.vector.tensor_scalar(t["gain"][:, :], mod[:, at:at + B], tmp[:, 0:1], None, ALU.mult).then_inc(vstep, 1)
                dve.sem_inc(x_copied, 1)
                dve.sem_inc(cut, 8)
                with dve.Fori(0, NCH) as c:
                    dve.wait_ge(xz_ready, c + 1)
                    nc.vector.tensor_copy(t["xs"][:, :, bass.ds(c * CH, CH)], ps[:, 0:2, :]).then_inc(x_copied, 1)
                    dve.wait_ge(bc_ready, c + 1)
                    src, dst = ps[0:96, 4, :], t["bc"]
                    at = bass.ds(c * CH, CH)
                    n = 8 * c + 8
                    nc.vector.tensor_copy(p_all[:, :], src).then_inc(cut, 1)
                    dve.wait_ge(cut, n + 1)
                    nc.vector.tensor_copy(dst[0:32, at], p_all[0:32, :]).then_inc(cut, 1)
                    nc.vector.scalar_tensor_tensor(rest[:, :], p_all[:, :], -1.0, src, ALU.mult, ALU.add).then_inc(cut, 1)
                    dve.wait_ge(cut, n + 3)
                    nc.vector.tensor_copy(p_all[:, :], rest[:, :]).then_inc(cut, 1)
                    dve.wait_ge(cut, n + 4)
                    nc.vector.tensor_copy(dst[32:64, at], p_all[32:64, :]).then_inc(cut, 1)
                    nc.vector.tensor_tensor(rest[:, :], rest[:, :], p_all[:, :], ALU.subtract).then_inc(cut, 1)
                    dve.wait_ge(cut, n + 6)
                    nc.vector.tensor_copy(p_all[:, :], rest[:, :]).then_inc(cut, 1)
                    dve.wait_ge(cut, n + 7)
                    nc.vector.tensor_copy(dst[64:96, at], p_all[64:96, :]).then_inc(cut, 1)
                    dve.wait_ge(cut, n + 8)


def steps(nc, g, t):
    with ExitStack() as ctx:
        pair = lambda name: [ctx.enter_context(nc.sbuf_tensor(f"sp_{name}{i}", [P, NH, CH], FP)) for i in range(2)]
        sem = lambda name: take_semaphore(nc, g, "sp_" + name)
        ps, w, dt = g["ps"], g["w_even"], t["dt"]
        size, e, log, fix = pair("size"), pair("e"), pair("log"), pair("fix")
        v_ready, v_read, abs_done, exp_done, log_done, fix_step, added = (sem(n) for n in ("v", "r", "a", "e", "l", "f", "d"))
        NFIX = 5
        SMALL = 2.0 ** -6

        def chunks(engine, body):
            with engine.Fori(0, NCH // 2) as i:
                for side in range(2):
                    body(i * 2 + side, side)

        with nc.Block() as block:
            @block.tensor
            def _(pe):
                def body(c, side):
                    pe.wait_ge(v_read, c + 1)
                    for half in range(NH):
                        for k in range(NH):
                            last = nc.tensor.matmul(
                                ps[:, 2 * side + half, :], L1A(w, "W_dt")[:, k * DI + half * P:k * DI + (half + 1) * P],
                                t["xs"][:, k, bass.ds(c * CH, CH)], start=(k == 0), stop=(k == NH - 1))
                    last.then_inc(v_ready, 1)

                chunks(pe, body)

            @block.scalar
            def _(act):
                nc.scalar.preload_act_table_set("natural_log_exp_and_others")
                act.sem_inc(v_read, 2)

                def body(c, side):
                    act.wait_ge(v_ready, c + 1)
                    for half in range(NH):
                        nc.scalar.activation(size[side][:, half, :], ps[:, 2 * side + half, :], ACT.Abs,
                                             bias=L1A(w, "b_dt")[:, half:half + 1]).then_inc(abs_done, 1)
                    for half in range(NH):
                        last = nc.scalar.activation(dt[:, half, bass.ds(c * CH, CH)], ps[:, 2 * side + half, :], ACT.Relu,
                                                    bias=L1A(w, "b_dt")[:, half:half + 1])
                    last.then_inc(v_read, 1)
                    act.wait_ge(abs_done, 2 * c + 2)
                    act.wait_ge(fix_step, NFIX * c + NFIX)
                    nc.scalar.activation(e[side][:, :, :], size[side][:, :, :], ACT.Exp, scale=-1.0).then_inc(exp_done, 1)
                    act.wait_ge(exp_done, c + 1)
                    act.wait_ge(added, 2 * c + 2)
                    nc.scalar.activation(log[side][:, :, :], e[side][:, :, :], ACT.Ln, bias=1.0).then_inc(log_done, 1)

                chunks(act, body)

            @block.vector
            def _(dve):
                dve.sem_inc(fix_step, 2 * NFIX)

                def body(c, side):
                    x, f = e[side][:, :, :], fix[side][:, :, :]
                    dve.wait_ge(log_done, c + 1)
                    dve.wait_ge(added, 2 * c + 2)
                    ops = (lambda: nc.vector.scalar_tensor_tensor(f, x, -4.0 / 3.0, x, ALU.add, ALU.mult),
                           lambda: nc.vector.scalar_tensor_tensor(f, f, 2.0, x, ALU.add, ALU.mult),
                           lambda: nc.vector.scalar_tensor_tensor(f, f, -4.0, x, ALU.add, ALU.mult),
                           lambda: nc.vector.scalar_tensor_tensor(f, f, -0.25, log[side][:, :, :], ALU.mult, ALU.subtract),
                           lambda: nc.vector.scalar_tensor_tensor(f, x, SMALL, f, ALU.is_lt, ALU.mult))
                    for n, op in enumerate(ops):
                        op().then_inc(fix_step, 1)
                        dve.wait_ge(fix_step, NFIX * c + 2 * NFIX + n + 1)

                chunks(dve, body)

            @block.gpsimd
            def _(pool):
                pool.sem_inc(added, 4)

                def body(c, side):
                    pool.wait_ge(fix_step, NFIX * c + 3 * NFIX)
                    nc.gpsimd.tensor_tensor(log[side][:, :, :], log[side][:, :, :], fix[side][:, :, :],
                                            ALU.add).then_inc(added, 1)
                    pool.wait_ge(added, 2 * c + 5)
                    pool.wait_ge(v_read, c + 3)
                    at = dt[:, :, bass.ds(c * CH, CH)]
                    nc.gpsimd.tensor_tensor(at, at, log[side][:, :, :], ALU.add).then_inc(added, 1)

                chunks(pool, body)


def scan(nc, g, t):
    with ExitStack() as ctx:
        sb = lambda name, shape, dt=FP: ctx.enter_context(nc.sbuf_tensor("sc_" + name, shape, dt))
        sem = lambda name: take_semaphore(nc, g, "sc_" + name)
        ps, w, resid = g["ps"], g["w_even"], g["resid"]
        drive = sb("drive", [P, NH, S])
        decay = [sb(f"decay{i}", [P, S]) for i in range(NH)]
        push = [sb(f"push{i}", [P, S]) for i in range(NH)]
        free = lambda k: g["hT"][:, k * S:(k + 1) * S]
        state = [[sb(f"state{i}", [P, S])[:, :] for i in range(NH)], [free(0), free(1)]]
        c_rows = [free(2), free(3)]
        seen = [sb(f"seen{i}", [P, S]) for i in range(NH)]
        driven = sem("dr")
        b_ready, c_ready, decayed, pushed, scanned, weighed, summed = (sem(n) for n in ("b", "c", "d", "p", "s", "w", "u"))
        y_step, mapped, scaled, turned, added = (sem(n) for n in ("y", "m", "sl", "t", "a"))
        c_kept = sem("ck")
        NY = 4
        with nc.Block() as block:
            def spread(pe, b, n, which):
                if n:
                    pe.wait_ge(c_kept, NS * b + n) if which else pe.wait_ge(pushed, 2 * NS * b + 2 * n)
                for c in range(2):
                    last = nc.tensor.matmul(ps[:, 2 * which + c, :], t["select"][:, which * NS + n, :],
                                            t["bc"][:, bass.ds(b * S + c * CH, CH)], start=True, stop=True)
                last.then_inc(c_ready if which else b_ready, 1)

            def add_up(pe, b, n, half):
                pe.wait_ge(weighed, 2 * NS * b + 2 * n + half + 1)
                for c in range(2):
                    last = nc.tensor.matmul(ps[:, 4 + 2 * half + c, :], g["ident"][:, :],
                                            seen[half][:, c * CH:(c + 1) * CH], start=(n == 0), stop=(n == NS - 1))
                last.then_inc(summed, 1)

            @block.tensor
            def _(pe):
                with pe.Fori(0, B) as b:
                    pe.wait_ge(added, b + 1)
                    for which in range(2):
                        spread(pe, b, 0, which)
                    for n in range(NS):
                        if n:
                            add_up(pe, b, n - 1, 0)
                        if n < NS - 1:
                            spread(pe, b, n + 1, 0)
                        if n:
                            add_up(pe, b, n - 1, 1)
                        if n < NS - 1:
                            spread(pe, b, n + 1, 1)
                    for half in range(NH):
                        add_up(pe, b, NS - 1, half)
                    pe.wait_ge(y_step, NY * b + NY)
                    for c in range(2):
                        for k in range(NH):
                            last = nc.tensor.matmul(ps[:, c, :], L1A(w, "W_out")[:, k * E:(k + 1) * E],
                                                    seen[k][:, c * CH:(c + 1) * CH], start=(k == 0), stop=(k == NH - 1))
                    last.then_inc(mapped, 1)
                    pe.wait_ge(scaled, b + 1)
                    for j in range(TPB):
                        last = nc.tensor.transpose(ps[:, 2 + j // TPC, (j % TPC) * P:(j % TPC + 1) * P],
                                                   push[0][:, j * P:(j + 1) * P], g["ident"][:, :])
                    last.then_inc(turned, 1)

            @block.scalar
            def _(act):
                nc.scalar.preload_act_table_set("exp_and_others")
                with act.Fori(0, B) as b:
                    act.wait_ge(driven, b + 1)
                    for n in range(NS):
                        for half in range(NH):
                            if n:
                                act.wait_ge(scanned, 2 * NS * b + 2 * n + half - 1)
                            a = half * NS + n
                            nc.scalar.activation(decay[half][:, :], t["dt"][:, half, bass.ds(b * S, S)], ACT.Exp,
                                                 scale=t["neg_a"][:, a:a + 1]).then_inc(decayed, 1)
                        act.wait_ge(c_ready, NS * b + n + 1)
                        if n >= 2:
                            act.wait_ge(weighed, 2 * NS * b + 2 * (n - 1))
                        nc.scalar.activation(c_rows[n % 2], ps[:, 2:4, :].rearrange("p c n -> p (c n)"),
                                             ACT.Copy).then_inc(c_kept, 1)

            @block.gpsimd
            def _(pool):
                with pool.Fori(0, B) as b:
                    for n in range(NS):
                        for half in range(NH):
                            at = 2 * NS * b + 2 * n + half
                            if half == 0:
                                pool.wait_ge(c_kept, NS * b + n + 1)
                                if n == 0:
                                    pool.wait_ge(driven, b + 1)
                            pool.wait_ge(scanned, at + 1)
                            if n:
                                pool.wait_ge(summed, at - 1)
                            nc.gpsimd.tensor_tensor(seen[half][:, :], state[n % 2][half], c_rows[n % 2],
                                                    ALU.mult).then_inc(weighed, 1)

            @block.vector
            def _(dve):
                dve.sem_inc(added, 1)

                def step(b):
                    nc.vector.tensor_tensor(drive[:, :, :], t["dt"][:, :, bass.ds(b * S, S)], t["xs"][:, :, bass.ds(b * S, S)],
                                            ALU.mult).then_inc(driven, 1)

                def body(b, more):
                    dve.wait_ge(driven, b + 1)
                    for n in range(NS):
                        at = 2 * NS * b + 2 * n
                        dve.wait_ge(b_ready, NS * b + n + 1)
                        for half in range(NH):
                            if n:
                                dve.wait_ge(scanned, at + half - 1)
                            nc.vector.tensor_tensor(push[half][:, :], drive[:, half, :],
                                                    ps[:, 0:2, :].rearrange("p c n -> p (c n)"), ALU.mult).then_inc(pushed, 1)
                        for half in range(NH):
                            dve.wait_ge(pushed, at + half + 1)
                            dve.wait_ge(decayed, at + half + 1)
                            if n >= 2:
                                dve.wait_ge(weighed, at + half - 3)
                            nc.vector.tensor_tensor_scan(state[n % 2][half], decay[half][:, :], push[half][:, :], 0.0,
                                                         ALU.mult, ALU.add).then_inc(scanned, 1)
                    if more:
                        step(b + 1)
                    for half in range(NH):
                        dve.wait_ge(summed, 2 * NS * b + 2 * NS - 1 + half)
                        dve.wait_ge(scanned, 2 * NS * b + 2 * NS - 1 + half)
                        nc.vector.scalar_tensor_tensor(
                            push[half][:, :], t["xs"][:, half, bass.ds(b * S, S)], L1A(w, "D")[:, half:half + 1],
                            ps[:, 4 + 2 * half:6 + 2 * half, :].rearrange("p c n -> p (c n)"), ALU.mult, ALU.add).then_inc(y_step, 1)
                    dve.wait_ge(y_step, NY * b + 2)
                    for half in range(NH):
                        nc.vector.tensor_tensor(seen[half][:, :], push[half][:, :], t["sz"][:, half, bass.ds(b * S, S)],
                                                ALU.mult).then_inc(y_step, 1)
                    dve.wait_ge(mapped, b + 1)
                    nc.vector.tensor_scalar(push[0][:, :], ps[:, 0:2, :].rearrange("p c n -> p (c n)"),
                                            t["gain"][:, bass.ds(b, 1)], None, ALU.mult).then_inc(scaled, 1)
                    dve.wait_ge(turned, b + 1)
                    r = resid[:, bass.ds(b * S, S)]
                    nc.vector.tensor_tensor(r, r, ps[:, 2:4, :].rearrange("p c n -> p (c n)"), ALU.add).then_inc(added, 1)
                    dve.wait_ge(added, b + 2)

                step(0)
                with dve.Fori(0, B - 1) as b:
                    body(b, True)
                body(B - 1, False)


SP1 = S + 1


def local_transformer(nc, dram, g):
    with ExitStack() as ctx:
        other = ctx.enter_context(nc.sbuf_tensor("lt_x", [P, B * SP1], FP))
        masks = ctx.enter_context(nc.sbuf_tensor("lt_masks", [P, 2 * KW], BF))
        window_masks(nc, g, other, masks)
        for layer in range(DEPTH):
            local_attention(nc, g, layer, g["hT"], other, masks)
            feed_forward(nc, g, layer, other, g["hT"])
        add_branch(nc, g, g["hT"])


def window_masks(nc, g, other, masks):
    with ExitStack() as ctx:
        zero = ctx.enter_context(nc.sbuf_tensor("wm_z", [P, 2 * KW], FP))
        step = take_semaphore(nc, g, "wm_s")
        with nc.Block() as block:
            @block.gpsimd
            def _(pool):
                nc.gpsimd.memset(zero[:, :], 0.0).then_inc(step, 1)
                for x in (g["hT"], other):
                    pads = x[:, :].rearrange("p (b s) -> p b s", s=SP1)[:, :, 0:1]
                    nc.gpsimd.memset(pads, 0.0).then_inc(step, 1)
                pool.wait_ge(step, 3)
                z3 = zero[:, :].rearrange("p (v k) -> p v k", v=2)
                m3 = masks[:, :].rearrange("p (v k) -> p v k", v=2)
                nc.gpsimd.affine_select(out=z3, in_=z3, compare_op=ALU.is_ge, fill=MASKED, base=WIN,
                                        pattern=[[0, 2], [-1, KW]], channel_multiplier=1).then_inc(step, 1)
                pool.wait_ge(step, 4)
                nc.gpsimd.affine_select(out=m3, in_=z3, compare_op=ALU.is_ge, fill=MASKED, base=0,
                                        pattern=[[0, 2], [1, KW]], channel_multiplier=-1).then_inc(step, 1)
                pool.wait_ge(step, 5)
                nc.gpsimd.memset(masks[:, 0:WIN], MASKED).then_inc(step, 1)


def local_attention(nc, g, layer, x, out, masks):
    with ExitStack() as ctx:
        tag = f"la{layer}_"
        sb = lambda name, shape, dt=FP: ctx.enter_context(nc.sbuf_tensor(tag + name, shape, dt))
        sem = lambda name: take_semaphore(nc, g, tag + name)
        ps, w, ident = g["ps"], g["w_odd"], g["ident"]
        W = lambda n: L1F(w, f"{n}{layer}")
        QK = 2 * INNER
        cos = sb("cos", [P, TPB, 2, DL])
        sin = sb("sin", [P, TPB, 2, DL])
        shifted = [sb(f"hs{i}", [P, P]) for i in range(2)]
        square = sb("sq", [P, QK])
        straight = sb("t1", [P, QK])
        turned = sb("t2", [P, QK])
        qk = sb("qk", [P, QK])
        sumsq = sb("ss", [P, 16])
        rnorm = sb("rn", [P, 16])
        power = sb("pw", [P, 16])
        qT = [sb(f"qT{i}", [P, 4, 2, P]) for i in range(2)]
        kT = [sb(f"kT{i}", [P, 4, KW]) for i in range(2)]
        v = [sb(f"v{i}", [P, INNER]) for i in range(2)]
        probs = [sb(f"p{i}", [P, 2, 2 * P]) for i in range(2)]
        probsT = [sb(f"pT{i}", [P, 2, 2, P]) for i in range(2)]
        neg_max = [sb(f"nm{i}", [P, 2]) for i in range(2)]
        sums = [sb(f"rs{i}", [P, HL]) for i in range(2)]
        inv = sb("inv", [P, HL])
        o = sb("o", [P, INNER])
        oT = sb("oT", [P, 4, P])
        (tables, shift_ready, qk_made, v_made, squared, v_kept, roped, ss_ready, joined, rn_step, scaled, qT_turned,
         qT_kept, kT_turned, kT_kept, k_tail, scored, maxed, exped, pT_turned, pT_kept, pv_done, normed, oT_turned,
         oT_kept, y_made, y_added, preset, pool_past) = (sem(n) for n in (
             "tb", "sh", "qm", "vm", "sq", "vk", "ro", "ss", "jo", "rn", "sc", "qt", "qk", "kt", "kk", "kl", "so", "mx",
             "ex", "pt", "pk", "pv", "no", "ot", "ok", "ym", "ya", "pr", "pp"))
        NPAIR = HL // 2
        PRESET = 9
        later = lambda n: not isinstance(n, int) or n > 0

        def tiles(engine, body):
            body(0, 0, 2)
            with engine.Fori(0, NT // 2 - 2) as i:
                body(i * 2 + 1, 1, 2)
                body(i * 2 + 2, 0, 2)
            body(NT - 3, 1, 2)
            body(NT - 2, 0, 1)
            body(NT - 1, 1, 0)

        with nc.Block() as block:
            @block.gpsimd
            def _(pool):
                nc.gpsimd.memset(power[:, :], -0.5).then_inc(preset, 1)
                for i in range(2):
                    nc.gpsimd.memset(probs[i][:, :, 0:WIN], 0.0).then_inc(preset, 1)
                    nc.gpsimd.memset(v[i][:, :], 0.0).then_inc(preset, 1)
                    nc.gpsimd.memset(kT[i][:, :, :], 0.0).then_inc(preset, 1)
                    nc.gpsimd.memset(qT[i][:, :, :, :], 0.0).then_inc(preset, 1)
                pool.wait_ge(preset, PRESET)

                def past():
                    pool.sem_inc(pool_past, 1)

                def shift(n, half):
                    at = n * P + n // TPB
                    nc.gpsimd.tensor_copy(shifted[half][0:64, :], x[0:64, bass.ds(at + 1, P)]).then_inc(shift_ready, 1)
                    pool.wait_ge(shift_ready, 2 * n + 1)
                    past()
                    nc.gpsimd.tensor_copy(shifted[half][64:P, :], x[64:P, bass.ds(at, P)]).then_inc(shift_ready, 1)
                    pool.wait_ge(shift_ready, 2 * n + 2)
                    past()

                def join(n):
                    pool.wait_ge(ss_ready, n + 1)
                    past()
                    nc.gpsimd.tensor_scalar(rnorm[:, :], sumsq[:, :], 1e-24, None, ALU.max).then_inc(rn_step, 1)
                    pool.wait_ge(rn_step, 3 * n + 1)
                    past()
                    nc.gpsimd.tensor_tensor(rnorm[:, :], rnorm[:, :], power[:, :], ALU.pow).then_inc(rn_step, 1)
                    pool.wait_ge(rn_step, 3 * n + 2)
                    past()
                    nc.gpsimd.tensor_scalar(rnorm[:, 0:HL], rnorm[:, 0:HL], 8.0, None, ALU.mult).then_inc(rn_step, 1)
                    pool.wait_ge(roped, 3 * n + 3)
                    past()
                    nc.gpsimd.tensor_tensor(straight[:, :], straight[:, :], turned[:, :], ALU.add).then_inc(joined, 1)

                def tail(n, half):
                    pool.wait_ge(kT_kept, n + 1)
                    past()
                    nc.gpsimd.tensor_copy(kT[1 - half][:, :, 0:WIN], kT[half][:, :, P:KW]).then_inc(k_tail, 1)

                shift(0, 0)
                shift(1, 1)
                join(0)
                tail(0, 0)

                def body(n, half, follow):
                    if follow > 1:
                        pool.wait_ge(v_made, n + 1)
                        past()
                        shift(n + 2, half)
                    if follow:
                        join(n + 1)
                    if follow > 1:
                        pool.wait_ge(scored, NPAIR * (n + 1))
                        past()
                        tail(n + 1, 1 - half)

                tiles(pool, body)

            @block.tensor
            def _(pe):
                pe.wait_ge(g["l1f_loaded"], 16)
                pe.wait_ge(preset, PRESET)

                def project_qk(n, half):
                    pe.wait_ge(shift_ready, 2 * n + 2)
                    for k, kept in ((0, qT_kept), (1, kT_kept)):
                        if later(n):
                            pe.wait_ge(kept, n)
                        last = nc.tensor.matmul(ps[:, k, :], shifted[half][:, :], W("wqkv")[:, k * INNER:(k + 1) * INNER],
                                                start=True, stop=True)
                    last.then_inc(qk_made, 1)

                def project_v(n, half):
                    nc.tensor.matmul(ps[:, 2, :], shifted[half][:, :], W("wqkv")[:, 2 * INNER:3 * INNER],
                                     start=True, stop=True).then_inc(v_made, 1)

                def turn(n, k):
                    pe.wait_ge(scaled, n + 1)
                    for j in range(4):
                        last = nc.tensor.transpose(ps[:, k, j * P:(j + 1) * P], qk[:, (4 * k + j) * P:(4 * k + j + 1) * P],
                                                   ident[:, :])
                    last.then_inc((qT_turned, kT_turned)[k], 1)

                def score(n, half, p):
                    s = p % 2
                    if p == 0:
                        pe.wait_ge(kT_kept, n + 1)
                        if later(n):
                            pe.wait_ge(k_tail, n)
                    pe.wait_ge(exped, 2 * NPAIR * n + 2 * p + 2)
                    for r in range(2):
                        dst = ps[:, 4 + s, r * KW:(r + 1) * KW]
                        nc.tensor.matmul(dst, qT[half][:, p, r, :], kT[half][:, p, :], start=True, stop=False)
                        at = KW if half else ((n % TPB + TPB - 1) // TPB) * KW
                        last = nc.tensor.matmul(dst, g["ident_bf"][:, :], masks[:, bass.ds(at, KW)], start=False, stop=True)
                    last.then_inc(scored, 1)

                def turn_probs(n, p):
                    m = NPAIR * n + p
                    pe.wait_ge(exped, 2 * m + 6)
                    pe.wait_ge(pT_kept, m + 1)
                    for r in range(2):
                        for k in range(2):
                            last = nc.tensor.transpose(ps[:, 6, (2 * r + k) * P:(2 * r + k + 1) * P],
                                                       probs[p % 2][:, r, k * P:(k + 1) * P], ident[:, :])
                    last.then_inc(pT_turned, 1)

                def weigh(n, half, p):
                    if p == 0:
                        pe.wait_ge(normed, 2 * n + 2)
                        pe.wait_ge(v_kept, n + 1)
                    pe.wait_ge(pT_kept, NPAIR * n + p + 2)
                    for r in range(2):
                        h = 2 * p + r
                        for k in range(2):
                            last = nc.tensor.matmul(ps[:, 7, h * DL:(h + 1) * DL], probsT[p % 2][:, r, k, :],
                                                    v[half if k else 1 - half][:, h * DL:(h + 1) * DL],
                                                    start=(k == 0), stop=(k == 1))
                    last.then_inc(pv_done, 1)

                def turn_out(n):
                    pe.wait_ge(normed, 2 * n + 4)
                    for j in range(4):
                        last = nc.tensor.transpose(ps[:, 3, j * P:(j + 1) * P], o[:, j * P:(j + 1) * P], ident[:, :])
                    last.then_inc(oT_turned, 1)

                def map_out(n):
                    pe.wait_ge(oT_kept, n + 1)
                    for j in range(4):
                        last = nc.tensor.matmul(ps[:, 2, 0:P], W("wo")[:, j * E:(j + 1) * E], oT[:, j, :],
                                                start=(j == 0), stop=(j == 3))
                    last.then_inc(y_made, 1)

                def body(n, half, follow):
                    if follow:
                        project_qk(n + 1, 1 - half)
                    score(n, half, 0)
                    if later(n):
                        turn_out(n - 1)
                    score(n, half, 1)
                    turn_probs(n, 0)
                    pe.wait_ge(v_kept, n + 1)
                    if later(n):
                        map_out(n - 1)
                    score(n, half, 2)
                    turn_probs(n, 1)
                    weigh(n, half, 0)
                    if follow:
                        if later(n):
                            pe.wait_ge(y_added, n)
                        project_v(n + 1, 1 - half)
                    score(n, half, 3)
                    turn_probs(n, 2)
                    weigh(n, half, 1)
                    turn_probs(n, 3)
                    if follow:
                        turn(n + 1, 0)
                    weigh(n, half, 2)
                    if follow:
                        turn(n + 1, 1)
                    weigh(n, half, 3)

                project_qk(0, 0)
                project_v(0, 0)
                turn(0, 0)
                turn(0, 1)
                tiles(pe, body)
                turn_out(NT - 1)
                map_out(NT - 1)

            @block.scalar
            def _(act):
                nc.scalar.preload_act_table_set("exp_and_others")
                act.sem_inc(exped, 4)
                act.sem_inc(pT_kept, 1)
                act.wait_ge(preset, PRESET)

                def square_qk(n):
                    act.wait_ge(qk_made, n + 1)
                    if later(n):
                        act.wait_ge(ss_ready, n)
                    nc.scalar.activation(square[:, :], ps[:, 0:2, :].rearrange("p c n -> p (c n)"), ACT.Square).then_inc(squared, 1)

                def keep_v(n, half):
                    act.wait_ge(v_made, n + 1)
                    if later(n):
                        act.wait_ge(pv_done, NPAIR * n)
                    nc.scalar.activation(v[half][:, :], ps[:, 2, :], ACT.Copy).then_inc(v_kept, 1)

                def keep_qkT(n, half):
                    act.wait_ge(qT_turned, n + 1)
                    for r in range(2):
                        rows = slice(64 * r, 64 * r + 64)
                        last = nc.scalar.activation(qT[half][rows, :, r, :],
                                                    ps[rows, 0, :].rearrange("p (j q) -> p j q", j=4), ACT.Copy)
                    last.then_inc(qT_kept, 1)
                    act.wait_ge(kT_turned, n + 1)
                    nc.scalar.activation(kT[half][:, :, WIN:KW], ps[:, 1, :].rearrange("p (j q) -> p j q", j=4),
                                         ACT.Copy).then_inc(kT_kept, 1)

                def exps(n, half, p):
                    s = p % 2
                    m = NPAIR * n + p
                    act.wait_ge(maxed, m + 1)
                    act.wait_ge(pT_turned, m + 1)
                    for r in range(2):
                        h = 2 * p + r
                        nc.scalar.activation(probs[s][:, r, WIN:2 * P], ps[:, 4 + s, r * KW:(r + 1) * KW], ACT.Exp,
                                             bias=neg_max[s][:, r:r + 1],
                                             accum_out=sums[half][:, h:h + 1]).then_inc(exped, 1)

                def keep_pT(n, p):
                    act.wait_ge(pT_turned, NPAIR * n + p + 3)
                    nc.scalar.activation(probsT[p % 2][:, :, :, :].rearrange("p r k q -> p (r k q)"), ps[:, 6, :],
                                         ACT.Copy).then_inc(pT_kept, 1)

                def keep_oT(n):
                    act.wait_ge(oT_turned, n + 1)
                    if later(n):
                        act.wait_ge(y_made, n)
                    nc.scalar.activation(oT[:, :, :], ps[:, 3, :].rearrange("p (j q) -> p j q", j=4),
                                         ACT.Copy).then_inc(oT_kept, 1)

                def body(n, half, follow):
                    if follow:
                        square_qk(n + 1)
                    exps(n, half, 0)
                    if later(n):
                        keep_oT(n - 1)
                    exps(n, half, 1)
                    keep_pT(n, 0)
                    exps(n, half, 2)
                    exps(n, half, 3)
                    keep_pT(n, 2)
                    if follow:
                        keep_qkT(n + 1, 1 - half)
                        keep_v(n + 1, 1 - half)

                square_qk(0)
                keep_qkT(0, 0)
                keep_v(0, 0)
                tiles(act, body)
                keep_oT(NT - 1)

            @block.vector
            def _(dve):
                dve.wait_ge(g["l1f_loaded"], 16)
                dve.wait_ge(preset, PRESET)
                base = lambda n: w[:, L1F.at[n][0]:L1F.at[n][0] + TPB * DL].rearrange("p (t d) -> p t d", t=TPB)
                for k, (n, sc) in enumerate((("q", "qs"), ("k", "ks"))):
                    s3 = lambda lo, hi: W(sc)[:, lo:hi].unsqueeze(1).to_broadcast([P, TPB, hi - lo])
                    nc.vector.tensor_tensor(cos[:, :, k, :], base("cos_" + n), s3(0, DL), ALU.mult).then_inc(tables, 1)
                    nc.vector.tensor_tensor(sin[:, :, k, 0:32], base("sin_" + n)[:, :, 0:32], s3(32, 64), ALU.mult).then_inc(tables, 1)
                    nc.vector.tensor_tensor(sin[:, :, k, 32:64], base("sin_" + n)[:, :, 32:64], s3(0, 32), ALU.mult).then_inc(tables, 1)
                dve.wait_ge(tables, 6)
                dve.sem_inc(pT_turned, 2)
                dve.sem_inc(normed, 2)
                split = lambda t: t.rearrange("p (k h d) -> p k h d", k=2, h=HL)
                src = ps[:, 0:2, :].rearrange("p k (h d) -> p k h d", h=HL)

                def table(t, n, lo, hi):
                    j = n % TPB
                    flat = t[:, :, :, :].rearrange("p t k d -> p (t k d)")
                    one = flat[:, bass.ds(j * (2 * DL), 2 * DL)].rearrange("p (k d) -> p k d", k=2)[:, :, lo:hi]
                    return one.unsqueeze(2).to_broadcast([P, 2, HL, hi - lo])

                def rope_straight(n):
                    dve.wait_ge(squared, n + 1)
                    if later(n):
                        dve.wait_ge(scaled, n)
                    nc.vector.tensor_tensor(split(straight[:, :]), src, table(cos, n, 0, DL), ALU.mult).then_inc(roped, 1)

                def rope_turned(n):
                    for lo, hi in ((0, 32), (32, 64)):
                        nc.vector.tensor_tensor(split(turned[:, :])[:, :, :, lo:hi], src[:, :, :, 32 - lo:64 - lo],
                                                table(sin, n, lo, hi), ALU.mult).then_inc(roped, 1)

                def sum_squares(n):
                    dve.wait_ge(squared, n + 1)
                    if later(n):
                        dve.wait_ge(rn_step, 3 * n)
                    nc.vector.tensor_reduce(sumsq[:, :], square[:, :].rearrange("p (h d) -> p h d", d=DL), axis=AX.X,
                                            op=ALU.add).then_inc(ss_ready, 1)

                def scale(n):
                    dve.wait_ge(joined, n + 1)
                    dve.wait_ge(rn_step, 3 * n + 3)
                    if later(n):
                        dve.wait_ge(kT_turned, n)
                    nc.vector.tensor_tensor(qk[:, :].rearrange("p (h d) -> p h d", d=DL),
                                            straight[:, :].rearrange("p (h d) -> p h d", d=DL),
                                            rnorm[:, :].unsqueeze(2).to_broadcast([P, 16, DL]), ALU.mult).then_inc(scaled, 1)

                def maxima(n, p):
                    s = p % 2
                    m = NPAIR * n + p
                    dve.wait_ge(scored, m + 1)
                    dve.wait_ge(exped, 2 * m + 2)
                    nc.vector.tensor_reduce(neg_max[s][:, :], ps[:, 4 + s, 0:2 * KW].rearrange("p (r k) -> p r k", r=2),
                                            axis=AX.X, op=ALU.max, negate=True).then_inc(maxed, 1)

                def keep_pT(n, p):
                    dve.wait_ge(pT_turned, NPAIR * n + p + 3)
                    nc.vector.tensor_copy(probsT[p % 2][:, :, :, :].rearrange("p r k q -> p (r k q)"),
                                          ps[:, 6, :]).then_inc(pT_kept, 1)

                def finish(n, half):
                    dve.wait_ge(pv_done, NPAIR * (n + 1))
                    nc.vector.reciprocal(inv[:, :], sums[half][:, :]).then_inc(normed, 1)
                    dve.wait_ge(normed, 2 * n + 3)
                    if later(n):
                        dve.wait_ge(oT_turned, n)
                    nc.vector.tensor_tensor(o[:, :].rearrange("p (h d) -> p h d", d=DL),
                                            ps[:, 7, :].rearrange("p (h d) -> p h d", d=DL),
                                            inv[:, :].unsqueeze(2).to_broadcast([P, HL, DL]), ALU.mult).then_inc(normed, 1)

                def add(n):
                    dve.wait_ge(y_made, n + 1)
                    at = bass.ds(n * P + n // TPB + 1, P)
                    nc.vector.tensor_tensor(out[:, at], x[:, at], ps[:, 2, 0:P], ALU.add).then_inc(y_added, 1)

                rope_straight(0)
                rope_turned(0)
                sum_squares(0)
                scale(0)

                def body(n, half, follow):
                    if later(n):
                        finish(n - 1, 1 - half)
                    maxima(n, 0)
                    if follow:
                        sum_squares(n + 1)
                    maxima(n, 1)
                    if follow:
                        rope_straight(n + 1)
                        rope_turned(n + 1)
                    if later(n):
                        add(n - 1)
                    maxima(n, 2)
                    keep_pT(n, 1)
                    maxima(n, 3)
                    if follow:
                        scale(n + 1)
                    keep_pT(n, 3)

                tiles(dve, body)
                finish(NT - 1, 1)
                add(NT - 1)


def feed_forward(nc, g, layer, x, out):
    with ExitStack() as ctx:
        tag = f"ff{layer}_"
        sb = lambda name, shape, dt=FP: ctx.enter_context(nc.sbuf_tensor(tag + name, shape, dt))
        sem = lambda name: take_semaphore(nc, g, tag + name)
        ps, w, ident = g["ps"], g["w_odd"], g["ident"]
        W = lambda n: L1F(w, f"{n}{layer}")
        mean_w = sb("mw", [P, P])
        shifted = sb("hs", [P, CH])
        centred = sb("hc", [P, CH])
        square = sb("sq", [P, CH])
        var = sb("var", [P, TPC])
        rstd = sb("rs", [P, TPC])
        power = sb("pw", [P, TPC])
        rows = sb("rw", [P, TPC, P])
        scaled = sb("sc", [P, CH])
        normed = [sb(f"hn{i}", [P, CH]) for i in range(2)]
        gelu = [sb(f"ge{i}", [P, CH]) for i in range(2)]
        prod = [sb(f"pr{i}", [P, CH]) for i in range(2)]
        (preset, shift_ready, mean_ready, centred_ready, squared, var_ready, var_kept, rstd_ready, rows_ready, spread,
         scaled_ready, normed_ready, made, gelued, used, downed, y_made, y_added, pool_past) = (sem(n) for n in (
             "ps", "sh", "me", "ce", "sq", "va", "vk", "rd", "rr", "sp", "sl", "nr", "ma", "ge", "us", "do", "ym", "ya", "pp"))
        NU = NHID
        early = lambda u: 1 if u == 0 else 0
        with nc.Block() as block:
            @block.gpsimd
            def _(pool):
                nc.gpsimd.memset(power[:, :], -0.5).then_inc(preset, 1)
                nc.gpsimd.memset(mean_w[:, :], 1.0 / P).then_inc(preset, 1)
                pool.wait_ge(preset, 2)

                def norm(c, first):
                    b, half = c // 2, c % 2
                    at = c * CH + b
                    if not first:
                        pool.wait_ge(centred_ready, c)
                        pool.sem_inc(pool_past, 1)
                    nc.gpsimd.tensor_copy(shifted[0:64, :], x[0:64, bass.ds(at + 1, CH)]).then_inc(shift_ready, 1)
                    pool.wait_ge(shift_ready, 2 * c + 1)
                    pool.sem_inc(pool_past, 1)
                    nc.gpsimd.tensor_copy(shifted[64:P, :], x[64:P, bass.ds(at, CH)]).then_inc(shift_ready, 1)
                    pool.wait_ge(shift_ready, 2 * c + 2)
                    pool.sem_inc(pool_past, 1)
                    pool.wait_ge(var_kept, c + 1)
                    pool.sem_inc(pool_past, 1)
                    nc.gpsimd.tensor_tensor(rstd[:, :], var[:, :], power[:, :], ALU.pow).then_inc(rstd_ready, 1)
                    pool.wait_ge(rstd_ready, c + 1)
                    pool.wait_ge(spread, c + 1)
                    pool.sem_inc(pool_past, 1)
                    nc.gpsimd.tensor_copy(rows[:, :, :], rstd[:, :].unsqueeze(2).to_broadcast([P, TPC, P])).then_inc(rows_ready, 1)

                norm(0, True)
                with pool.Fori(1, NCH) as c:
                    norm(c, False)

            @block.tensor
            def _(pe):
                pe.wait_ge(preset, 2)

                def norm(c, step):
                    if step == 0:
                        pe.wait_ge(shift_ready, 2 * c + 2)
                        nc.tensor.matmul(ps[:, 0, :], mean_w[:, :], shifted[:, :], start=True, stop=True).then_inc(mean_ready, 1)
                    elif step == 1:
                        pe.wait_ge(squared, c + 1)
                        for j in range(TPC):
                            last = nc.tensor.matmul(ps[:, 1, j:j + 1], square[:, j * P:(j + 1) * P], mean_w[:, 0:1],
                                                    start=True, stop=True)
                        last.then_inc(var_ready, 1)
                    else:
                        pe.wait_ge(rows_ready, c + 1)
                        pe.wait_ge(scaled_ready, c + 1)
                        for j in range(TPC):
                            last = nc.tensor.matmul(ps[:, 2, j * P:(j + 1) * P], rows[:, j, :], ident[:, :], start=True, stop=True)
                        last.then_inc(spread, 1)

                def make(c, half, u):
                    s = u % 2
                    if u == 0:
                        pe.wait_ge(normed_ready, c + 1)
                    pe.wait_ge(used, NU * c + u + 1 + early(u))
                    nc.tensor.matmul(ps[:, 3 + s, :], W("w1g")[:, u * P:(u + 1) * P], normed[half][:, :], start=True, stop=True)
                    nc.tensor.matmul(ps[:, 5 + s, :], W("w1a")[:, u * P:(u + 1) * P], normed[half][:, :], start=True,
                                     stop=True).then_inc(made, 1)

                def down(c, u):
                    pe.wait_ge(used, NU * c + u + 3)
                    if u == 0:
                        pe.wait_ge(y_added, c + 1)
                    mm = nc.tensor.matmul(ps[:, 7, :], W("w2")[:, u * E:(u + 1) * E], prod[u % 2][:, :], start=(u == 0),
                                          stop=(u == NU - 1))
                    mm.then_inc(downed, 1)
                    return mm

                for step in range(3):
                    norm(0, step)

                def body(c, half, more):
                    for u in range(NU):
                        if more:
                            norm(c + 1, u)
                        make(c, half, u)
                        if u:
                            down(c, u - 1)
                    down(c, NU - 1)

                with pe.Fori(0, NCH // 2 - 1) as i:
                    for half in range(2):
                        body(i * 2 + half, half, True)
                body(NCH - 2, 0, True)
                body(NCH - 1, 1, False)

            @block.scalar
            def _(act):
                nc.scalar.preload_act_table_set("gelu_and_others")

                def norm(c, half, step):
                    if step == 0:
                        act.wait_ge(centred_ready, c + 1)
                        nc.scalar.activation(square[:, :], centred[:, :], ACT.Square).then_inc(squared, 1)
                    else:
                        act.wait_ge(scaled_ready, c + 2)
                        nc.scalar.activation(normed[half][:, :], scaled[:, :], ACT.Identity, bias=W("ln_b"),
                                             scale=W("ln_g")).then_inc(normed_ready, 1)

                norm(0, 0, 0)
                norm(0, 0, 1)

                def body(c, half, more):
                    for u in range(NU):
                        if more and u == 0:
                            norm(c + 1, 1 - half, 0)
                        act.wait_ge(made, NU * c + u + 1)
                        act.wait_ge(used, NU * c + u + 1 + early(u))
                        nc.scalar.activation(gelu[u % 2][:, :], ps[:, 3 + u % 2, :], ACT.Gelu,
                                             bias=W("b1g")[:, u:u + 1]).then_inc(gelued, 1)
                    if more:
                        norm(c + 1, 1 - half, 1)

                with act.Fori(0, NCH // 2 - 1) as i:
                    for half in range(2):
                        body(i * 2 + half, half, True)
                body(NCH - 2, 0, True)
                body(NCH - 1, 1, False)

            @block.vector
            def _(dve):
                dve.sem_inc(used, 2)
                dve.sem_inc(downed, 2)
                dve.sem_inc(y_added, 1)
                dve.sem_inc(scaled_ready, 1)
                dve.sem_inc(spread, 1)

                def norm(c, step):
                    if step == 0:
                        dve.wait_ge(mean_ready, c + 1)
                        if not isinstance(c, int) or c:
                            dve.wait_ge(scaled_ready, c + 1)
                        nc.vector.tensor_tensor(centred[:, :], shifted[:, :], ps[:, 0, :], ALU.subtract).then_inc(centred_ready, 1)
                    elif step == 1:
                        dve.wait_ge(var_ready, c + 1)
                        nc.vector.tensor_scalar(var[:, :], ps[:, 1, 0:TPC], LN_EPS, None, ALU.add).then_inc(var_kept, 1)
                    else:
                        dve.wait_ge(spread, c + 2)
                        if not isinstance(c, int) or c:
                            dve.wait_ge(normed_ready, c)
                        nc.vector.tensor_tensor(scaled[:, :], centred[:, :], ps[:, 2, :], ALU.mult).then_inc(scaled_ready, 1)

                for step in range(3):
                    norm(0, step)

                def body(c, half, more):
                    for u in range(NU):
                        if more:
                            norm(c + 1, u)
                        dve.wait_ge(gelued, NU * c + u + 1)
                        dve.wait_ge(downed, NU * c + u + 1 + early(u))
                        nc.vector.scalar_tensor_tensor(prod[u % 2][:, :], ps[:, 5 + u % 2, :], W("b1a")[:, u:u + 1],
                                                       gelu[u % 2][:, :], ALU.add, ALU.mult).then_inc(used, 1)
                    dve.wait_ge(downed, NU * (c + 1) + 2)
                    at = bass.ds(c * CH + c // 2 + 1, CH)
                    nc.vector.scalar_tensor_tensor(out[:, at], ps[:, 7, :], W("b2"), x[:, at], ALU.add, ALU.add).then_inc(y_added, 1)

                with dve.Fori(0, NCH // 2 - 1) as i:
                    for half in range(2):
                        body(i * 2 + half, half, True)
                body(NCH - 2, 0, True)
                body(NCH - 1, 1, False)


def add_branch(nc, g, x):
    with ExitStack() as ctx:
        tail = Residual(nc, g, "ab", ctx)
        with nc.Block() as block:
            @block.scalar
            def _(act):
                for c in range(NCH):
                    if c >= 2:
                        act.wait_ge(tail.back, c - 1)
                    at, col = c * CH + c // 2 + 1, mod_col(1, GB, c // 2)
                    nc.scalar.activation(tail.z[c % 2][:, :], x[:, at:at + CH], ACT.Copy,
                                         scale=g["mod"][:, col:col + 1]).then_inc(tail.gated, 1)

            @block.tensor
            def _(pe):
                for c in range(NCH):
                    tail.turn(pe, c)

            @block.vector
            def _(dve):
                for c in range(NCH):
                    tail.add(dve, c)



def rope_tables():
    f = (1.0 / np.float32(10000.0) ** (np.arange(0, E, 2, dtype=np.float32) / np.float32(E))).astype(np.float32)
    a = np.arange(S, dtype=np.float32)[:, None] * f[None, :]
    a = np.concatenate([a, a], -1)
    sign = np.where(np.arange(E) < E // 2, -1.0, 1.0).astype(np.float32)
    return np.cos(a).T.astype(np.float32), (np.sin(a) * sign).T.astype(np.float32)


def xpos_tables():
    half = np.arange(0, DL, 2, dtype=np.float32)
    f = (1.0 / np.float32(10000.0) ** (half / np.float32(DL))).astype(np.float32)
    t = np.arange(S, dtype=np.float32)
    a = t[:, None] * f[None, :]
    a = np.concatenate([a, a], -1)
    base = ((half + np.float32(0.4 * DL)) / np.float32(1.4 * DL)).astype(np.float32)
    power = ((t - S // 2) / np.float32(WIN // 2)).astype(np.float32)
    s = (base[None, :] ** power[:, None]).astype(np.float32)
    s = np.concatenate([s, s], -1)
    sign = np.where(np.arange(DL) < DL // 2, -1.0, 1.0).astype(np.float32)
    c, n = np.cos(a).astype(np.float32), np.sin(a).astype(np.float32)
    return [x.astype(np.float32) for x in (c * s, n * s * sign, c / s, n / s * sign)]


def pack(layout, **parts):
    a = np.zeros((P, layout.width), np.float32)
    for name, x in parts.items():
        n, w = layout.at[name]
        x = np.asarray(x)
        a[:x.shape[0], n:n + w] = x.reshape(x.shape[0], w)
    return a


def kernel(**i):
    import concourse.bacc as bacc
    from concourse.bass_utils import run_bass_kernel_spmd

    arrays = lay_out(i)
    nc = bacc.Bacc("TRN2", target_bir_lowering=False, num_devices=1)
    nc.disable_value_cache = True
    dram = {n: nc.dram_tensor(f"in_{n}", a.shape, FP, kind="ExternalInput").ap() for n, a in arrays.items()}
    out = nc.dram_tensor("out_0", (B, S, E), FP, kind="ExternalOutput").ap()
    build(nc, dram, out)
    r = run_bass_kernel_spmd(nc, [{f"in_{n}": a for n, a in arrays.items()}], core_ids=[0])
    return r.results[0]["out_0"]


def lay_out(i):
    i = {k: np.asarray(v) for k, v in i.items()}
    col = lambda v: np.reshape(v, (-1, 1))
    rows = lambda v, n=P: np.broadcast_to(np.reshape(v, (1, -1)), (n, np.size(v)))
    turn = np.concatenate([np.arange(E // 2, E), np.arange(E // 2)])
    a = lambda n: i["L0_attn_" + n]
    cos, sin = rope_tables()
    out = {"x": i["L0_attn_x"]}
    out["w_mod"] = pack(MOD, cT0=i["L0_c"].T, cT1=i["L1_c"].T, wmod0=i["L0_wmod"], wmod1=i["L1_wmod"])
    out["w_l0a"] = pack(L0A, wqr=a("wqr"), wqr_rot=a("wqr")[:, turn], wkr=a("wkr"), wkr_rot=a("wkr")[:, turn],
                        wkv=a("wkv"), wv=np.concatenate([a("wv"), a("bv")[None, :]]), wo=a("wo"),
                        bqr=col(a("bqr")), bqr_rot=col(a("bqr")[turn]), bkr=col(a("bkr")), bkr_rot=col(a("bkr")[turn]),
                        bkv=col(a("bkv")), bo=np.broadcast_to(col(a("bo")), (E, E)), cos=cos, sin=sin)
    f = lambda n: i["L0_ffn_" + n]
    out["w_l0f"] = pack(
        L0F, Wr=f("Wr"), br=rows(f("br")), Wg_s=f("Wg_s"), Wu_s=f("Wu_s"), Wd_s=f("Wd_s"), bg_s=col(f("bg_s")),
        bu_s=col(f("bu_s")), bd_s=col(f("bd_s")), bg=f("bg").reshape(NP_, 2 * NI).T, bu=f("bu").reshape(NP_, 2 * NI).T,
        bd=f("bd"), Wg=f("Wg").transpose(1, 0, 2).reshape(E, -1), Wu=f("Wu").transpose(1, 0, 2).reshape(E, -1),
        Wd=f("Wd").reshape(NP_, 2 * NI, E).transpose(1, 0, 2).reshape(2 * NI, -1))
    s = lambda n: i["L1_attn_" + n]
    halves = lambda m: m.reshape(NH, P, -1).transpose(1, 0, 2).reshape(P, -1)
    bc = np.concatenate([s("W_B"), s("W_C")]).T
    out["w_l1a"] = pack(L1A, W_in=s("W_in").T, W_bc=halves(np.concatenate([bc, bc, bc], 1)), W_dt=halves(s("W_dt").T),
                        b_dt=halves(s("b_dt")), A_log=halves(s("A_log")), D=halves(s("D")),
                        gate=rows(s("output_gate")), W_out=halves(s("W_out").T))
    t = lambda n, l: i["L1_ffn_" + n][l]
    parts = {}
    for l in range(DEPTH):
        def padded(m, w):
            z = np.zeros((m.shape[0], w), np.float32)
            z[:, :m.shape[1]] = m
            return z
        w2 = np.zeros((NHID * P, E), np.float32)
        w2[:HID] = t("w2", l)
        one = dict(wqkv=t("wqkv", l), wo=t("wo", l).reshape(4, P, E).transpose(1, 0, 2).reshape(P, -1),
                   ln_g=col(t("ln_g", l)), ln_b=col(t("ln_b", l)), w1a=padded(t("w1", l)[:, :HID], NHID * P),
                   w1g=padded(t("w1", l)[:, HID:], NHID * P),
                   b1a=padded(t("b1", l)[None, :HID], NHID * P).reshape(NHID, P).T,
                   b1g=padded(t("b1", l)[None, HID:], NHID * P).reshape(NHID, P).T,
                   w2=w2.reshape(NHID, P, E).transpose(1, 0, 2).reshape(P, -1), b2=col(t("b2", l)),
                   qs=rows(t("q_scale", l)), ks=rows(t("k_scale", l)))
        parts.update({f"{n}{l}": v for n, v in one.items()})
    for n, v in zip(("cos_q", "sin_q", "cos_k", "sin_k"), xpos_tables()):
        parts[n] = v.reshape(TPB, P, DL).transpose(1, 0, 2).reshape(P, -1)
    out["w_l1f"] = pack(L1F, **parts)
    return {n: np.ascontiguousarray(v) for n, v in out.items()}
```
